# Optimizing a Trainium2 kernel written in Bass

```python
import numpy as np
import jax
import jax.numpy as jnp

def _softmax(x, axis=-1):
    return jax.nn.softmax(x, axis=axis)

def _gelu(x):
    return jax.nn.gelu(x, approximate=True)

def _silu(x):
    return jax.nn.silu(x)

def _sigmoid(x):
    return jax.nn.sigmoid(x)

def _layernorm(x, axis=-1, eps=1e-05):
    m = jnp.mean(x, axis=axis, keepdims=True)
    v = jnp.var(x, axis=axis, keepdims=True)
    return (x - m) / jnp.sqrt(v + eps)

def _scatter_add(tgt, idx, src, axis=0):
    return tgt.at[idx].add(src)

def _segment_sum(src, seg, n):
    return jax.ops.segment_sum(src, seg, n)
kernel_name = 'mk_gps_d2_gnn_r32_ce4fe8'

def setup_inputs(seed: int=0):
    np.random.seed(seed)
    _w = jnp.asarray

    def _rec_inputs():
        import jax
        import jax.numpy as jnp
        _gk = jax.random.key(seed)
        x = -0.0002117 + 1 * jax.random.normal(jax.random.fold_in(_gk, 1), (3125, 256), jnp.float32)
        _s = jax.random.randint(jax.random.fold_in(_gk, 2), (25000,), 0, 3125, jnp.int32)
        _d = jax.random.randint(jax.random.fold_in(_gk, 3), (25000,), 0, 3125, jnp.int32)
        _loop = jnp.arange(3125, dtype=jnp.int32)
        src = jnp.concatenate([_s, _d, _loop])
        dst = jnp.concatenate([_d, _s, _loop])
        _o = jnp.argsort(dst, stable=True)
        src = src[_o]
        dst = dst[_o]
        return (x, src, dst)
    x, src, dst = _rec_inputs()

    def _L0_gnn_setup():
        import jax, jax.numpy as jnp
        import numpy as np
        N_NODES = 3125
        N_EDGES = 100000
        D_IN = 256
        D_OUT = 256
        key = jax.random.key(seed)
        k1, k2, k3, k4 = jax.random.split(key, 4)
        x = jax.random.normal(k1, (N_NODES, D_IN), dtype=jnp.float32)
        edge_row = jax.random.randint(k2, (N_EDGES,), 0, N_NODES, dtype=jnp.int32)
        edge_col = jax.random.randint(k3, (N_EDGES,), 0, N_NODES, dtype=jnp.int32)
        bound = float(np.sqrt(6.0 / D_IN))
        weight = jax.random.uniform(k4, (D_IN, D_OUT), dtype=jnp.float32, minval=-bound, maxval=bound)
        bias = jnp.zeros((D_OUT,), dtype=jnp.float32)
        return {'x': x, 'edge_row': edge_row, 'edge_col': edge_col, 'weight': weight, 'bias': bias}
    _L0_gnn_all = _L0_gnn_setup()
    _L0_gnn_in = {k: v for k, v in _L0_gnn_all.items() if k in ('weight', 'bias')}
    del _L0_gnn_all

    def _L0_mix_setup():
        import jax, jax.numpy as jnp
        import numpy as np
        A, Bc, Cc = (0.5, 1.0, 1.0)
        H = 8
        EPS = 1e-12

        def _normalize(t):
            n = jnp.linalg.norm(t, axis=-1, keepdims=True)
            return t / jnp.maximum(n, EPS)
        key = jax.random.key(seed)
        ks = jax.random.split(key, 5)
        B, N, C = (8, 64, 256)
        D = C // H
        x = jax.random.normal(ks[0], (B, N, C), dtype=jnp.float32)
        Wqkv = jax.random.normal(ks[1], (3 * H * D, C), dtype=jnp.float32) * 0.02
        bqkv = jnp.zeros((3 * H * D,), dtype=jnp.float32)
        Wproj = jax.random.normal(ks[2], (C, H * D), dtype=jnp.float32) * 0.02
        bproj = jnp.zeros((C,), dtype=jnp.float32)
        temperature = jnp.ones((1, H, 1, 1), dtype=jnp.float32)
        return {'x': x, 'Wqkv': Wqkv, 'bqkv': bqkv, 'Wproj': Wproj, 'bproj': bproj, 'temperature': temperature}
    _L0_mix_all = _L0_mix_setup()
    _L0_mix_in = {k: v for k, v in _L0_mix_all.items() if k in ('Wqkv', 'bqkv', 'Wproj', 'bproj', 'temperature')}
    del _L0_mix_all

    def _L0_ffn_setup():
        import jax, jax.numpy as jnp
        import numpy as np
        B, S, D = (8, 128, 256)
        H = 4 * D
        CAPACITY = 0.5
        key = jax.random.key(seed)
        ks = jax.random.split(key, 6)
        x = jax.random.normal(ks[0], (B, S, D), dtype=jnp.float32)
        attention_mask = jnp.zeros((B, 1, 1, S), dtype=jnp.float32)
        wr = jax.random.normal(ks[1], (D, 1), dtype=jnp.float32) * 0.02
        br = jnp.zeros((1,), dtype=jnp.float32)
        w1 = jax.random.normal(ks[2], (D, H), dtype=jnp.float32) * 0.02
        b1 = jnp.zeros((H,), dtype=jnp.float32)
        w2 = jax.random.normal(ks[3], (H, D), dtype=jnp.float32) * 0.02
        b2 = jnp.zeros((D,), dtype=jnp.float32)
        return {'x': x, 'attention_mask': attention_mask, 'wr': wr, 'br': br, 'w1': w1, 'b1': b1, 'w2': w2, 'b2': b2}
    _L0_ffn_all = _L0_ffn_setup()
    _L0_ffn_in = {k: v for k, v in _L0_ffn_all.items() if k in ('attention_mask', 'wr', 'br', 'w1', 'b1', 'w2', 'b2')}
    del _L0_ffn_all

    def _L1_gnn_setup():
        import jax, jax.numpy as jnp
        import numpy as np
        N, E = (50000, 25000)
        IN_DIM = 256
        OUT_DIM = 256
        H = 8
        D = OUT_DIM // H
        SCALE = D ** (-0.5)
        LN_EPS = 1e-05

        def _layernorm(x, g, b):
            mu = jnp.mean(x, axis=-1, keepdims=True)
            var = jnp.mean((x - mu) ** 2, axis=-1, keepdims=True)
            return (x - mu) * jax.lax.rsqrt(var + LN_EPS) * g + b
        key = jax.random.key(seed)
        ks = jax.random.split(key, 12)
        s = 1.0 / np.sqrt(IN_DIM)
        inp = {'x': jax.random.normal(ks[0], (N, IN_DIM), jnp.float32), 'edge_index': jax.random.randint(ks[1], (2, E), 0, N, jnp.int64), 'batch': jnp.zeros((N,), jnp.int64), 'Wq': jax.random.uniform(ks[2], (IN_DIM, OUT_DIM), jnp.float32, -s, s), 'Wk': jax.random.uniform(ks[3], (IN_DIM, OUT_DIM), jnp.float32, -s, s), 'Wv': jax.random.uniform(ks[4], (IN_DIM, OUT_DIM), jnp.float32, -s, s), 'Wo_w': jax.random.uniform(ks[5], (OUT_DIM, OUT_DIM), jnp.float32, -s, s), 'Wo_b': jnp.zeros((OUT_DIM,), jnp.float32), 'ln1_g': jnp.ones((OUT_DIM,), jnp.float32), 'ln1_b': jnp.zeros((OUT_DIM,), jnp.float32), 'ln2_g': jnp.ones((OUT_DIM,), jnp.float32), 'ln2_b': jnp.zeros((OUT_DIM,), jnp.float32), 'ffn_w1': jax.random.uniform(ks[6], (OUT_DIM, 2 * OUT_DIM), jnp.float32, -s, s), 'ffn_b1': jnp.zeros((2 * OUT_DIM,), jnp.float32), 'ffn_w2': jax.random.uniform(ks[7], (2 * OUT_DIM, OUT_DIM), jnp.float32, -s, s), 'ffn_b2': jnp.zeros((OUT_DIM,), jnp.float32)}
        return inp
    _L1_gnn_all = _L1_gnn_setup()
    _L1_gnn_in = {k: v for k, v in _L1_gnn_all.items() if k in ('Wq', 'Wk', 'Wv', 'Wo_w', 'Wo_b', 'ln1_g', 'ln1_b', 'ln2_g', 'ln2_b', 'ffn_w1', 'ffn_b1', 'ffn_w2', 'ffn_b2')}
    del _L1_gnn_all

    def _L1_mix_setup():
        import jax, jax.numpy as jnp
        import numpy as np
        B, S, D = (8, 64, 256)
        H, KD = (8, 256)
        M = 256
        EPS_LN = 1e-06
        EPS_ATT = 1e-06

        def _layernorm(x, g, b):
            mu = jnp.mean(x, axis=-1, keepdims=True)
            var = jnp.mean(jnp.square(x - mu), axis=-1, keepdims=True)
            return (x - mu) * jax.lax.rsqrt(var + EPS_LN) * g + b

        def _phi(x, proj):
            u = jnp.einsum('bshd,md->bshm', x, proj)
            sq = 0.5 * jnp.sum(jnp.square(x), axis=-1, keepdims=True)
            return jnp.exp(u - sq) * (1.0 / np.sqrt(M)) + EPS_ATT
        key = jax.random.key(seed)
        ks = jax.random.split(key, 16)
        sd = lambda *s: 1.0 / np.sqrt(s[0])
        return {'inputs': jax.random.normal(ks[0], (B, S, D), dtype=jnp.float32), 'Wq': jax.random.normal(ks[1], (D, H, KD), jnp.float32) * sd(D), 'bq': jnp.zeros((H, KD), jnp.float32), 'Wk': jax.random.normal(ks[2], (D, H, KD), jnp.float32) * sd(D), 'bk': jnp.zeros((H, KD), jnp.float32), 'Wv': jax.random.normal(ks[3], (D, H, KD), jnp.float32) * sd(D), 'bv': jnp.zeros((H, KD), jnp.float32), 'Wo': jax.random.normal(ks[4], (H, KD, D), jnp.float32) * sd(H * KD), 'bo': jnp.zeros((D,), jnp.float32), 'proj': jax.random.normal(ks[5], (M, KD), jnp.float32), 'W1': jax.random.normal(ks[6], (D, D), jnp.float32) * sd(D), 'bias1': jnp.zeros((D,), jnp.float32), 'W2': jax.random.normal(ks[7], (D, D), jnp.float32) * sd(D), 'bias2': jnp.zeros((D,), jnp.float32), 'g1': jnp.ones((D,), jnp.float32), 'beta1': jnp.zeros((D,), jnp.float32), 'g2': jnp.ones((D,), jnp.float32), 'beta2': jnp.zeros((D,), jnp.float32)}
    _L1_mix_all = _L1_mix_setup()
    _L1_mix_in = {k: v for k, v in _L1_mix_all.items() if k in ('Wq', 'bq', 'Wk', 'bk', 'Wv', 'bv', 'Wo', 'bo', 'proj', 'W1', 'bias1', 'W2', 'bias2', 'g1', 'beta1', 'g2', 'beta2')}
    del _L1_mix_all

    def _L1_ffn_setup():
        import jax, jax.numpy as jnp
        import numpy as np
        C = 256
        HID = 1024
        E = 8
        TEMP = 1.0
        key = jax.random.key(seed)
        ks = jax.random.split(key, 7)
        x = jax.random.normal(ks[0], (8, 512, C), dtype=jnp.float32)
        W1 = jax.random.normal(ks[1], (C, HID), dtype=jnp.float32) * 0.02
        b1 = jnp.zeros((HID,), dtype=jnp.float32)
        Wg = jax.random.normal(ks[2], (HID, E), dtype=jnp.float32) * 0.02
        bg = jnp.zeros((E,), dtype=jnp.float32)
        Wd = jax.random.normal(ks[3], (E, HID, C), dtype=jnp.float32) * 0.02
        bd = jnp.zeros((E, C), dtype=jnp.float32)
        return {'x': x, 'W1': W1, 'b1': b1, 'Wg': Wg, 'bg': bg, 'Wd': Wd, 'bd': bd}
    _L1_ffn_all = _L1_ffn_setup()
    _L1_ffn_in = {k: v for k, v in _L1_ffn_all.items() if k in ('W1', 'b1', 'Wg', 'bg', 'Wd', 'bd')}
    del _L1_ffn_all
    return {'x': x, 'src': src, 'dst': dst, 'L0_gnn_weight': _L0_gnn_in['weight'], 'L0_gnn_bias': _L0_gnn_in['bias'], 'L0_mix_Wqkv': _L0_mix_in['Wqkv'], 'L0_mix_bqkv': _L0_mix_in['bqkv'], 'L0_mix_Wproj': _L0_mix_in['Wproj'], 'L0_mix_bproj': _L0_mix_in['bproj'], 'L0_mix_temperature': _L0_mix_in['temperature'], 'L0_ffn_attention_mask': _L0_ffn_in['attention_mask'], 'L0_ffn_wr': _L0_ffn_in['wr'], 'L0_ffn_br': _L0_ffn_in['br'], 'L0_ffn_w1': _L0_ffn_in['w1'], 'L0_ffn_b1': _L0_ffn_in['b1'], 'L0_ffn_w2': _L0_ffn_in['w2'], 'L0_ffn_b2': _L0_ffn_in['b2'], 'L1_gnn_Wq': _L1_gnn_in['Wq'], 'L1_gnn_Wk': _L1_gnn_in['Wk'], 'L1_gnn_Wv': _L1_gnn_in['Wv'], 'L1_gnn_Wo_w': _L1_gnn_in['Wo_w'], 'L1_gnn_Wo_b': _L1_gnn_in['Wo_b'], 'L1_gnn_ln1_g': _L1_gnn_in['ln1_g'], 'L1_gnn_ln1_b': _L1_gnn_in['ln1_b'], 'L1_gnn_ln2_g': _L1_gnn_in['ln2_g'], 'L1_gnn_ln2_b': _L1_gnn_in['ln2_b'], 'L1_gnn_ffn_w1': _L1_gnn_in['ffn_w1'], 'L1_gnn_ffn_b1': _L1_gnn_in['ffn_b1'], 'L1_gnn_ffn_w2': _L1_gnn_in['ffn_w2'], 'L1_gnn_ffn_b2': _L1_gnn_in['ffn_b2'], 'L1_mix_Wq': _L1_mix_in['Wq'], 'L1_mix_bq': _L1_mix_in['bq'], 'L1_mix_Wk': _L1_mix_in['Wk'], 'L1_mix_bk': _L1_mix_in['bk'], 'L1_mix_Wv': _L1_mix_in['Wv'], 'L1_mix_bv': _L1_mix_in['bv'], 'L1_mix_Wo': _L1_mix_in['Wo'], 'L1_mix_bo': _L1_mix_in['bo'], 'L1_mix_proj': _L1_mix_in['proj'], 'L1_mix_W1': _L1_mix_in['W1'], 'L1_mix_bias1': _L1_mix_in['bias1'], 'L1_mix_W2': _L1_mix_in['W2'], 'L1_mix_bias2': _L1_mix_in['bias2'], 'L1_mix_g1': _L1_mix_in['g1'], 'L1_mix_beta1': _L1_mix_in['beta1'], 'L1_mix_g2': _L1_mix_in['g2'], 'L1_mix_beta2': _L1_mix_in['beta2'], 'L1_ffn_W1': _L1_ffn_in['W1'], 'L1_ffn_b1': _L1_ffn_in['b1'], 'L1_ffn_Wg': _L1_ffn_in['Wg'], 'L1_ffn_bg': _L1_ffn_in['bg'], 'L1_ffn_Wd': _L1_ffn_in['Wd'], 'L1_ffn_bd': _L1_ffn_in['bd']}

def reference(x, src, dst, L0_gnn_weight, L0_gnn_bias, L0_mix_Wqkv, L0_mix_bqkv, L0_mix_Wproj, L0_mix_bproj, L0_mix_temperature, L0_ffn_attention_mask, L0_ffn_wr, L0_ffn_br, L0_ffn_w1, L0_ffn_b1, L0_ffn_w2, L0_ffn_b2, L1_gnn_Wq, L1_gnn_Wk, L1_gnn_Wv, L1_gnn_Wo_w, L1_gnn_Wo_b, L1_gnn_ln1_g, L1_gnn_ln1_b, L1_gnn_ln2_g, L1_gnn_ln2_b, L1_gnn_ffn_w1, L1_gnn_ffn_b1, L1_gnn_ffn_w2, L1_gnn_ffn_b2, L1_mix_Wq, L1_mix_bq, L1_mix_Wk, L1_mix_bk, L1_mix_Wv, L1_mix_bv, L1_mix_Wo, L1_mix_bo, L1_mix_proj, L1_mix_W1, L1_mix_bias1, L1_mix_W2, L1_mix_bias2, L1_mix_g1, L1_mix_beta1, L1_mix_g2, L1_mix_beta2, L1_ffn_W1, L1_ffn_b1, L1_ffn_Wg, L1_ffn_bg, L1_ffn_Wd, L1_ffn_bd):
    import jax
    import jax.numpy as jnp

    def _L0_gnn_ref(x, edge_row, edge_col, weight, bias):
        import jax, jax.numpy as jnp
        import numpy as np
        N_NODES = 3125
        N_EDGES = 100000
        D_IN = 256
        D_OUT = 256
        support = x @ weight
        gathered = jnp.take(support, edge_col, axis=0)
        out = jax.ops.segment_sum(gathered, edge_row, num_segments=N_NODES)
        return out + bias

    def _L0_mix_ref(x, Wqkv, bqkv, Wproj, bproj, temperature):
        import jax, jax.numpy as jnp
        import numpy as np
        A, Bc, Cc = (0.5, 1.0, 1.0)
        H = 8
        EPS = 1e-12

        def _normalize(t):
            n = jnp.linalg.norm(t, axis=-1, keepdims=True)
            return t / jnp.maximum(n, EPS)
        B, N, C = x.shape
        D = C // H
        scale = float(D) ** 0.25
        qkv = (x @ Wqkv.T + bqkv).reshape(B, N, 3, H, D)
        qkv = jnp.transpose(qkv, (2, 0, 3, 1, 4))
        q, k, v = (qkv[0], qkv[1], qkv[2])
        q = q * scale
        v1 = jnp.concatenate([jnp.ones((B, H, N, 1), dtype=v.dtype), v], axis=-1)
        qn = _normalize(q) * (scale * temperature)
        kn = _normalize(k) * scale
        vN = v1 / N
        kv_mod = jnp.einsum('bhni,bhnj,bhne->bhije', kn, kn, vN)
        kv = jnp.einsum('bhnd,bhne->bhde', kn, vN)
        vsum = jnp.sum(vN, axis=-2)[:, :, None, :]
        y = A * jnp.einsum('bhni,bhnj,bhije->bhne', qn, qn, kv_mod) + scale ** 2 * Bc * jnp.einsum('bhnd,bhde->bhne', qn, kv) + scale ** 4 * Cc * vsum
        y_norm, y = (y[..., :1], y[..., 1:])
        y = y / y_norm
        out = jnp.transpose(y, (0, 2, 1, 3)).reshape(B, N, H * D)
        return out @ Wproj.T + bproj

    def _L0_ffn_ref(x, attention_mask, wr, br, w1, b1, w2, b2):
        import jax, jax.numpy as jnp
        import numpy as np
        B, S, D = (8, 128, 256)
        H = 4 * D
        CAPACITY = 0.5
        b, s, d = x.shape
        weights = (jnp.einsum('bsd,do->bso', x, wr) + br)[..., 0]
        k = max(1, int(CAPACITY * s))
        kk = k - 1 if k > 1 else 1
        _, idx = jax.lax.top_k(weights, k)
        sel_idx = idx[:, :kk]
        sel = jnp.take_along_axis(x, sel_idx[:, :, None], axis=1)
        h = jax.nn.gelu(jnp.einsum('bkd,dh->bkh', sel, w1) + b1)
        y = jnp.einsum('bkh,hd->bkd', h, w2) + b2
        w_sel = jnp.take_along_axis(weights, sel_idx, axis=1)
        y = y * w_sel[..., None]
        batch_idx = jnp.arange(b)[:, None]
        processed = jnp.zeros_like(x).at[batch_idx, sel_idx].set(y)
        return processed + x

    def _L1_gnn_ref(x, edge_index, batch, Wq, Wk, Wv, Wo_w, Wo_b, ln1_g, ln1_b, ln2_g, ln2_b, ffn_w1, ffn_b1, ffn_w2, ffn_b2):
        import jax, jax.numpy as jnp
        import numpy as np
        N, E = (50000, 25000)
        IN_DIM = 256
        OUT_DIM = 256
        H = 8
        D = OUT_DIM // H
        SCALE = D ** (-0.5)
        LN_EPS = 1e-05

        def _layernorm(x, g, b):
            mu = jnp.mean(x, axis=-1, keepdims=True)
            var = jnp.mean((x - mu) ** 2, axis=-1, keepdims=True)
            return (x - mu) * jax.lax.rsqrt(var + LN_EPS) * g + b
        n = x.shape[0]
        residual = x
        Q = (x @ Wq).reshape(n, H, D)
        K = (x @ Wk).reshape(n, H, D)
        V = (x @ Wv).reshape(n, H, D)
        src, dst = (edge_index[0], edge_index[1])
        scores = jnp.einsum('ehd,ehd->eh', Q[dst], K[src]) * SCALE
        attn_max = jnp.zeros((n, H), scores.dtype).at[dst].max(scores)
        w = jnp.exp(scores - attn_max[dst])
        attn_sum = jnp.zeros((n, H), w.dtype).at[dst].add(w)
        w = w / (attn_sum[dst] + 1e-08)
        msg = V[src] * w[:, :, None]
        out = jnp.zeros((n, H, D), msg.dtype).at[dst].add(msg)
        out = out.reshape(n, OUT_DIM) @ Wo_w + Wo_b
        out = _layernorm(residual + out, ln1_g, ln1_b)
        ffn = jax.nn.gelu(out @ ffn_w1 + ffn_b1, approximate=False) @ ffn_w2 + ffn_b2
        out = _layernorm(out + ffn, ln2_g, ln2_b)
        return out

    def _L1_mix_ref(inputs, Wq, bq, Wk, bk, Wv, bv, Wo, bo, proj, W1, bias1, W2, bias2, g1, beta1, g2, beta2):
        import jax, jax.numpy as jnp
        import numpy as np
        B, S, D = (8, 64, 256)
        H, KD = (8, 256)
        M = 256
        EPS_LN = 1e-06
        EPS_ATT = 1e-06

        def _layernorm(x, g, b):
            mu = jnp.mean(x, axis=-1, keepdims=True)
            var = jnp.mean(jnp.square(x - mu), axis=-1, keepdims=True)
            return (x - mu) * jax.lax.rsqrt(var + EPS_LN) * g + b

        def _phi(x, proj):
            u = jnp.einsum('bshd,md->bshm', x, proj)
            sq = 0.5 * jnp.sum(jnp.square(x), axis=-1, keepdims=True)
            return jnp.exp(u - sq) * (1.0 / np.sqrt(M)) + EPS_ATT
        scale = KD ** (-0.25)
        q = (jnp.einsum('bsd,dhk->bshk', inputs, Wq) + bq) * scale
        k = (jnp.einsum('bsd,dhk->bshk', inputs, Wk) + bk) * scale
        v = jnp.einsum('bsd,dhk->bshk', inputs, Wv) + bv
        phi_q = _phi(q, proj)
        phi_k = _phi(k, proj)
        kv = jnp.einsum('bshm,bshk->bhmk', phi_k, v)
        z = jnp.einsum('bshm,bhm->bsh', phi_q, phi_k.sum(axis=1))
        attn = jnp.einsum('bshm,bhmk->bshk', phi_q, kv) / z[..., None]
        attn_out = jnp.einsum('bshk,hkd->bsd', attn, Wo) + bo
        out1 = _layernorm(inputs + attn_out, g1, beta1)
        h = jax.nn.relu(out1 @ W1 + bias1)
        ffn_out = h @ W2 + bias2
        return _layernorm(out1 + ffn_out, g2, beta2)

    def _L1_ffn_ref(x, W1, b1, Wg, bg, Wd, bd):
        import jax, jax.numpy as jnp
        import numpy as np
        C = 256
        HID = 1024
        E = 8
        TEMP = 1.0
        orig_shape = x.shape
        xf = x.reshape(-1, orig_shape[-1])
        H = jax.nn.gelu(xf @ W1 + b1, approximate=False)
        probs = jax.nn.softmax((H @ Wg + bg) / TEMP, axis=-1)
        assign = jnp.argmax(probs, axis=-1)
        out = jnp.zeros_like(xf)
        for e in range(Wd.shape[0]):
            y = H @ Wd[e] + bd[e]
            sel = (assign == e)[:, None]
            out = out + jnp.where(sel, probs[:, e:e + 1] * y, 0.0)
        return out.reshape(orig_shape)
    edge_index = jnp.stack([src, dst])
    batch0 = jnp.zeros((3125,), jnp.int32)
    xn = _layernorm(x, axis=-1)
    x = x + _L0_gnn_ref(xn, src, dst, L0_gnn_weight, L0_gnn_bias) + _L0_mix_ref(xn[None], L0_mix_Wqkv, L0_mix_bqkv, L0_mix_Wproj, L0_mix_bproj, L0_mix_temperature)[0]
    x = x + _L0_ffn_ref(_layernorm(x, axis=-1)[None], L0_ffn_attention_mask, L0_ffn_wr, L0_ffn_br, L0_ffn_w1, L0_ffn_b1, L0_ffn_w2, L0_ffn_b2)[0]
    xn = _layernorm(x, axis=-1)
    x = x + _L1_gnn_ref(xn, edge_index, batch0, L1_gnn_Wq, L1_gnn_Wk, L1_gnn_Wv, L1_gnn_Wo_w, L1_gnn_Wo_b, L1_gnn_ln1_g, L1_gnn_ln1_b, L1_gnn_ln2_g, L1_gnn_ln2_b, L1_gnn_ffn_w1, L1_gnn_ffn_b1, L1_gnn_ffn_w2, L1_gnn_ffn_b2) + _L1_mix_ref(xn[None], L1_mix_Wq, L1_mix_bq, L1_mix_Wk, L1_mix_bk, L1_mix_Wv, L1_mix_bv, L1_mix_Wo, L1_mix_bo, L1_mix_proj, L1_mix_W1, L1_mix_bias1, L1_mix_W2, L1_mix_bias2, L1_mix_g1, L1_mix_beta1, L1_mix_g2, L1_mix_beta2)[0]
    x = x + _L1_ffn_ref(_layernorm(x, axis=-1)[None], L1_ffn_W1, L1_ffn_b1, L1_ffn_Wg, L1_ffn_bg, L1_ffn_Wd, L1_ffn_bd)[0]
    return x

_drawn_inputs = setup_inputs


def setup_inputs(seed=0):
    import zlib

    import numpy as np

    out = dict(_drawn_inputs(seed))
    spreads = {'L0_gnn_bias': (0.0, 0.466),
     'L0_mix_bqkv': (0.0, 0.8),
     'L0_mix_bproj': (0.0, 0.451),
     'L0_mix_temperature': (1.0, 0.6),
     'L0_ffn_b1': (0.0, 0.8),
     'L0_ffn_b2': (0.0, 0.8),
     'L1_gnn_Wo_b': (0.0, 0.659),
     'L1_gnn_ln1_g': (1.0, 0.6),
     'L1_gnn_ln1_b': (0.0, 0.721),
     'L1_gnn_ln2_g': (1.0, 0.6),
     'L1_gnn_ln2_b': (0.0, 0.695),
     'L1_gnn_ffn_b1': (0.0, 0.8),
     'L1_gnn_ffn_b2': (0.0, 0.771),
     'L1_mix_bq': (0.0, 0.8),
     'L1_mix_bk': (0.0, 0.8),
     'L1_mix_bv': (0.0, 0.705),
     'L1_mix_bo': (0.0, 0.71),
     'L1_mix_bias1': (0.0, 0.8),
     'L1_mix_bias2': (0.0, 0.8),
     'L1_mix_g1': (1.0, 0.6),
     'L1_mix_beta1': (0.0, 0.683),
     'L1_mix_g2': (1.0, 0.6),
     'L1_mix_beta2': (0.0, 0.723),
     'L1_ffn_b1': (0.0, 0.8),
     'L1_ffn_bg': (0.0, 0.8),
     'L1_ffn_bd': (0.0, 0.8)}
    factors = {'L0_mix_Wqkv': 8.0,
     'L0_mix_Wproj': 8.0,
     'L0_ffn_wr': 8.0,
     'L0_ffn_w1': 8.0,
     'L0_ffn_w2': 8.0,
     'L1_gnn_Wq': 8.0,
     'L1_gnn_Wk': 8.0,
     'L1_gnn_Wv': 3.943,
     'L1_gnn_Wo_w': 3.957,
     'L1_ffn_W1': 8.0,
     'L1_ffn_Wg': 8.0,
     'L1_ffn_Wd': 8.0}
    for name, (base, spread) in spreads.items():
        noise = np.random.default_rng([zlib.crc32(name.encode()), seed]).standard_normal(out[name].shape)
        drawn = base * np.exp(spread * noise) if base else spread * noise
        out[name] = jnp.asarray(drawn.astype(out[name].dtype))
    for name, factor in factors.items():
        out[name] = (out[name] * factor).astype(out[name].dtype)
    return out
```

```python
from contextlib import ExitStack

import numpy as np

import concourse.bass as bass
from concourse import mybir

F32 = mybir.dt.float32
I32 = mybir.dt.int32
ALU = mybir.AluOpType
ACT = mybir.ActivationFunctionType
AX = mybir.AxisListType

P = 125
T = 25
N = P * T
TE = 425
E = P * TE
D = 256
KC = D // 128
H = 8
DH = D // H
B = 5
ITERS = T // B
HID = 1024
HC = HID // 128
GW = D + H

NQ = 17 * DH
NF = NQ + DH + 1
FC = 5
FW = FC * 128
V1 = DH + 1


def second_order_weights():
    scale = float(DH) ** 0.25
    w = np.zeros(FW, np.float64)
    w[:NQ] = 0.5 * np.where((np.arange(NQ) // DH > 0) & (np.arange(NQ) // DH < 16), 2.0, 1.0)
    w[NQ:NQ + DH] = scale ** 2
    w[NQ + DH] = scale ** 4
    return np.tile((w / N).reshape(FC, 128).T, (1, H)).astype(np.float32)


def constants():
    p = np.arange(P, dtype=np.float32)
    return {
        "c_ident": np.eye(128, dtype=np.float32),
        "c_node": (p[:, None] * T + np.arange(T, dtype=np.float32)).astype(np.float32),
        "c_column": np.tile(np.arange(T, dtype=np.float32), (P, 1)),
        "c_before": np.triu(np.ones((P, P), np.float32), 1).T.copy(),
        "c_after": np.triu(np.ones((P, P), np.float32), 1),
        "c_base": np.tile(p * T, (P, 1)).astype(np.float32),
        "c_reversed": np.tile(8.0 - np.arange(8, dtype=np.float32), (P, 1)).astype(np.float32),
        "c_second": second_order_weights(),
    }


class Core:

    def __init__(self, nc, a, stack):
        self.nc, self.a, self.stack = nc, a, stack
        self.count = 0

    def scope(self):
        return Scope(self)


class Scope:

    def __init__(self, core):
        self.core, self.nc = core, core.nc

    def __enter__(self):
        self.stack = ExitStack()
        self.stack.__enter__()
        self.sems = []
        return self

    def __exit__(self, *e):
        if self.sems and e[0] is None:
            sems = self.sems
            with self.nc.Block() as block:
                @block.gpsimd
                def _(pool):
                    for sem in sems:
                        pool.sem_clear(sem)
        return self.stack.__exit__(*e)

    def sb(self, name, shape, dt=F32):
        self.core.count += 1
        return self.stack.enter_context(self.nc.sbuf_tensor(f"{name}_{self.core.count}", shape, dt))

    def ps(self, name, shape, dt=F32):
        self.core.count += 1
        return self.stack.enter_context(self.nc.psum_tensor(f"{name}_{self.core.count}", shape, dt))

    def gather_sem(self, name):
        self.core.count += 1
        return self.core.stack.enter_context(self.nc.semaphore(f"{name}_{self.core.count}"))

    def sem(self, name):
        self.core.count += 1
        self.sems.append(self.stack.enter_context(self.nc.semaphore(f"{name}_{self.core.count}")))
        return self.sems[-1]


def node_rows(table):
    return table.rearrange("(p j) d -> p j d", p=P)


def row(vector, n):
    return vector.rearrange("(a d) -> a d", a=1).broadcast_to([n, vector.shape[0]])


def chunks(matrix):
    return matrix.rearrange("(k p) n -> p k n", p=128)


def bcast(ap, n):
    p, h = ap.shape
    return ap.unsqueeze(2).to_broadcast([p, h, n])


def node_stats(k, s, eps, var_ready, sd_ready):
    nc, v = k.nc, k.nc.vector
    with v.Fori(0, ITERS) as i:
        for b in range(B):
            v.bn_stats(s.stat[:, b, :], k.X[:, i * B + b, :])
        v.drain()
        for b in range(B):
            v.bn_aggr(s.mv[:, b, :], s.stat[:, b, :])
        v.drain()
        v.tensor_copy(k.MV[:, bass.ds(i * B, B), :], s.mv[:])
        v.drain()
    v.tensor_scalar(k.RSTD[:], k.MV[:, :, 1], eps, None, ALU.add).then_inc(var_ready, 1)
    v.wait_ge(sd_ready, 1)
    v.reciprocal(k.RSTD[:], k.SD[:])
    v.drain()


def stage_load(k):
    nc, a = k.nc, k.a
    with k.scope() as s:
        loaded = s.sem("loaded")
        with nc.Block() as block:
            @block.sync
            def _(sp):
                sp.dma_start(k.X[:], node_rows(a["x"])).then_inc(loaded, 16)
                sp.dma_start(k.IDENT[:], a["c_ident"]).then_inc(loaded, 16)
                sp.dma_start(k.NODE[:], a["c_node"]).then_inc(loaded, 16)
                sp.wait_ge(loaded, 48)


def stage_edges(k):
    nc, a = k.nc, k.a
    with k.scope() as s:
        dstf = s.sb("dstf", [P, TE])
        firstrow = s.sb("firstrow", [P, P])
        lastrow = s.sb("lastrow", [P, P])
        wide = s.sb("wide", [P, 2, P])
        nexti = s.sb("nexti", [P, 1], I32)
        nextf = s.sb("nextf", [P, 1])
        lc = s.sb("lc", [P, 1])
        before = s.sb("before", [P, P])
        after = s.sb("after", [P, P])
        scratch = s.sb("scratch", [P, TE])
        pc = s.sb("pc", [P, T])
        rowi = s.sb("rowi", [P, T], I32)
        drow = s.sb("drow", [P, B, TE], I32)
        stage_row = s.sb("stage_row", [P, B], I32)
        colc = s.sb("colc", [P, T])
        cnt = s.sb("cnt", [P, T])
        c5 = s.sb("c5", [P, B])
        h5 = s.sb("h5", [P, B])
        rows_ps = s.ps("rows_ps", [P, 2, 512])
        loaded, none, wide_ready, rows_ready = s.sem("loaded"), s.sem("none"), s.sem("wide_ready"), s.sem("rows_ready")
        row_index, staged, gathered, counted = s.sem("row_index"), s.sem("staged"), s.gather_sem("gathered"), s.sem("counted")
        with nc.Block() as block:
            @block.sync
            def _(sp):
                dst2 = a["dst"].rearrange("(p t) -> p t", p=P)
                sp.dma_start(k.SRC[:], a["src"].rearrange("(p t) -> p t", p=P)).then_inc(loaded, 16)
                sp.dma_start(k.DST[:], dst2).then_inc(loaded, 16)
                sp.dma_start(before[:], a["c_before"]).then_inc(loaded, 16)
                sp.dma_start(after[:], a["c_after"]).then_inc(loaded, 16)
                sp.dma_start(colc[:], a["c_column"]).then_inc(loaded, 16)
                sp.wait_ge(none, 1)
                sp.dma_start(nexti[0:P - 1, :], dst2[1:P, 0:1], allow_slow_non_contiguous=True).then_inc(loaded, 16)
                sp.wait_ge(loaded, 96)

            @block.tensor
            def _(pe):
                pe.wait_ge(wide_ready, 1)
                for r in range(2):
                    ins = nc.tensor.matmul(rows_ps[:, r, 0:P], wide[:, r, :], k.IDENT[0:P, 0:P], start=True, stop=True)
                ins.then_inc(rows_ready, 1)

            @block.vector
            def _(v):
                v.memset(nexti[:], -1).then_inc(none, 1)
                v.wait_ge(loaded, 96)
                v.tensor_copy(dstf[:], k.DST[:])
                v.tensor_copy(nextf[:], nexti[:])
                v.drain()
                v.tensor_copy(wide[:, 0, :], dstf[:, 0:1].to_broadcast([P, P]))
                v.tensor_copy(wide[:, 1, :], dstf[:, TE - 1:TE].to_broadcast([P, P])).then_inc(wide_ready, 1)
                v.memset(k.SAME[:, 0:1], 0.0)
                v.tensor_tensor(k.SAME[:, 1:TE], dstf[:, 1:TE], dstf[:, 0:TE - 1], ALU.is_equal)
                v.tensor_tensor(lc[:], dstf[:, TE - 1:TE], nextf[:], ALU.is_equal)
                v.tensor_scalar(cnt[:, 0:1], dstf[:, TE - 1:TE], 1.0, None, ALU.add)
                v.drain()
                v.tensor_tensor(lc[:], lc[:], cnt[:, 0:1], ALU.mult)
                v.drain()
                v.tensor_scalar(lc[:], lc[:], -1.0, None, ALU.add)
                v.drain()
                v.tensor_scalar(k.OPEN[:], colc[:], lc[:, 0:1], -1.0, ALU.subtract, ALU.mult)
                v.wait_ge(rows_ready, 1)
                v.tensor_copy(firstrow[:], rows_ps[:, 0, 0:P])
                v.tensor_copy(lastrow[:], rows_ps[:, 1, 0:P])
                v.drain()
                v.scalar_tensor_tensor(k.FROM_LEFT[:], lastrow[:], dstf[:, 0:1], before[:], ALU.is_equal, ALU.mult)
                v.scalar_tensor_tensor(k.FROM_RIGHT[:], firstrow[:], dstf[:, TE - 1:TE], after[:], ALU.is_equal, ALU.mult)
                for j in range(T):
                    v.tensor_scalar(scratch[:, 0:P], firstrow[:], k.NODE[:, j:j + 1], 0.0, ALU.is_le, ALU.add,
                                    accum_out=pc[:, j:j + 1])
                    v.drain()
                v.tensor_scalar(pc[:], pc[:], -1.0, 0.0, ALU.add, ALU.max)
                v.drain()
                v.tensor_copy(rowi[:], pc[:])
                v.drain()
                with v.Fori(0, ITERS) as i:
                    v.tensor_copy(stage_row[:], rowi[:, bass.ds(i * B, B)]).then_inc(staged, 1)
                    v.wait_ge(gathered, (i + 1) * 16 * B)
                    for b in range(B):
                        v.tensor_scalar(scratch[:], drow[:, b, :], k.NODE[:, bass.ds(i * B + b, 1)], 0.0, ALU.is_le, ALU.add,
                                        accum_out=c5[:, b:b + 1])
                        v.drain()
                        v.tensor_scalar(scratch[:], drow[:, b, :], k.NODE[:, bass.ds(i * B + b, 1)], 0.0, ALU.is_equal, ALU.max,
                                        accum_out=h5[:, b:b + 1])
                        v.drain()
                    v.tensor_copy(cnt[:, bass.ds(i * B, B)], c5[:])
                    v.tensor_copy(k.HAS[:, bass.ds(i * B, B)], h5[:])
                    v.drain()
                v.scalar_tensor_tensor(pc[:], pc[:], float(TE), cnt[:], ALU.mult, ALU.add)
                v.drain()
                v.tensor_scalar(pc[:], pc[:], -1.0, 0.0, ALU.add, ALU.max)
                v.drain()
                v.tensor_copy(k.LAST[:], pc[:])

            @block.gpsimd
            def _(pool):
                table = a["dst"].rearrange("(p t) -> p t", p=P)
                with pool.Fori(0, ITERS) as i:
                    pool.wait_ge(staged, i + 1)
                    pool.sem_inc(counted, 1)
                    for b in range(B):
                        nc.gpsimd.indirect_dma_start(out=drow[:, b, :], out_offset=None, in_=table,
                                                     in_offset=bass.IndirectOffsetOnAxis(ap=stage_row[:, b:b + 1], axis=0)
                                                     ).then_inc(gathered, 16)


def stage_weights0(k, s0):
    nc, a = k.nc, k.a
    with k.scope() as s:
        wq = s.sb("wq", [128, 6, D])
        wp = s.sb("wp", [128, 2, D])
        pt = s.ps("pt", [128, 8, 512])
        loaded, turned, taken = s.sem("loaded"), s.sem("turned"), s.sem("taken")
        with nc.Block() as block:
            @block.sync
            def _(sp):
                sp.dma_start(wq[:], chunks(a["L0_mix_Wqkv"])).then_inc(loaded, 16)
                sp.dma_start(wp[:], chunks(a["L0_mix_Wproj"])).then_inc(loaded, 16)
                sp.dma_start(s0.W[:, :, 768:1024], chunks(a["L0_gnn_weight"])).then_inc(loaded, 16)
                sp.dma_start(s0.bias[:], row(a["L0_mix_bqkv"], P)).then_inc(loaded, 16)
                sp.dma_start(s0.second[:], a["c_second"]).then_inc(loaded, 16)
                sp.dma_start(s0.fac[:, 0:H], row(a["L0_mix_temperature"], P)).then_inc(loaded, 16)
                sp.dma_start(s0.bsum[:, 0, :], row(a["L0_gnn_bias"], P)).then_inc(loaded, 16)
                sp.dma_start(s0.bsum[:, 1, :], row(a["L0_mix_bproj"], P)).then_inc(loaded, 16)
                sp.wait_ge(loaded, 128)

            @block.tensor
            def _(pe):
                pe.wait_ge(loaded, 128)
                for r in range(8):
                    src = wq[:, r, :] if r < 6 else wp[:, r - 6, :]
                    for c in range(KC):
                        ins = nc.tensor.transpose(pt[:, r, c * 128:c * 128 + 128], src[:, c * 128:c * 128 + 128], k.IDENT[:])
                    ins.then_inc(turned, 1)

            @block.vector
            def _(v):
                for r in range(8):
                    v.wait_ge(turned, r + 1)
                    out = s0.W[:, :, r * 128:r * 128 + 128] if r < 6 else s0.WPT[:, :, (r - 6) * 128:(r - 5) * 128]
                    v.tensor_copy(out, pt[:, r, 0:256].rearrange("p (c n) -> p c n", c=KC))
                v.wait_ge(loaded, 128)
                v.tensor_scalar(s0.fac[:, 0:H], s0.fac[:, 0:H], float(DH) ** 0.5, None, ALU.mult)
                v.memset(s0.fac[:, H:2 * H], float(DH) ** 0.25)
                v.memset(s0.qscale[:, 0:H], float(DH) ** 0.25)
                v.memset(s0.qscale[:, H:2 * H], 1.0)


def stage_layer0_rows(k, s0):
    nc, a = k.nc, k.a
    with k.scope() as s:
        s.stat = s.sb("stat", [P, B, 6])
        s.mv = s.sb("mv", [P, B, 2])
        XS = s.sb("XS", [P, B, D])
        XT = s.sb("XT", [128, B, KC, P])
        QK = s.sb("QK", [P, 2 * D])
        SQ = s.sb("SQ", [P, 2 * D])
        nrm = s.sb("nrm", [P, 2 * H])
        nsd = s.sb("nsd", [P, 2 * H])
        VV = s.sb("VV", [P, B, H, V1])
        SUP = s.sb("SUP", [P, B, D])
        KN = s.sb("KN", [P, H, DH + 16])
        PHI = s.sb("PHI", [P, H, FW])
        PT = s.ps("PT", [128, 3, 512])
        PR = s.ps("PR", [P, 2, 512])
        KVP = s.ps("KVP", [128, 3, 512])

        def pt(b):
            return PT[:, b % 3, 0:KC * P].rearrange("p (c n) -> p c n", c=KC)

        sem = s.sem
        var_ready, sd_ready, zeroed = sem("var_ready"), sem("sd_ready"), sem("zeroed")
        rows_ready, rows_free = sem("rows_ready"), sem("rows_free")
        turned_ready, turned_free = sem("turned_ready"), sem("turned_free")
        xt_ready, xt_free = sem("xt_ready"), sem("xt_free")
        proj_ready, qk_free, vs_free = sem("proj_ready"), sem("qk_free"), sem("vs_free")
        v_ready, kv_done = sem("v_ready"), sem("kv_done")
        sup_ready, sup_out = sem("sup_ready"), [sem(f"sup_out{b}") for b in range(B)]
        norm_ready, root_ready = sem("norm_ready"), sem("root_ready")
        phi_ready, phi_free = sem("phi_ready"), sem("phi_free")
        with nc.Block() as block:
            @block.vector
            def _(v):
                v.memset(KVP[:], 0.0)
                v.memset(PHI[:, :, NQ + DH:FW], 0.0)
                v.memset(VV[:, :, :, 0:1], 1.0)
                v.drain()
                v.memset(PHI[:, :, NF - 1:NF], 1.0).then_inc(zeroed, 1)
                node_stats(k, s, 1e-5, var_ready, sd_ready)
                v.sem_inc(qk_free, 1)
                v.sem_inc(vs_free, 2)
                with v.Fori(0, ITERS) as i:
                    for b in range(B):
                        n = i * B + b
                        v.wait_ge(rows_free, n + 1)
                        v.tensor_scalar(XS[:, b, :], k.X[:, n, :], k.MV[:, n, 0:1], k.RSTD[:, bass.ds(n, 1)],
                                        ALU.subtract, ALU.mult).then_inc(rows_ready, 1)
                    for b in range(B):
                        n = i * B + b
                        v.wait_ge(proj_ready, 2 * n + 1)
                        v.tensor_tensor(QK[:], PR[:, 0, :], s0.bias[:, 0:2 * D], ALU.add).then_inc(qk_free, 1)
                        v.wait_ge(sup_ready, n + 1)
                        v.wait_ge(kv_done, n + 1)
                        v.tensor_tensor(VV[:, b, :, 1:V1], PR[:, 1, 0:D].rearrange("p (h d) -> p h d", h=H),
                                        s0.bias[:, 2 * D:3 * D].rearrange("p (h d) -> p h d", h=H), ALU.add
                                        ).then_inc(vs_free, 1)
                        v.drain()
                        v.tensor_tensor(SQ[:], QK[:], QK[:], ALU.mult)
                        v.drain()
                        v.tensor_reduce(nrm[:], SQ[:].rearrange("p (g d) -> p g d", d=DH), AX.X, ALU.add
                                        ).then_inc(norm_ready, 1)
                        v.wait_ge(root_ready, n + 1)
                        v.tensor_tensor(nrm[:], nsd[:], s0.qscale[:], ALU.mult)
                        v.drain()
                        v.tensor_scalar(nrm[:], nrm[:], 1e-12, None, ALU.max)
                        v.drain()
                        v.reciprocal(nrm[:], nrm[:])
                        v.drain()
                        v.tensor_tensor(nrm[:], nrm[:], s0.fac[:], ALU.mult)
                        v.drain()
                        v.tensor_tensor(k.QN[:, n, :].rearrange("p (h d) -> p h d", h=H),
                                        QK[:, 0:D].rearrange("p (h d) -> p h d", h=H), bcast(nrm[:, 0:H], DH), ALU.mult)
                        v.tensor_tensor(KN[:, :, 0:DH], QK[:, D:2 * D].rearrange("p (h d) -> p h d", h=H),
                                        bcast(nrm[:, H:2 * H], DH), ALU.mult)
                        v.drain()
                        v.tensor_copy(KN[:, :, DH:DH + 16], KN[:, :, 0:16])
                        v.drain()
                        for half in range(2):
                            features(v, KN, PHI, half, phi_free, phi_ready, 2 * n + half)

            @block.tensor
            def _(pe):
                pe.sem_inc(rows_free, B)
                pe.sem_inc(xt_free, B)
                pe.sem_inc(kv_done, B)
                pe.sem_inc(phi_free, 2)
                pe.wait_ge(zeroed, 1)

                def sums(n, b):
                    for half in range(2):
                        pe.wait_ge(phi_ready, 2 * n + half + 1)
                        for h in range(4 * half, 4 * half + 4):
                            for c in range(FC):
                                g = h * FC + c
                                ins = nc.tensor.matmul(KVP[:, g // 15, (g % 15) * V1:(g % 15 + 1) * V1],
                                                       PHI[:, h, c * 128:c * 128 + 128], VV[:, b, h, :],
                                                       start=False, stop=False, skip_group_check=True)
                        ins.then_inc(phi_free, 1)
                    pe.drain().then_inc(kv_done, 1)

                with pe.Fori(0, ITERS) as i:
                    for b in range(B):
                        n = i * B + b
                        pe.wait_ge(rows_ready, n + 1)
                        pe.wait_ge(turned_free, n + 1)
                        for c in range(KC):
                            ins = nc.tensor.transpose(pt(b)[:, c, :], XS[:, b, c * 128:c * 128 + 128], k.IDENT[0:P, 0:P])
                        ins.then_inc(turned_ready, 1)
                    for b in range(B):
                        n = i * B + b
                        pe.wait_ge(xt_ready, n + 1)
                        for half, free in ((0, qk_free), (1, vs_free)):
                            pe.wait_ge(free, (n + 1) * (1 + half))
                            for c in range(KC):
                                ins = nc.tensor.matmul(PR[:, half, :], XT[:, b, c, :], s0.W[:, c, half * 512:half * 512 + 512],
                                                       start=(c == 0), stop=(c == KC - 1))
                            ins.then_inc(proj_ready, 1)
                        sums(n, b)

            @block.scalar
            def _(act):
                act.sem_inc(turned_free, 2)
                act.wait_ge(var_ready, 1)
                nc.scalar.activation(k.SD[:], k.RSTD[:], ACT.Sqrt).then_inc(sd_ready, 1)
                with act.Fori(0, ITERS) as i:
                    for b in range(B):
                        n = i * B + b
                        act.wait_ge(turned_ready, n + 1)
                        act.wait_ge(xt_free, n + 1)
                        nc.scalar.activation(XT[:, b, :, :], pt(b), ACT.Copy).then_inc(xt_ready, 1)
                        act.sem_inc(rows_free, 1)
                        act.drain().then_inc(turned_free, 1)
                    for b in range(B):
                        n = i * B + b
                        act.wait_ge(proj_ready, 2 * n + 2)
                        act.sem_inc(xt_free, 1)
                        act.wait_ge(sup_out[b], 16 * i + 16)
                        nc.scalar.activation(SUP[:, b, :], PR[:, 1, D:2 * D], ACT.Copy).then_inc(vs_free, 1)
                        act.drain().then_inc(sup_ready, 1)
                        act.wait_ge(norm_ready, n + 1)
                        nc.scalar.activation(nsd[:], nrm[:], ACT.Sqrt).then_inc(root_ready, 1)

            @block.sync
            def _(sp):
                for b in range(B):
                    sp.sem_inc(sup_out[b], 16)
                with sp.Fori(0, ITERS) as i:
                    for b in range(B):
                        n = i * B + b
                        sp.wait_ge(sup_ready, n + 1)
                        sp.dma_start(node_rows(k.sup)[:, n, :], SUP[:, b, :]).then_inc(sup_out[b], 16)
                for b in range(B):
                    sp.wait_ge(sup_out[b], 16 * (ITERS + 1))
        with nc.Block() as block:
            @block.vector
            def _(v):
                for g in range(3):
                    m = min(15, H * FC - 15 * g)
                    v.tensor_tensor(s0.KV[:, 15 * g:15 * g + m, :],
                                    KVP[:, g, 0:m * V1].rearrange("p (g e) -> p g e", e=V1),
                                    bcast(s0.second[:, 15 * g:15 * g + m], V1), ALU.mult)


def features(v, U, PHI, half, phi_free, phi_ready, count):
    heads = slice(4 * half, 4 * half + 4)
    v.wait_ge(phi_free, count + 1)
    once = U[:, heads, 0:DH].unsqueeze(2).to_broadcast([P, 4, 17, DH])
    u = U[:, heads, 0:DH]
    shifted = bass.AP(u.tensor, u.offset, [list(u.ap[0]), list(u.ap[1]), [1, 17], [1, DH]])
    v.tensor_copy(PHI[:, heads, NQ:NQ + DH], U[:, heads, 0:DH])
    v.tensor_tensor(PHI[:, heads, 0:NQ].rearrange("p h (o i) -> p h o i", i=DH), once, shifted, ALU.mult)
    v.drain().then_inc(phi_ready, 1)


def stage_layer0_attention(k, s0):
    nc, a = k.nc, k.a
    GROUPS = H * FC // 4
    with k.scope() as s:
        QS = s.sb("QS", [P, H, DH + 16])
        PHI = s.sb("PHI", [P, H, FW])
        PHT = s.sb("PHT", [128, H * FC, P])
        Y = s.sb("Y", [P, H, V1])
        YO = s.sb("YO", [P, D])
        YT = s.sb("YT", [128, KC, P])
        rec = s.sb("rec", [P, H])
        PT = s.ps("PT", [128, 2, 512])
        PY = s.ps("PY", [P, 512])
        PYT = s.ps("PYT", [128, 512])
        PO = s.ps("PO", [P, 512])
        sem = s.sem
        phi_ready, phi_free = sem("phi_ready"), sem("phi_free")
        pt_ready, pt_free, pht_ready, pht_free = sem("pt_ready"), sem("pt_free"), sem("pht_ready"), sem("pht_free")
        y_ready, y_free, yo_ready = sem("y_ready"), sem("y_free"), sem("yo_ready")
        yt_turned, yt_ready, out_ready, out_free = sem("yt_turned"), sem("yt_ready"), sem("out_ready"), sem("out_free")
        with nc.Block() as block:
            @block.vector
            def _(v):
                v.memset(PHI[:, :, NQ + DH:FW], 0.0)
                v.drain()
                v.memset(PHI[:, :, NF - 1:NF], 1.0)
                v.drain().then_inc(y_free, 1)
                v.sem_inc(out_free, 1)
                with v.Fori(0, T) as n:
                    v.tensor_copy(QS[:, :, 0:DH], k.QN[:, n, :].rearrange("p (h d) -> p h d", h=H))
                    v.tensor_copy(QS[:, :, DH:DH + 16], k.QN[:, n, :].rearrange("p (h d) -> p h d", h=H)[:, :, 0:16])
                    v.drain()
                    for half in range(2):
                        features(v, QS, PHI, half, phi_free, phi_ready, 2 * n + half)
                    v.wait_ge(y_ready, n + 1)
                    v.reciprocal(rec[:], PY[:, 0:H * V1].rearrange("p (h e) -> p h e", e=V1)[:, :, 0])
                    v.drain()
                    v.tensor_tensor(YO[:].rearrange("p (h d) -> p h d", h=H),
                                    PY[:, 0:H * V1].rearrange("p (h e) -> p h e", e=V1)[:, :, 1:V1],
                                    bcast(rec[:], DH), ALU.mult).then_inc(yo_ready, 1)
                    v.drain().then_inc(y_free, 1)
                    v.wait_ge(out_ready, n + 1)
                    v.tensor_tensor(k.ACC[:, n, :], PO[:, 0:D], k.X[:, n, :], ALU.add)
                    v.drain().then_inc(out_free, 1)

            @block.tensor
            def _(pe):
                pe.sem_inc(phi_free, 2)
                pe.sem_inc(pht_free, 1)
                with pe.Fori(0, T) as n:
                    def products(g):
                        pe.wait_ge(pht_ready, n * GROUPS + g + 1)
                        for q in range(4 * g, 4 * g + 4):
                            h, c = q // FC, q % FC
                            ins = nc.tensor.matmul(PY[:, h * V1:(h + 1) * V1], PHT[:, q, :], s0.KV[:, q, :],
                                                   start=(c == 0), stop=(c == FC - 1))
                        return ins
                    pe.wait_ge(y_free, n + 1)
                    for g in range(GROUPS):
                        if g % 5 == 0:
                            pe.wait_ge(phi_ready, 2 * n + g // 5 + 1)
                        pe.wait_ge(pt_free, n * GROUPS + g + 1)
                        for q in range(4):
                            h, c = (4 * g + q) // FC, (4 * g + q) % FC
                            ins = nc.tensor.transpose(PT[:, g % 2, q * P:q * P + P], PHI[:, h, c * 128:c * 128 + 128],
                                                      k.IDENT[0:P, 0:P])
                        ins.then_inc(pt_ready, 1)
                        if g % 5 == 4:
                            pe.drain().then_inc(phi_free, 1)
                        if g:
                            products(g - 1)
                    products(GROUPS - 1).then_inc(y_ready, 1)
                    pe.drain().then_inc(pht_free, 1)
                    pe.wait_ge(yo_ready, n + 1)
                    for c in range(KC):
                        ins = nc.tensor.transpose(PYT[:, c * P:c * P + P], YO[:, c * 128:c * 128 + 128], k.IDENT[0:P, 0:P])
                    ins.then_inc(yt_turned, 1)
                    pe.wait_ge(yt_ready, n + 1)
                    pe.wait_ge(out_free, n + 1)
                    for c in range(KC):
                        ins = nc.tensor.matmul(PO[:, 0:D], YT[:, c, :], s0.WPT[:, c, :], start=(c == 0), stop=(c == KC - 1))
                    ins.then_inc(out_ready, 1)

            @block.scalar
            def _(act):
                act.sem_inc(pt_free, 2)
                with act.Fori(0, T) as n:
                    act.wait_ge(pht_free, n + 1)
                    for g in range(GROUPS):
                        act.wait_ge(pt_ready, n * GROUPS + g + 1)
                        nc.scalar.activation(PHT[:, 4 * g:4 * g + 4, :],
                                             PT[:, g % 2, 0:4 * P].rearrange("p (q n) -> p q n", n=P), ACT.Copy
                                             ).then_inc(pht_ready, 1)
                        act.drain().then_inc(pt_free, 1)
                    act.wait_ge(yt_turned, n + 1)
                    nc.scalar.activation(YT[:], PYT[:, 0:KC * P].rearrange("p (c n) -> p c n", c=KC), ACT.Copy
                                         ).then_inc(yt_ready, 1)


GT = 5
GB = 5
EITERS = TE // (GT * GB)


def gather_loop(pool, nc, index, staged, table, idx, out, ready, frees, outs_done, go):
    with pool.Fori(0, EITERS) as i:
        for b in range(GB):
            n = i * GB + b
            frees(i, b, n)
            nc.gpsimd.tensor_copy(idx[:, b, :], index[:, bass.ds(n * GT, GT)]).then_inc(staged, 1)
            pool.wait_ge(staged, n + 1)
            pool.sem_inc(go, 1)
            for t in range(GT):
                nc.gpsimd.indirect_dma_start(out=out(b, t), out_offset=None, in_=table,
                                             in_offset=bass.IndirectOffsetOnAxis(ap=idx[:, b, t:t + 1], axis=0)
                                             ).then_inc(ready[b], 16)


def stage_edge_sums(k, table, width, weights):
    nc, a = k.nc, k.a
    with k.scope() as s:
        G = s.sb("G", [P, GB, GT, width])
        idx = s.sb("idx", [P, GB, GT], I32)
        sem = s.sem
        staged, go, loop_ready = sem("staged"), sem("go"), sem("loop_ready")
        rows = [s.gather_sem(f"rows{b}") for b in range(GB)]
        out = [sem(f"out{b}") for b in range(GB)]
        summed = sem("summed")
        run = k.run[:, 0:width].rearrange("(p t) d -> p t d", p=P)
        with nc.Block() as block:
            @block.gpsimd
            def _(pool):
                def frees(i, b, n):
                    pool.wait_ge(out[b], i * 16 + 16)
                    pool.wait_ge(summed, n + 2)
                gather_loop(pool, nc, k.SRC, staged, table, idx, lambda b, t: G[:, b, t, 0:D], rows, frees, out, go)

            @block.vector
            def _(v):
                v.memset(G[:, GB - 1, GT - 1, :], 0.0)
                v.drain()
                v.sem_inc(summed, GB)
                with v.Fori(0, EITERS) as i:
                    for b in range(GB):
                        n = i * GB + b
                        v.wait_ge(rows[b], i * 16 * GT + 16 * GT)
                        if weights is not None:
                            w = weights[:, :, bass.ds(n * GT, GT)].rearrange("p h t -> p t h")
                            v.tensor_copy(G[:, b, :, D:GW], w)
                            v.drain()
                            for t in range(GT):
                                g = G[:, b, t, 0:D].rearrange("p (h d) -> p h d", h=H)
                                v.tensor_tensor(g, g, bcast(G[:, b, t, D:GW], DH), ALU.mult)
                            v.drain()
                        for t in range(GT):
                            before = G[:, b, t - 1, :] if t else G[:, (b - 1) % GB, GT - 1, :]
                            ins = v.scalar_tensor_tensor(G[:, b, t, :], before, k.SAME[:, bass.ds(n * GT + t, 1)],
                                                         G[:, b, t, :], ALU.mult, ALU.add)
                            if t < GT - 1:
                                v.drain()
                        v.drain().then_inc(summed, 1)
                v.tensor_copy(k.RLAST[:, 0:width], G[:, GB - 1, GT - 1, :])

            @block.sync
            def _(sp):
                for b in range(GB):
                    sp.sem_inc(out[b], 16)
                with sp.Fori(0, EITERS) as i:
                    for b in range(GB):
                        n = i * GB + b
                        sp.wait_ge(summed, n + GB + 1)
                        sp.dma_start(run[:, bass.ds(n * GT, GT), :], G[:, b, :, :]).then_inc(out[b], 16)
                for b in range(GB):
                    sp.wait_ge(out[b], 16 * (EITERS + 1))


def open_nodes(v, k, out, base, n):
    return v.tensor_scalar(out, base, k.OPEN[:, bass.ds(n, 1)], None, ALU.is_equal)


def stage_layer0_nodes(k, s0):
    nc, a = k.nc, k.a
    with k.scope() as s:
        base = s.sb("base", [P, P])
        idx = s.sb("idx", [P, B], I32)
        G = s.sb("G", [P, B, D])
        GM = s.sb("GM", [P, B, P])
        bias = s.sb("bias", [P, D])
        PS = s.ps("PS", [P, B, 512])
        sem = s.sem
        loaded, staged, go, open_ready, sums_ready = (sem(x) for x in (
            "loaded", "staged", "go", "open_ready", "sums_ready"))
        rows = s.gather_sem("rows")
        with nc.Block() as block:
            @block.sync
            def _(sp):
                sp.dma_start(base[:], a["c_base"]).then_inc(loaded, 16)
                sp.wait_ge(loaded, 16)

            @block.gpsimd
            def _(pool):
                with pool.Fori(0, ITERS) as i:
                    pool.wait_ge(staged, i + 1)
                    pool.sem_inc(go, 1)
                    for b in range(B):
                        nc.gpsimd.indirect_dma_start(out=G[:, b, :], out_offset=None, in_=k.run0,
                                                     in_offset=bass.IndirectOffsetOnAxis(ap=idx[:, b:b + 1], axis=0)
                                                     ).then_inc(rows, 16)

            @block.tensor
            def _(pe):
                with pe.Fori(0, ITERS) as i:
                    for b in range(B):
                        pe.wait_ge(open_ready, i * B + b + 1)
                        nc.tensor.matmul(PS[:, b, 0:D], GM[:, b, :], k.RLAST[:, 0:D], start=True, stop=True
                                         ).then_inc(sums_ready, 1)

            @block.vector
            def _(v):
                v.wait_ge(loaded, 16)
                v.tensor_tensor(bias[:], s0.bsum[:, 0, :], s0.bsum[:, 1, :], ALU.add)
                with v.Fori(0, ITERS) as i:
                    v.drain()
                    v.tensor_copy(idx[:], k.LAST[:, bass.ds(i * B, B)]).then_inc(staged, 1)
                    for b in range(B):
                        open_nodes(v, k, GM[:, b, :], base[:], i * B + b).then_inc(open_ready, 1)
                    v.wait_ge(rows, (i + 1) * 16 * B)
                    for b in range(B):
                        n = i * B + b
                        v.wait_ge(sums_ready, n + 1)
                        v.tensor_tensor(G[:, b, :], G[:, b, :], PS[:, b, 0:D], ALU.add)
                        v.tensor_tensor(k.X[:, n, :], k.ACC[:, n, :], bias[:], ALU.add)
                        v.drain()
                        v.scalar_tensor_tensor(k.X[:, n, :], G[:, b, :], k.HAS[:, bass.ds(n, 1)], k.X[:, n, :],
                                               ALU.mult, ALU.add)




def stage_normalise(k, eps, XNT, ranked=None, XN=None, tables=None):
    nc, a = k.nc, k.a
    with k.scope() as s:
        s.stat = s.sb("stat", [P, B, 6])
        s.mv = s.sb("mv", [P, B, 2])
        XS = s.sb("XS", [P, B, D])
        XT = s.sb("XT", [128, B, KC, P])
        PT = s.ps("PT", [128, 3, 512])
        nt = len(tables or ())
        if tables:
            W = s.sb("W", [128, KC, nt * D])
            OUT = s.sb("OUT", [P, B, nt * D])
            PR = s.ps("PR", [P, 2, 512])
        if ranked:
            wr = s.sb("wr", [P, D])
            br = s.sb("br", [P, 1])
            prod = s.sb("prod", [P, D])
            w5 = s.sb("w5", [P, B])

        def pt(b):
            return PT[:, b % 3, 0:KC * P].rearrange("p (c n) -> p c n", c=KC)

        sem = s.sem
        loaded, var_ready, sd_ready = sem("loaded"), sem("var_ready"), sem("sd_ready")
        rows_ready, rows_free, rows_kept = sem("rows_ready"), sem("rows_free"), sem("rows_kept")
        turned_ready, turned_free = sem("turned_ready"), sem("turned_free")
        xt_ready, xt_free, xt_kept = sem("xt_ready"), sem("xt_free"), sem("xt_kept")
        proj_ready, pr_free = sem("proj_ready"), [sem("pr_free0"), sem("pr_free1")]
        out_ready, stored = sem("out_ready"), [sem(f"stored{b}") for b in range(B)]
        weights_ready = sem("weights_ready")
        nload = 16 * ((nt if tables else 0) + (2 if ranked else 0))
        with nc.Block() as block:
            @block.sync
            def _(sp):
                for m, (w, _) in enumerate(tables or ()):
                    sp.dma_start(W[:, :, m * D:(m + 1) * D], chunks(w)).then_inc(loaded, 16)
                if ranked:
                    sp.dma_start(wr[:], row(a["L0_ffn_wr"].rearrange("d o -> (d o)"), P)).then_inc(loaded, 16)
                    sp.dma_start(br[:], row(a["L0_ffn_br"], P)).then_inc(loaded, 16)
                if tables:
                    for b in range(B):
                        sp.sem_inc(stored[b], 16)
                    with sp.Fori(0, ITERS) as i:
                        for b in range(B):
                            n = i * B + b
                            sp.wait_ge(out_ready, n + 1)
                            for m, (_, table) in enumerate(tables):
                                sp.dma_start(node_rows(table)[:, n, :], OUT[:, b, m * D:(m + 1) * D]).then_inc(stored[b], 16)
                    for b in range(B):
                        sp.wait_ge(stored[b], 16 * (nt * ITERS + 1))
                if ranked:
                    sp.wait_ge(weights_ready, 1)
                    sp.dma_start(k.weights.rearrange("(p t) d -> p (t d)", p=P), ranked.selw[:]).then_inc(loaded, 16)
                    sp.wait_ge(loaded, nload + 16)

            @block.vector
            def _(v):
                node_stats(k, s, eps, var_ready, sd_ready)
                if ranked:
                    v.wait_ge(loaded, nload)
                with v.Fori(0, ITERS) as i:
                    for b in range(B):
                        n = i * B + b
                        v.wait_ge(rows_free, n + 1)
                        v.wait_ge(rows_kept, n + 1)
                        v.tensor_scalar(XS[:, b, :], k.X[:, n, :], k.MV[:, n, 0:1], k.RSTD[:, bass.ds(n, 1)],
                                        ALU.subtract, ALU.mult).then_inc(rows_ready, 1)
                        if ranked:
                            v.drain()
                            v.tensor_tensor_reduce(prod[:], XS[:, b, :], wr[:], 1.0, 0.0, ALU.mult, ALU.add,
                                                   w5[:, b:b + 1])
                    if ranked:
                        v.drain()
                        v.tensor_scalar(ranked.selw[:, bass.ds(i * B, B)], w5[:], br[:, 0:1], None, ALU.add)
                        v.drain()
                if ranked:
                    v.drain().then_inc(weights_ready, 1)

            @block.tensor
            def _(pe):
                pe.sem_inc(rows_free, B)
                pe.sem_inc(xt_free, B)
                if tables:
                    pe.wait_ge(loaded, nload)
                with pe.Fori(0, ITERS) as i:
                    for b in range(B):
                        n = i * B + b
                        pe.wait_ge(rows_ready, n + 1)
                        pe.wait_ge(turned_free, n + 1)
                        for c in range(KC):
                            ins = nc.tensor.transpose(pt(b)[:, c, :], XS[:, b, c * 128:c * 128 + 128], k.IDENT[0:P, 0:P])
                        ins.then_inc(turned_ready, 1)
                    for b in range(B if tables else 0):
                        n = i * B + b
                        pe.wait_ge(xt_ready, n + 1)
                        for half in range(2):
                            lo, hi = half * 512, min(half * 512 + 512, nt * D)
                            pe.wait_ge(pr_free[half], n + 1)
                            for c in range(KC):
                                ins = nc.tensor.matmul(PR[:, half, 0:hi - lo], XT[:, b, c, :], W[:, c, lo:hi],
                                                       start=(c == 0), stop=(c == KC - 1))
                            ins.then_inc(proj_ready, 1)
                        pe.drain().then_inc(xt_free, 1)

            @block.scalar
            def _(act):
                act.sem_inc(turned_free, 2)
                if tables:
                    act.sem_inc(pr_free[0], 1)
                    act.sem_inc(pr_free[1], 1)
                act.wait_ge(var_ready, 1)
                nc.scalar.activation(k.SD[:], k.RSTD[:], ACT.Sqrt).then_inc(sd_ready, 1)
                with act.Fori(0, ITERS) as i:
                    for b in range(B):
                        n = i * B + b
                        act.wait_ge(turned_ready, n + 1)
                        if tables:
                            act.wait_ge(xt_free, n + 1)
                            nc.scalar.activation(XT[:, b, :, :], pt(b), ACT.Copy).then_inc(xt_ready, 1)
                        nc.scalar.activation(XNT[:, :, bass.ds(n * P, P)], pt(b), ACT.Copy)
                        act.sem_inc(rows_free, 1)
                        act.drain().then_inc(turned_free, 1)
                    for b in range(B if tables else 0):
                        n = i * B + b
                        act.wait_ge(stored[b], 16 * (nt * i + 1))
                        for half in range(2):
                            lo, hi = half * 512, min(half * 512 + 512, nt * D)
                            act.wait_ge(proj_ready, 2 * n + half + 1)
                            nc.scalar.activation(OUT[:, b, lo:hi], PR[:, half, 0:hi - lo], ACT.Copy
                                                 ).then_inc(pr_free[half], 1)
                        act.drain().then_inc(out_ready, 1)

            @block.gpsimd
            def _(pool):
                pool.sem_inc(rows_kept, B)
                if XN is not None:
                    nc.gpsimd.memset(XN[:, :, D:D + 1], 1.0)
                if XN is not None or ranked:
                    with pool.Fori(0, ITERS) as i:
                        for b in range(B):
                            n = i * B + b
                            pool.wait_ge(rows_ready, n + 1)
                            if ranked:
                                nc.gpsimd.tensor_tensor(k.X[:, n, :], k.X[:, n, :], XS[:, b, :], ALU.add).then_inc(rows_kept, 1)
                            else:
                                nc.gpsimd.tensor_copy(XN[:, n, 0:D], XS[:, b, :]).then_inc(rows_kept, 1)
                else:
                    pool.sem_inc(rows_kept, T)


KEEP = int(0.5 * N) - 1


def stage_selection(k, f):
    nc, a = k.nc, k.a
    with k.scope() as s:
        wrow = s.sb("wrow", [P, N])
        scratch = s.sb("scratch", [P, N])
        gt = s.sb("gt", [P, T])
        ge = s.sb("ge", [P, T])
        tie = s.sb("tie", [P, T])
        ones = s.sb("ones", [P, T])
        upto = s.sb("upto", [P, T])
        after = s.sb("after", [P, P])
        PS = s.ps("PS", [P, 512])
        loaded, ties_ready, before_ready = s.sem("loaded"), s.sem("ties_ready"), s.sem("before_ready")
        with nc.Block() as block:
            @block.sync
            def _(sp):
                sp.dma_start(wrow[:], row(k.weights.rearrange("n d -> (n d)"), P)).then_inc(loaded, 16)
                sp.dma_start(after[:], a["c_after"]).then_inc(loaded, 16)
                sp.wait_ge(loaded, 32)

            @block.vector
            def _(v):
                v.memset(ones[:], 1.0)
                v.wait_ge(loaded, 32)
                for out, op in ((gt, ALU.is_gt), (ge, ALU.is_ge)):
                    for n in range(T):
                        v.drain()
                        v.tensor_scalar(scratch[:], wrow[:], f.selw[:, n:n + 1], 0.0, op, ALU.add,
                                        accum_out=out[:, n:n + 1])
                v.drain()
                v.tensor_scalar(tie[:], gt[:], float(KEEP), None, ALU.is_lt)
                v.drain()
                v.scalar_tensor_tensor(tie[:], ge[:], float(KEEP), tie[:], ALU.is_gt, ALU.mult)
                v.drain()
                v.tensor_tensor_scan(upto[:], ones[:], tie[:], 0.0, ALU.mult, ALU.add).then_inc(ties_ready, 1)
                v.wait_ge(before_ready, 1)
                v.tensor_tensor(upto[:], upto[:], tie[:], ALU.subtract)
                v.drain()
                v.tensor_scalar(upto[:], upto[:], PS[:, 0:1], None, ALU.add)
                v.drain()
                v.tensor_tensor(upto[:], upto[:], tie[:], ALU.mult)
                v.drain()
                v.tensor_tensor(gt[:], gt[:], upto[:], ALU.add)
                v.drain()
                v.scalar_tensor_tensor(f.selw[:], gt[:], float(KEEP), f.selw[:], ALU.is_lt, ALU.mult)

            @block.tensor
            def _(pe):
                pe.wait_ge(ties_ready, 1)
                nc.tensor.matmul(PS[:, 0:1], after[:], upto[:, T - 1:T], start=True, stop=True).then_inc(before_ready, 1)


PIECES = ((0, 3 * P), (3 * P, B * P))


def stage_layer0_ffn(k, f, XNT):
    nc, a = k.nc, k.a
    with k.scope() as s:
        W1 = s.sb("W1", [128, KC, HID])
        W2 = s.sb("W2", [128, HC, D])
        b1 = s.sb("b1", [128, HC])
        b2 = s.sb("b2", [P, D])
        HT = s.sb("HT", [128, HC, B * P])
        tmp = s.sb("tmp", [P, 2, D])
        HP = s.ps("HP", [128, 4, 512])
        YP = s.ps("YP", [P, 3, 512])
        sem = s.sem
        loaded, h_ready, h_free, ht_ready, ht_free, y_ready, y_free = (sem(x) for x in (
            "loaded", "h_ready", "h_free", "ht_ready", "ht_free", "y_ready", "y_free"))
        with nc.Block() as block:
            @block.sync
            def _(sp):
                sp.dma_start(W1[:], chunks(a["L0_ffn_w1"])).then_inc(loaded, 16)
                sp.dma_start(W2[:], chunks(a["L0_ffn_w2"])).then_inc(loaded, 16)
                sp.dma_start(b1[:], a["L0_ffn_b1"].rearrange("(c p) -> p c", p=128), allow_slow_non_contiguous=True).then_inc(loaded, 16)
                sp.dma_start(b2[:], row(a["L0_ffn_b2"], P)).then_inc(loaded, 16)
                sp.wait_ge(loaded, 64)

            @block.tensor
            def _(pe):
                pe.sem_inc(ht_free, 1)
                pe.wait_ge(loaded, 64)
                with pe.Fori(0, ITERS) as i:
                    for c in range(HC):
                        for q, (lo, hi) in enumerate(PIECES):
                            m = 2 * c + q
                            pe.wait_ge(h_free, i * 2 * HC + m + 1)
                            for kc in range(KC):
                                ins = nc.tensor.matmul(HP[:, m % 4, 0:hi - lo], W1[:, kc, c * 128:c * 128 + 128],
                                                       XNT[:, kc, bass.ds(i * B * P + lo, hi - lo)],
                                                       start=(kc == 0), stop=(kc == KC - 1))
                            ins.then_inc(h_ready, 1)
                    pe.wait_ge(ht_ready, (i + 1) * 2 * HC)
                    for b in range(B):
                        pe.wait_ge(y_free, i * B + b + 1)
                        for c in range(HC):
                            ins = nc.tensor.matmul(YP[:, b % 3, 0:D], HT[:, c, b * P:b * P + P], W2[:, c, :],
                                                   start=(c == 0), stop=(c == HC - 1))
                        ins.then_inc(y_ready, 1)
                    pe.drain().then_inc(ht_free, 1)

            @block.scalar
            def _(act):
                act.sem_inc(h_free, 4)
                act.wait_ge(loaded, 64)
                with act.Fori(0, ITERS) as i:
                    act.wait_ge(ht_free, i + 1)
                    for c in range(HC):
                        for q, (lo, hi) in enumerate(PIECES):
                            m = 2 * c + q
                            act.wait_ge(h_ready, i * 2 * HC + m + 1)
                            nc.scalar.activation(HT[:, c, lo:hi], HP[:, m % 4, 0:hi - lo], ACT.Gelu_apprx_tanh,
                                                 bias=b1[:, c:c + 1]).then_inc(h_free, 1)
                    act.drain().then_inc(ht_ready, 2 * HC)

            @block.vector
            def _(v):
                v.sem_inc(y_free, 2)
                v.wait_ge(loaded, 64)
                with v.Fori(0, ITERS) as i:
                    for b in range(B):
                        n = i * B + b
                        v.wait_ge(y_ready, n + 1)
                        v.tensor_tensor(tmp[:, b % 2, :], YP[:, b % 3, 0:D], b2[:], ALU.add)
                        v.drain().then_inc(y_free, 1)
                        v.scalar_tensor_tensor(k.X[:, n, :], tmp[:, b % 2, :], f.selw[:, bass.ds(n, 1)], k.X[:, n, :],
                                               ALU.mult, ALU.add)
                    v.drain()


def stage_experts(k, XNT, out):
    nc, a = k.nc, k.a
    NE = 8
    with k.scope() as s:
        W1 = s.sb("W1", [128, KC, HID])
        WG = s.sb("WG", [128, HC, NE])
        WD = s.sb("WD", [128, HC, NE, D])
        BD = s.sb("BD", [B * NE, B, D])
        b1 = s.sb("b1", [128, HC])
        bg = s.sb("bg", [P, NE])
        rev = s.sb("rev", [P, NE])
        HT = s.sb("HT", [128, HC, B * P])
        lg = s.sb("lg", [P, B, NE])
        key = s.sb("key", [P, B, NE])
        one = s.sb("one", [P, B])
        coef = s.sb("coef", [P, 16, NE])
        CT = s.sb("CT", [B * NE, P])
        HP = s.ps("HP", [128, 2, 512])
        YP = s.ps("YP", [P, 4, 512])
        LG = s.ps("LG", [P, 512])
        CB = s.ps("CB", [128, 512])
        sem = s.sem
        (loaded, zeroed, h_ready, h_free, ht_ready, ht_free, lg_ready, lg_free, coef_ready, ct_ready, ct_kept, bd_ready,
         bd_free, y_ready, y_free, x_ready, shifted, exp_ready, stored) = (sem(x) for x in (
             "loaded", "zeroed", "h_ready", "h_free", "ht_ready", "ht_free", "lg_ready", "lg_free", "coef_ready", "ct_ready",
             "ct_kept", "bd_ready", "bd_free", "y_ready", "y_free", "x_ready", "shifted", "exp_ready", "stored"))
        NL = 16 * (5 + NE + B)
        with nc.Block() as block:
            @block.sync
            def _(sp):
                sp.dma_start(W1[:], chunks(a["L1_ffn_W1"])).then_inc(loaded, 16)
                sp.dma_start(b1[:], a["L1_ffn_b1"].rearrange("(c p) -> p c", p=128), allow_slow_non_contiguous=True).then_inc(loaded, 16)
                sp.dma_start(WG[:], chunks(a["L1_ffn_Wg"])).then_inc(loaded, 16)
                sp.dma_start(bg[:], row(a["L1_ffn_bg"], P)).then_inc(loaded, 16)
                sp.dma_start(rev[:], a["c_reversed"]).then_inc(loaded, 16)
                for e in range(NE):
                    sp.dma_start(WD[:, :, e, :], chunks(a["L1_ffn_Wd"][e])).then_inc(loaded, 16)
                sp.wait_ge(zeroed, 1)
                for b in range(B):
                    sp.dma_start(BD[b * NE:(b + 1) * NE, b, :], a["L1_ffn_bd"]).then_inc(loaded, 16)
                sp.wait_ge(loaded, NL)
                with sp.Fori(0, T) as n:
                    sp.wait_ge(x_ready, n + 1)
                    sp.dma_start(node_rows(out)[:, n, :], k.X[:, n, :]).then_inc(stored, 16)
                sp.wait_ge(stored, 16 * T)

            @block.tensor
            def _(pe):
                pe.sem_inc(ht_free, 1)
                pe.wait_ge(loaded, NL)
                with pe.Fori(0, ITERS) as i:
                    for c in range(HC):
                        for q, (lo, hi) in enumerate(PIECES):
                            pe.wait_ge(h_free, i * 2 * HC + 2 * c + q + 1)
                            for kc in range(KC):
                                ins = nc.tensor.matmul(HP[:, q, 0:hi - lo], W1[:, kc, c * 128:c * 128 + 128],
                                                       XNT[:, kc, bass.ds(i * B * P + lo, hi - lo)],
                                                       start=(kc == 0), stop=(kc == KC - 1))
                            ins.then_inc(h_ready, 1)
                    pe.wait_ge(ht_ready, i + 1)
                    pe.wait_ge(lg_free, i + 1)
                    for b in range(B):
                        for c in range(HC):
                            ins = nc.tensor.matmul(LG[:, b * NE:(b + 1) * NE], HT[:, c, b * P:b * P + P], WG[:, c, :],
                                                   start=(c == 0), stop=(c == HC - 1))
                    ins.then_inc(lg_ready, 1)
                    for b in range(B):
                        for q in range(NE // 2):
                            pe.wait_ge(y_free, (i * B + b) * 4 + q + 1)
                            for c in range(HC):
                                ins = nc.tensor.matmul(YP[:, q, :], HT[:, c, b * P:b * P + P],
                                                       WD[:, c, 2 * q:2 * q + 2, :], start=(c == 0), stop=(c == HC - 1))
                            ins.then_inc(y_ready, 1)
                        if b == 0:
                            pe.wait_ge(coef_ready, i + 1)
                            pe.wait_ge(bd_free, i * B + 1)
                            nc.tensor.transpose(CB[:, D:D + P], coef[:].rearrange("p b e -> p (b e)"),
                                                k.IDENT[0:P, 0:P]).then_inc(ct_ready, 1)
                            pe.wait_ge(ct_kept, i + 1)
                        pe.wait_ge(bd_free, i * B + b + 1)
                        nc.tensor.matmul(CB[0:P, 0:D], CT[:], BD[:, b, :], start=True, stop=True).then_inc(bd_ready, 1)
                    pe.drain().then_inc(ht_free, 1)

            @block.scalar
            def _(act):
                act.sem_inc(h_free, 2)
                act.wait_ge(loaded, NL)
                with act.Fori(0, ITERS) as i:
                    act.wait_ge(ht_free, i + 1)
                    for c in range(HC):
                        for q, (lo, hi) in enumerate(PIECES):
                            act.wait_ge(h_ready, i * 2 * HC + 2 * c + q + 1)
                            nc.scalar.activation(HT[:, c, lo:hi], HP[:, q, 0:hi - lo], ACT.Gelu,
                                                 bias=b1[:, c:c + 1]).then_inc(h_free, 1)
                    act.drain().then_inc(ht_ready, 1)
                    act.wait_ge(shifted, i + 1)
                    nc.scalar.activation(lg[:], lg[:], ACT.Exp).then_inc(exp_ready, 1)
                    act.wait_ge(ct_ready, i + 1)
                    nc.scalar.activation(CT[:], CB[0:B * NE, D:D + P], ACT.Copy).then_inc(ct_kept, 1)

            @block.vector
            def _(v):
                v.memset(coef[:], 0.0)
                v.memset(BD[:], 0.0).then_inc(zeroed, 1)
                v.sem_inc(lg_free, 1)
                v.sem_inc(bd_free, 1)
                v.sem_inc(y_free, 4)
                v.wait_ge(loaded, NL)
                with v.Fori(0, ITERS) as i:
                    v.wait_ge(lg_ready, i + 1)
                    v.tensor_tensor(lg[:], LG[:, 0:B * NE].rearrange("p (b e) -> p b e", b=B),
                                    bg[:].unsqueeze(1).to_broadcast([P, B, NE]), ALU.add)
                    v.drain().then_inc(lg_free, 1)
                    v.tensor_reduce(one[:], lg[:], AX.X, ALU.max)
                    v.drain()
                    v.tensor_tensor(lg[:], lg[:], bcast(one[:], NE), ALU.subtract).then_inc(shifted, 1)
                    v.wait_ge(exp_ready, i + 1)
                    v.tensor_reduce(one[:], lg[:], AX.X, ALU.add)
                    v.drain()
                    v.reciprocal(one[:], one[:])
                    v.drain()
                    v.tensor_tensor(lg[:], lg[:], bcast(one[:], NE), ALU.mult)
                    v.drain()
                    v.tensor_reduce(one[:], lg[:], AX.X, ALU.max)
                    v.drain()
                    v.tensor_tensor(key[:], lg[:], bcast(one[:], NE), ALU.is_equal)
                    v.drain()
                    v.tensor_tensor(key[:], key[:], rev[:].unsqueeze(1).to_broadcast([P, B, NE]), ALU.mult)
                    v.drain()
                    v.tensor_reduce(one[:], key[:], AX.X, ALU.max)
                    v.drain()
                    v.tensor_tensor(key[:], key[:], bcast(one[:], NE), ALU.is_equal)
                    v.drain()
                    v.tensor_tensor(coef[:, 0:B, :], key[:], lg[:], ALU.mult).then_inc(coef_ready, 1)
                    v.drain()
                    for b in range(B):
                        n = i * B + b
                        for q in range(NE // 2):
                            v.wait_ge(y_ready, n * 4 + q + 1)
                            for e in range(2):
                                v.scalar_tensor_tensor(k.X[:, n, :], YP[:, q, e * D:(e + 1) * D],
                                                       coef[:, b, 2 * q + e:2 * q + e + 1], k.X[:, n, :], ALU.mult, ALU.add)
                                last = v.drain()
                            last.then_inc(y_free, 1)
                        v.wait_ge(bd_ready, n + 1)
                        v.tensor_tensor(k.X[:, n, :], k.X[:, n, :], CB[0:P, 0:D], ALU.add).then_inc(x_ready, 1)
                        v.drain().then_inc(bd_free, 1)


SCALE1 = DH ** -0.5
KD = 256
QSCALE = KD ** -0.25
EPS_ATT = 1e-6
LN_SQRT_M = float(0.5 * np.log(256.0))


def stage_scores(k, S):
    nc, a = k.nc, k.a
    with k.scope() as s:
        GK = s.sb("GK", [P, GB, GT, D])
        GQ = s.sb("GQ", [P, GB, GT, D])
        ki = s.sb("ki", [P, GB, GT], I32)
        qi = s.sb("qi", [P, GB, GT], I32)
        sem = s.sem
        staged, go, used, multiplied = sem("staged"), sem("go"), sem("used"), sem("multiplied")
        rows = [s.gather_sem(f"rows{b}") for b in range(GB)]
        with nc.Block() as block:
            @block.gpsimd
            def _(pool):
                with pool.Fori(0, EITERS) as i:
                    for b in range(GB):
                        n = i * GB + b
                        pool.wait_ge(used, n + 1)
                        nc.gpsimd.tensor_copy(ki[:, b, :], k.SRC[:, bass.ds(n * GT, GT)]).then_inc(staged, 1)
                        nc.gpsimd.tensor_copy(qi[:, b, :], k.DST[:, bass.ds(n * GT, GT)]).then_inc(staged, 1)
                        pool.wait_ge(staged, 2 * n + 2)
                        pool.sem_inc(go, 1)
                        for t in range(GT):
                            for out, table, idx in ((GK, k.keys, ki), (GQ, k.queries, qi)):
                                nc.gpsimd.indirect_dma_start(out=out[:, b, t, :], out_offset=None, in_=table,
                                                             in_offset=bass.IndirectOffsetOnAxis(ap=idx[:, b, t:t + 1], axis=0)
                                                             ).then_inc(rows[b], 16)

            @block.vector
            def _(v):
                v.sem_inc(used, GB)
                with v.Fori(0, EITERS) as i:
                    for b in range(GB):
                        n = i * GB + b
                        v.wait_ge(rows[b], (i + 1) * 32 * GT)
                        v.tensor_tensor(GK[:, b, :, :], GK[:, b, :, :], GQ[:, b, :, :], ALU.mult)
                        v.drain()
                        v.tensor_reduce(S[:, :, bass.ds(n * GT, GT)].rearrange("p h t -> p t h"),
                                        GK[:, b, :, :].rearrange("p t (h d) -> p t h d", h=H), AX.X, ALU.add
                                        ).then_inc(used, 1)


def stage_edge_weights(k, S):
    nc, a = k.nc, k.a
    with k.scope() as s:
        F = s.sb("F", [P, H, TE])
        R = s.sb("R", [P, H, TE])
        forward = s.sb("forward", [P, TE])
        backward = s.sb("backward", [P, TE])
        ends = s.sb("ends", [P, H, P])
        masked = s.sb("masked", [P, H, P])
        ones = s.sb("ones", [P, P])
        carry = s.sb("carry", [P, 2, H])
        PS = s.ps("PS", [P, 2, 512])
        scaled, less, ends_ready, spread = s.sem("scaled"), s.sem("less"), s.sem("ends_ready"), s.sem("spread")
        with nc.Block() as block:
            @block.scalar
            def _(act):
                nc.scalar.activation(S[:], S[:], ACT.Copy, scale=SCALE1).then_inc(scaled, 1)
                act.wait_ge(less, 1)
                nc.scalar.activation(S[:], S[:], ACT.Exp)

            @block.tensor
            def _(pe):
                for r in range(2):
                    pe.wait_ge(ends_ready, r + 1)
                    for q in range(2):
                        ins = nc.tensor.matmul(PS[:, q, 0:4 * P], ones[:], ends[:, 4 * q:4 * q + 4, :], start=True, stop=True)
                    ins.then_inc(spread, 1)

            @block.vector
            def _(v):
                v.memset(ones[:], 1.0)
                v.tensor_copy(forward[:, 1:TE], k.SAME[:, 1:TE])
                v.memset(forward[:, 0:1], 1.0)
                v.tensor_copy(backward[:, 0:TE - 1], k.SAME[:, 1:TE])
                v.memset(backward[:, TE - 1:TE], 1.0)
                v.drain()
                v.wait_ge(scaled, 1)

                def scans(first):
                    for h in range(H):
                        start = (0.0, 0.0) if first else (carry[:, 0, h:h + 1], carry[:, 1, h:h + 1])
                        v.tensor_tensor_scan(F[:, h, :], forward[:], S[:, h, :], start[0], ALU.mult, ALU.max)
                        v.tensor_tensor_scan(R[:, h, ::-1], backward[:, ::-1], S[:, h, ::-1], start[1], ALU.mult, ALU.max)
                    v.drain()
                scans(True)
                for r, (edge, mask) in enumerate(((F[:, :, TE - 1], k.FROM_LEFT), (R[:, :, 0], k.FROM_RIGHT))):
                    v.tensor_tensor(ends[:], k.IDENT[0:P, 0:P].unsqueeze(1).to_broadcast([P, H, P]),
                                    bcast(edge, P), ALU.mult).then_inc(ends_ready, 1)
                    v.wait_ge(spread, r + 1)
                    for q in range(2):
                        v.tensor_tensor(masked[:, 4 * q:4 * q + 4, :], PS[:, q, 0:4 * P].rearrange("p (h n) -> p h n", h=4),
                                        mask[:].unsqueeze(1).to_broadcast([P, 4, P]), ALU.mult)
                    v.drain()
                    v.tensor_reduce(carry[:, r, :], masked[:], AX.X, ALU.max)
                    v.drain()
                scans(False)
                v.tensor_tensor(F[:], F[:], R[:], ALU.max)
                v.drain()
                v.tensor_tensor(S[:], S[:], F[:], ALU.subtract).then_inc(less, 1)


def stage_post(k, ones, fetch_blocks, nh, act_func, w1, bb1, w2, bb2, g1, be1, g2, be2, eps, graph, XN, add0):
    nc, a = k.nc, k.a
    with k.scope() as s:
        W1 = s.sb("W1", [128, KC, nh * 128])
        W2 = s.sb("W2", [128, nh, D])
        b1 = s.sb("b1", [128, nh])
        vec = s.sb("vec", [P, 6, D])
        R = s.sb("R", [P, B, D])
        RT = s.sb("RT", [128, KC, B, P])
        HT = s.sb("HT", [128, nh, B * P])
        stat = s.sb("stat", [P, B, 6])
        mv = s.sb("mv", [P, B, 2])
        var = s.sb("var", [P, B])
        sd = s.sb("sd", [P, B])
        PT = s.ps("PT", [128, 3, 512])
        PY = s.ps("PY", [P, 3, 512])
        HP = s.ps("HP", [128, 2, 512])
        if graph:
            WO = s.sb("WO", [128, KC, D])
            base = s.sb("base", [P, P])
            idx = s.sb("idx", [P, B], I32)
            G = s.sb("G", [P, B, GW])
            GM = s.sb("GM", [P, B, P])
        sem = s.sem
        (loaded, staged, go, open_ready, sums_ready, a_ready, at_ready, att_ready, n_var, n_sd, r_ready, rt_turned,
         rt_ready, h_ready, h_free, ht_ready, y_ready, msg_turned, sums_used) = (sem(x) for x in (
             "loaded", "staged", "go", "open_ready", "sums_ready", "a_ready", "at_ready", "att_ready", "n_var", "n_sd",
             "r_ready", "rt_turned", "rt_ready", "h_ready", "h_free", "ht_ready", "y_ready", "msg_turned", "sums_used"))
        rows = s.gather_sem("rows")
        NL = 16 * (9 + (2 if graph else 0))

        def pty(ps, b, w):
            return ps[:, b // 2, (b % 2) * 256:(b % 2) * 256 + w]

        with nc.Block() as block:
            @block.sync
            def _(sp):
                sp.dma_start(W1[:], chunks(w1)).then_inc(loaded, 16)
                sp.dma_start(W2[:], chunks(w2)).then_inc(loaded, 16)
                sp.dma_start(b1[:], bb1.rearrange("(c p) -> p c", p=128), allow_slow_non_contiguous=True).then_inc(loaded, 16)
                for m, x in enumerate((add0, g1, be1, bb2, g2, be2)):
                    sp.dma_start(vec[:, m, :], row(x, P)).then_inc(loaded, 16)
                if graph:
                    sp.dma_start(WO[:], chunks(a["L1_gnn_Wo_w"])).then_inc(loaded, 16)
                    sp.dma_start(base[:], a["c_base"]).then_inc(loaded, 16)
                sp.wait_ge(loaded, NL)

            if graph:
                @block.gpsimd
                def _(pool):
                    with pool.Fori(0, ITERS) as i:
                        pool.wait_ge(staged, i + 1)
                        pool.sem_inc(go, 1)
                        for b in range(B):
                            nc.gpsimd.indirect_dma_start(out=G[:, b, :], out_offset=None, in_=k.run,
                                                         in_offset=bass.IndirectOffsetOnAxis(ap=idx[:, b:b + 1], axis=0)
                                                         ).then_inc(rows, 16)

            def turn(pe, src, ready):
                for b in range(B):
                    for c in range(KC):
                        ins = nc.tensor.transpose(pty(PT, b, 250)[:, c * P:c * P + P], src[:, b, c * 128:c * 128 + 128],
                                                  k.IDENT[0:P, 0:P])
                ins.then_inc(ready, 1)

            def keep_turned(act, ready):
                for b in range(B):
                    ins = nc.scalar.activation(RT[:, :, b, :], pty(PT, b, 250).rearrange("p (c n) -> p c n", c=KC), ACT.Copy)
                ins.then_inc(ready, 1)

            @block.tensor
            def _(pe):
                pe.wait_ge(loaded, NL)
                with pe.Fori(0, ITERS) as i:
                    if graph:
                        for b in range(B):
                            pe.wait_ge(open_ready, i * B + b + 1)
                            pe.wait_ge(sums_used, i * B + b + 1)
                            nc.tensor.matmul(HP[0:P, b % 2, 0:GW], GM[:, b, :], k.RLAST[:], start=True, stop=True
                                             ).then_inc(sums_ready, 1)
                        pe.wait_ge(a_ready, i + 1)
                        turn(pe, G, msg_turned)
                        pe.wait_ge(at_ready, i + 1)
                        for b in range(B):
                            for c in range(KC):
                                ins = nc.tensor.matmul(pty(PY, b, D), RT[:, c, b, :], WO[:, c, :], start=(c == 0), stop=(c == KC - 1))
                        ins.then_inc(att_ready, 1)
                    pe.wait_ge(r_ready, i + 1)
                    turn(pe, R, rt_turned)
                    pe.wait_ge(rt_ready, i + 1)
                    for c in range(nh):
                        for q, (lo, hi) in enumerate(PIECES):
                            pe.wait_ge(h_free, i * 2 * nh + 2 * c + q + 1)
                            for kc in range(KC):
                                ins = nc.tensor.matmul(HP[:, q, 0:hi - lo], W1[:, kc, c * 128:c * 128 + 128],
                                                       RT[:, kc, lo // P:hi // P, :], start=(kc == 0), stop=(kc == KC - 1))
                            ins.then_inc(h_ready, 1)
                    pe.wait_ge(ht_ready, i + 1)
                    for b in range(B):
                        for c in range(nh):
                            ins = nc.tensor.matmul(pty(PY, b, D), HT[:, c, b * P:b * P + P], W2[:, c, :],
                                                   start=(c == 0), stop=(c == nh - 1))
                    ins.then_inc(y_ready, 1)

            @block.scalar
            def _(act):
                act.sem_inc(h_free, 2)
                act.wait_ge(loaded, NL)
                with act.Fori(0, ITERS) as i:
                    if graph:
                        act.wait_ge(msg_turned, i + 1)
                        keep_turned(act, at_ready)
                    act.wait_ge(n_var, 2 * i + 1)
                    nc.scalar.activation(sd[:], var[:], ACT.Sqrt).then_inc(n_sd, 1)
                    act.wait_ge(rt_turned, i + 1)
                    keep_turned(act, rt_ready)
                    for c in range(nh):
                        for q, (lo, hi) in enumerate(PIECES):
                            act.wait_ge(h_ready, i * 2 * nh + 2 * c + q + 1)
                            nc.scalar.activation(HT[:, c, lo:hi], HP[:, q, 0:hi - lo], act_func,
                                                 bias=b1[:, c:c + 1]).then_inc(h_free, 1)
                    act.drain().then_inc(ht_ready, 1)
                    act.wait_ge(n_var, 2 * i + 2)
                    nc.scalar.activation(sd[:], var[:], ACT.Sqrt).then_inc(n_sd, 1)

            def wide(m):
                return vec[:, m, :].unsqueeze(1).to_broadcast([P, B, D])

            @block.vector
            def _(v):
                def layernorm(i, which, gm):
                    for b in range(B):
                        v.bn_stats(stat[:, b, :], R[:, b, :])
                    v.drain()
                    for b in range(B):
                        v.bn_aggr(mv[:, b, :], stat[:, b, :])
                    v.drain()
                    v.tensor_scalar(var[:], mv[:, :, 1], eps, None, ALU.add).then_inc(n_var, 1)
                    v.wait_ge(n_sd, 2 * i + which + 1)
                    v.reciprocal(var[:], sd[:])
                    v.drain()
                    for b in range(B):
                        v.tensor_scalar(R[:, b, :], R[:, b, :], mv[:, b, 0:1], var[:, b:b + 1], ALU.subtract, ALU.mult)
                    v.drain()
                    v.tensor_tensor(R[:], R[:], wide(gm), ALU.mult)
                    v.drain()
                    v.tensor_tensor(R[:], R[:], wide(gm + 1), ALU.add)
                    return v.drain()

                v.sem_inc(sums_used, 2)
                v.wait_ge(loaded, NL)
                with v.Fori(0, ITERS) as i:
                    if graph:
                        v.tensor_copy(idx[:], k.LAST[:, bass.ds(i * B, B)]).then_inc(staged, 1)
                        for b in range(B):
                            open_nodes(v, k, GM[:, b, :], base[:], i * B + b).then_inc(open_ready, 1)
                        v.wait_ge(rows, (i + 1) * 16 * B)
                        for b in range(B):
                            v.wait_ge(sums_ready, i * B + b + 1)
                            v.tensor_tensor(G[:, b, :], G[:, b, :], HP[0:P, b % 2, 0:GW], ALU.add)
                            v.drain().then_inc(sums_used, 1)
                        v.tensor_scalar(G[:, :, D:GW], G[:, :, D:GW], 1e-8, None, ALU.add)
                        v.drain()
                        v.reciprocal(G[:, :, D:GW], G[:, :, D:GW])
                        v.drain()
                        for b in range(B):
                            g = G[:, b, 0:D].rearrange("p (h d) -> p h d", h=H)
                            v.tensor_tensor(g, g, bcast(G[:, b, D:GW], DH), ALU.mult)
                        v.drain()
                        for b in range(B):
                            v.tensor_scalar(G[:, b, 0:D], G[:, b, 0:D], k.HAS[:, bass.ds(i * B + b, 1)], None, ALU.mult)
                        v.drain().then_inc(a_ready, 1)
                        v.wait_ge(att_ready, i + 1)
                        for b in range(B):
                            v.tensor_tensor(R[:, b, :], pty(PY, b, D), XN[:, i * B + b, 0:D], ALU.add)
                    else:
                        v.tensor_tensor(R[:], k.ACC[:, bass.ds(i * B, B), :], XN[:, bass.ds(i * B, B), 0:D], ALU.add)
                    v.drain()
                    v.tensor_tensor(R[:], R[:], wide(0), ALU.add)
                    v.drain()
                    layernorm(i, 0, 1).then_inc(r_ready, 1)
                    v.wait_ge(y_ready, i + 1)
                    for b in range(B):
                        v.tensor_tensor(R[:, b, :], R[:, b, :], pty(PY, b, D), ALU.add)
                    v.drain()
                    v.tensor_tensor(R[:], R[:], wide(3), ALU.add)
                    v.drain()
                    layernorm(i, 1, 4)
                    v.tensor_tensor(k.X[:, bass.ds(i * B, B), :], k.X[:, bass.ds(i * B, B), :], R[:], ALU.add)
                    v.drain()


def stage_linear_attention(k, XN, XNT):
    nc, a = k.nc, k.a
    CB = B * P
    with k.scope() as s:
        WQ = s.sb("WQ", [128, KC, KD])
        WK = s.sb("WK", [128, KC, KD])
        WV = s.sb("WV", [128, KC, KD])
        WO = s.sb("WO", [128, KC, D])
        bv = s.sb("bv", [1, KD])
        PR = s.sb("PR", [128, 2, KD])
        PJ = s.sb("PJ", [128, KC, KD])
        bqk = s.sb("bqk", [128, 2, H, KC])
        bcur = s.sb("bcur", [128, 2, KC])
        half = s.sb("half", [128, 128])
        shift = s.sb("shift", [128, 1])
        QT = s.sb("QT", [128, KC, CB])
        SQ = s.sb("SQ", [128, KC, CB])
        PH = s.sb("PH", [128, 2, CB])
        PK = s.sb("PK", [P, 3, KD])
        nb = s.sb("nb", [P, 3])
        AS = s.sb("AS", [128, 2, D + 1])
        AT = s.sb("AT", [128, KC, KD])
        AL = s.sb("AL", [1, KD])
        KVT = s.sb("KVT", [128, KC, KD])
        KO = s.sb("KO", [128, 2, D + 1])
        rz = s.sb("rz", [P, 3])
        CP = s.ps("CP", [128, 2, 512])
        UP = s.ps("UP", [128, 3, 512])
        AP = s.ps("AP", [128, 2, 512])
        TP = s.ps("TP", [128, 512])
        sem = s.sem
        (loaded, proj_turned, proj_kept, ready0, wk_loaded, wq_loaded, wvo_loaded, k_used, q_used, vo_used,
         c_ready, c_free, qt_ready, qt_free, sq_ready, u_ready, u_read, pk_exp, pk_ready, a_zeroed, a_ready, as_ready,
         t_ready, t_kept, kv_ready, kv_kept, ko_ready, ko_kept, c_u_free, ph_exp, ph_ready, ph_free, o_ready, nb_ready,
         pk_free, u_free, begun) = (
            sem(x) for x in (
                "loaded", "proj_turned", "proj_kept", "ready0", "wk_loaded", "wq_loaded", "wvo_loaded", "k_used", "q_used",
                "vo_used", "c_ready", "c_free", "qt_ready", "qt_free", "sq_ready", "u_ready", "u_read", "pk_exp", "pk_ready",
                "a_zeroed", "a_ready", "as_ready", "t_ready", "t_kept", "kv_ready", "kv_kept", "ko_ready", "ko_kept", "c_u_free",
                "ph_exp", "ph_ready", "ph_free", "o_ready", "nb_ready", "pk_free", "u_free", "begun"))
        QTS, CPS = 2 * ITERS, 4 * ITERS + 8 * ITERS

        with nc.Block() as block:
            @block.sync
            def _(sp):
                sp.dma_start(PR[:], chunks(a["L1_mix_proj"])).then_inc(loaded, 16)
                for m, x in enumerate((a["L1_mix_bq"], a["L1_mix_bk"])):
                    for c in range(KC):
                        sp.dma_start(bqk[:, m, :, c], x.rearrange("h (c p) -> c p h", p=128)[c],
                                     allow_slow_non_contiguous=True).then_inc(loaded, 16)
                with sp.Fori(0, H) as h:
                    sp.wait_ge(k_used, h + 1)
                    sp.dma_start(WK[:], chunks(a["L1_mix_Wk"].rearrange("p h n -> p (h n)"))[:, :, bass.ds(h * KD, KD)]).then_inc(wk_loaded, 16)
                    sp.wait_ge(vo_used, h + 1)
                    sp.dma_start(WV[:], chunks(a["L1_mix_Wv"].rearrange("p h n -> p (h n)"))[:, :, bass.ds(h * KD, KD)]).then_inc(wvo_loaded, 16)
                    sp.dma_start(WO[:], a["L1_mix_Wo"].rearrange("h (c p) n -> h p c n", p=128)[h]).then_inc(wvo_loaded, 16)
                    sp.dma_start(bv[:], a["L1_mix_bv"][bass.ds(h, 1), :]).then_inc(wvo_loaded, 16)
                    sp.wait_ge(q_used, h + 1)
                    sp.dma_start(WQ[:], chunks(a["L1_mix_Wq"].rearrange("p h n -> p (h n)"))[:, :, bass.ds(h * KD, KD)]).then_inc(wq_loaded, 16)
                sp.wait_ge(wq_loaded, 16 * H)

            @block.tensor
            def _(pe):
                for free in (qt_free, k_used, vo_used, q_used):
                    pe.sem_inc(free, 1)
                pe.sem_inc(pk_free, 3)
                pe.sem_inc(ph_free, 1)
                pe.wait_ge(loaded, 80)
                for r in range(2):
                    for c in range(KC):
                        ins = nc.tensor.transpose(AP[:, r, c * 128:c * 128 + 128], PR[:, r, c * 128:c * 128 + 128], k.IDENT[:])
                ins.then_inc(proj_turned, 1)
                pe.wait_ge(ready0, 1)

                def turned(W, base_c, i):
                    for c in range(KC):
                        for q, (lo, hi) in enumerate(PIECES):
                            pe.wait_ge(c_free, base_c + 2 * c + q + 1)
                            for kc in range(KC):
                                ins = nc.tensor.matmul(CP[:, q, 0:hi - lo], W[:, kc, c * 128:c * 128 + 128],
                                                       XNT[:, kc, bass.ds(i * CB + lo, hi - lo)],
                                                       start=(kc == 0), stop=(kc == KC - 1))
                            ins.then_inc(c_ready, 1)

                with pe.Fori(0, H) as h:
                    pe.wait_ge(wk_loaded, 16 * h + 16)
                    pe.wait_ge(a_zeroed, h + 1)
                    pe.sem_inc(begun, 1)
                    with pe.Fori(0, ITERS) as i:
                        turned(WK, h * CPS + i * 4, i)
                        pe.wait_ge(sq_ready, h * QTS + i + 1)
                        for b in range(B):
                            n = h * 2 * T + i * B + b
                            pe.wait_ge(u_free, n + 1)
                            for kc in range(KC):
                                nc.tensor.matmul(UP[0:P, b % 3, 0:KD], QT[:, kc, b * P:b * P + P], PJ[:, kc, :],
                                                 start=(kc == 0), stop=(kc == KC - 1))
                            for kc in range(KC):
                                ins = nc.tensor.matmul(UP[0:P, b % 3, KD:KD + 1], SQ[:, kc, b * P:b * P + P], half[:, 0:1],
                                                       start=(kc == 0), stop=(kc == KC - 1))
                            ins.then_inc(u_ready, 1)
                            if b:
                                a_sum(pe, nc, h, i, b - 1, pk_ready, pk_free, AP, PK, XN)
                        a_sum(pe, nc, h, i, B - 1, pk_ready, pk_free, AP, PK, XN)
                        pe.drain().then_inc(qt_free, 1)
                    pe.drain().then_inc(a_ready, 1)
                    pe.sem_inc(k_used, 1)
                    pe.wait_ge(as_ready, h + 1)
                    for c in range(KC):
                        for r in range(2):
                            ins = nc.tensor.transpose(TP[:, c * 256 + r * 128:c * 256 + r * 128 + 128],
                                                      AS[:, r, c * 128:c * 128 + 128], k.IDENT[:])
                    ins.then_inc(t_ready, 1)
                    pe.wait_ge(t_kept, 2 * h + 1)
                    for r in range(2):
                        ins = nc.tensor.transpose(TP[0:1, r * 128:r * 128 + 128], AS[:, r, D:D + 1], k.IDENT[:])
                    ins.then_inc(t_ready, 1)
                    pe.wait_ge(t_kept, 2 * h + 2)
                    pe.wait_ge(wvo_loaded, 48 * h + 48)
                    for c in range(KC):
                        for kc in range(KC):
                            nc.tensor.matmul(TP[:, c * 256:c * 256 + 256], WV[:, kc, c * 128:c * 128 + 128], AT[:, kc, :],
                                             start=(kc == 0), stop=False)
                        ins = nc.tensor.matmul(TP[:, c * 256:c * 256 + 256], bv[:, c * 128:c * 128 + 128], AL[:],
                                               start=False, stop=True)
                    ins.then_inc(kv_ready, 1)
                    pe.wait_ge(kv_kept, h + 1)
                    for r in range(2):
                        for kc in range(KC):
                            ins = nc.tensor.matmul(TP[:, r * 256:r * 256 + 256], KVT[:, kc, r * 128:r * 128 + 128], WO[:, kc, :],
                                                   start=(kc == 0), stop=(kc == KC - 1))
                    ins.then_inc(ko_ready, 1)
                    pe.drain().then_inc(vo_used, 1)
                    pe.wait_ge(wq_loaded, 16 * h + 16)
                    pe.sem_inc(begun, 1)
                    with pe.Fori(0, ITERS) as i:
                        cbase = h * CPS + 4 * ITERS + i * 8
                        turned(WQ, cbase, i)
                        pe.wait_ge(sq_ready, h * QTS + ITERS + i + 1)
                        for r in range(2):
                            for q, (lo, hi) in enumerate(PIECES):
                                pe.wait_ge(c_free, cbase + 4 + 2 * r + q + 1)
                                for kc in range(KC):
                                    nc.tensor.matmul(CP[:, q, 0:hi - lo], PJ[:, kc, r * 128:r * 128 + 128], QT[:, kc, lo:hi],
                                                     start=(kc == 0), stop=False)
                                nc.tensor.matmul(CP[:, q, 0:hi - lo], half[:], SQ[:, 0, lo:hi],
                                                 start=False, stop=True).then_inc(c_ready, 1)
                        pe.drain().then_inc(qt_free, 1)
                        pe.wait_ge(ph_ready, h * ITERS + i + 1)
                        pe.wait_ge(ko_kept, h + 1)
                        for b in range(B):
                            n = h * 2 * T + T + i * B + b
                            pe.wait_ge(u_free, n + 1)
                            for r in range(2):
                                ins = nc.tensor.matmul(UP[0:P, b % 3, 0:D + 1], PH[:, r, b * P:b * P + P], KO[:, r, :],
                                                       start=(r == 0), stop=(r == 1))
                            ins.then_inc(o_ready, 1)
                        pe.drain().then_inc(ph_free, 1)
                    pe.sem_inc(q_used, 1)

            @block.scalar
            def _(act):
                act.sem_inc(c_free, 2)
                act.wait_ge(ready0, 1)

                def turned(m, h, i, item, cbase):
                    act.wait_ge(qt_free, item + 1)
                    for c in range(KC):
                        for q, (lo, hi) in enumerate(PIECES):
                            act.wait_ge(c_ready, cbase + 2 * c + q + 1)
                            nc.scalar.activation(QT[:, c, lo:hi], CP[:, q, 0:hi - lo], ACT.Identity, scale=QSCALE,
                                                 bias=bcur[:, m, c:c + 1]).then_inc(c_free, 1)
                    act.drain().then_inc(qt_ready, 1)

                with act.Fori(0, H) as h:
                    nc.scalar.activation(bcur[:], bqk[:, :, h, :], ACT.Copy)
                    act.drain()
                    with act.Fori(0, ITERS) as i:
                        turned(1, h, i, h * QTS + i, h * CPS + i * 4)
                        for b in range(B):
                            n = h * T + i * B + b
                            act.wait_ge(pk_free, n + 1)
                            act.wait_ge(nb_ready, n + 1)
                            nc.scalar.activation(PK[:, b % 3, :], UP[0:P, b % 3, 0:KD], ACT.Exp, bias=nb[:, b % 3:b % 3 + 1]
                                                 ).then_inc(pk_exp, 1)
                    act.wait_ge(a_ready, h + 1)
                    nc.scalar.activation(AS[:], AP[:, :, 0:D + 1], ACT.Copy).then_inc(as_ready, 1)
                    act.wait_ge(t_ready, 2 * h + 1)
                    nc.scalar.activation(AT[:], TP[:].rearrange("p (c m) -> p c m", c=KC), ACT.Copy).then_inc(t_kept, 1)
                    act.wait_ge(t_ready, 2 * h + 2)
                    nc.scalar.activation(AL[:], TP[0:1, 0:KD], ACT.Copy).then_inc(t_kept, 1)
                    act.wait_ge(kv_ready, h + 1)
                    nc.scalar.activation(KVT[:], TP[:].rearrange("p (c m) -> p c m", c=KC), ACT.Copy).then_inc(kv_kept, 1)
                    act.wait_ge(ko_ready, h + 1)
                    nc.scalar.activation(KO[:, :, 0:D], TP[:].rearrange("p (c m) -> p c m", c=2), ACT.Copy)
                    nc.scalar.activation(KO[:, :, D:D + 1], AS[:, :, D:D + 1], ACT.Copy)
                    act.drain().then_inc(ko_kept, 1)
                    with act.Fori(0, ITERS) as i:
                        cbase = h * CPS + 4 * ITERS + i * 8
                        turned(0, h, i, h * QTS + ITERS + i, cbase)
                        act.wait_ge(ph_free, h * ITERS + i + 1)
                        for r in range(2):
                            for q, (lo, hi) in enumerate(PIECES):
                                act.wait_ge(c_ready, cbase + 4 + 2 * r + q + 1)
                                nc.scalar.activation(PH[:, r, lo:hi], CP[:, q, 0:hi - lo], ACT.Exp, bias=shift[:, 0:1]
                                                     ).then_inc(c_free, 1)
                        act.drain().then_inc(ph_exp, 1)

            @block.vector
            def _(v):
                v.memset(half[:], -0.5)
                v.memset(shift[:], -LN_SQRT_M)
                v.wait_ge(proj_turned, 1)
                v.tensor_copy(PJ[:].rearrange("p c (r m) -> p r c m", r=2), AP[:, :, 0:256].rearrange("p r (c m) -> p r c m", c=KC))
                v.tensor_scalar(bqk[:], bqk[:], QSCALE, None, ALU.mult)
                v.drain()
                v.memset(AP[:], 0.0)
                v.memset(k.ACC[:], 0.0)
                v.sem_inc(u_free, 2)
                v.sem_inc(a_zeroed, 1)
                v.drain().then_inc(ready0, 1)
                with v.Fori(0, H) as h:
                    with v.Fori(0, ITERS) as i:
                        v.wait_ge(qt_ready, h * QTS + i + 1)
                        v.tensor_tensor(SQ[:], QT[:], QT[:], ALU.mult).then_inc(sq_ready, 1)
                        for b in range(B):
                            n = h * T + i * B + b
                            v.wait_ge(u_ready, n + 1)
                            v.tensor_scalar(nb[:, b % 3:b % 3 + 1], UP[0:P, b % 3, KD:KD + 1], -LN_SQRT_M, None, ALU.add
                                            ).then_inc(nb_ready, 1)
                            v.wait_ge(pk_exp, n + 1)
                            v.sem_inc(u_free, 1)
                            v.tensor_scalar(PK[:, b % 3, :], PK[:, b % 3, :], EPS_ATT, None, ALU.add).then_inc(pk_ready, 1)
                    v.wait_ge(as_ready, h + 1)
                    v.memset(AP[:], 0.0).then_inc(a_zeroed, 1)
                    with v.Fori(0, ITERS) as i:
                        v.wait_ge(qt_ready, h * QTS + ITERS + i + 1)
                        v.tensor_tensor(SQ[:], QT[:], QT[:], ALU.mult)
                        v.drain()
                        v.tensor_tensor(SQ[:, 0, :], SQ[:, 0, :], SQ[:, 1, :], ALU.add).then_inc(sq_ready, 1)
                        v.wait_ge(ph_exp, h * ITERS + i + 1)
                        v.tensor_scalar(PH[:], PH[:], EPS_ATT, None, ALU.add).then_inc(ph_ready, 1)
                        for b in range(B):
                            v.wait_ge(o_ready, h * T + i * B + b + 1)
                            v.reciprocal(rz[:, b % 3:b % 3 + 1], UP[0:P, b % 3, D:D + 1])
                            v.drain()
                            v.scalar_tensor_tensor(k.ACC[:, i * B + b, :], UP[0:P, b % 3, 0:D], rz[:, b % 3:b % 3 + 1],
                                                   k.ACC[:, i * B + b, :], ALU.mult, ALU.add).then_inc(u_free, 1)


def a_sum(pe, nc, h, i, b, pk_ready, pk_free, AP, PK, XN):
    n = h * T + i * B + b
    pe.wait_ge(pk_ready, n + 1)
    for r in range(2):
        ins = nc.tensor.matmul(AP[:, r, 0:D + 1], PK[:, b % 3, r * 128:r * 128 + 128], XN[:, i * B + b, :],
                               start=False, stop=False, skip_group_check=True)
    ins.then_inc(pk_free, 1)


def layer1_mix(k):
    a = k.a
    with k.scope() as f:
        XN = f.sb("XN", [P, T, D + 1])
        with k.scope() as g:
            XNT = g.sb("XNT", [128, KC, N])
            stage_normalise(k, 1e-5, XNT, XN=XN, tables=(
                (a["L1_gnn_Wq"], k.queries), (a["L1_gnn_Wk"], k.keys), (a["L1_gnn_Wv"], k.sup)))
            stage_linear_attention(k, XN, XNT)
        stage_post(k, None, None, 2, ACT.Relu, a["L1_mix_W1"], a["L1_mix_bias1"], a["L1_mix_W2"], a["L1_mix_bias2"],
                   a["L1_mix_g1"], a["L1_mix_beta1"], a["L1_mix_g2"], a["L1_mix_beta2"], 1e-6, False, XN, a["L1_mix_bo"])
        with k.scope() as g:
            S = g.sb("S", [P, H, TE])
            stage_scores(k, S)
            stage_edge_weights(k, S)
            stage_edge_sums(k, k.sup, GW, S)
        stage_post(k, None, None, 4, ACT.Gelu, a["L1_gnn_ffn_w1"], a["L1_gnn_ffn_b1"], a["L1_gnn_ffn_w2"], a["L1_gnn_ffn_b2"],
                   a["L1_gnn_ln1_g"], a["L1_gnn_ln1_b"], a["L1_gnn_ln2_g"], a["L1_gnn_ln2_b"], 1e-5, True, XN, a["L1_gnn_Wo_b"])
def program(nc, a, out):
    with ExitStack() as stack:
        k = Core(nc, a, stack)
        keep = stack.enter_context(k.scope())
        k.X = keep.sb("X", [P, T, D])
        k.ACC = keep.sb("ACC", [P, T, D])
        k.IDENT = keep.sb("IDENT", [128, 128])
        k.NODE = keep.sb("NODE", [P, T])
        k.MV = keep.sb("MV", [P, T, 2])
        k.RSTD = keep.sb("RSTD", [P, T])
        k.SD = keep.sb("SD", [P, T])
        k.SRC = keep.sb("SRC", [P, TE], I32)
        k.DST = keep.sb("DST", [P, TE], I32)
        k.SAME = keep.sb("SAME", [P, TE])
        k.FROM_LEFT = keep.sb("FROM_LEFT", [P, P])
        k.FROM_RIGHT = keep.sb("FROM_RIGHT", [P, P])
        k.OPEN = keep.sb("OPEN", [P, T])
        k.LAST = keep.sb("LAST", [P, T], I32)
        k.HAS = keep.sb("HAS", [P, T])
        k.RLAST = keep.sb("RLAST", [P, GW])
        k.keys = nc.dram_tensor("keys", [N, D], F32, kind="Internal").ap()
        k.queries = nc.dram_tensor("queries", [N, D], F32, kind="Internal").ap()
        k.weights = nc.dram_tensor("router_weights", [N, 1], F32, kind="Internal").ap()
        k.sup = nc.dram_tensor("support", [N, D], F32, kind="Internal").ap()
        k.run = nc.dram_tensor("running_sums", [E, GW], F32, kind="Internal").ap()
        k.run0 = nc.dram_tensor("running_sums0", [E, D], F32, kind="Internal").ap()
        stage_load(k)
        stage_edges(k)
        with k.scope() as s0:
            s0.W = s0.sb("W", [128, KC, 4 * D])
            s0.WPT = s0.sb("WPT", [128, KC, D])
            s0.bias = s0.sb("bias", [P, 3 * D])
            s0.second = s0.sb("second", [128, H * FC])
            s0.fac = s0.sb("fac", [P, 2 * H])
            s0.qscale = s0.sb("qscale", [P, 2 * H])
            s0.bsum = s0.sb("bsum", [P, 2, D])
            s0.KV = s0.sb("KV", [128, H * FC, V1])
            k.QN = s0.sb("QN", [P, T, D])
            stage_weights0(k, s0)
            stage_layer0_rows(k, s0)
            stage_layer0_attention(k, s0)
            run, k.run = k.run, k.run0
            stage_edge_sums(k, k.sup, D, None)
            k.run = run
            stage_layer0_nodes(k, s0)
        with k.scope() as f:
            XNT = f.sb("XNT", [128, KC, N])
            f.selw = f.sb("selw", [P, T])
            stage_normalise(k, 1e-5, XNT, ranked=f)
            stage_selection(k, f)
            stage_layer0_ffn(k, f, XNT)
        layer1_mix(k)
        with k.scope() as f:
            XNT = f.sb("XNT", [128, KC, N])
            stage_normalise(k, 1e-5, XNT)
            stage_experts(k, XNT, out)


def kernel(**inputs):
    import concourse.bacc as bacc
    from concourse.bass_utils import run_bass_kernel_spmd

    nc = bacc.Bacc("TRN2", target_bir_lowering=False, num_devices=1)
    arrays = {name: np.ascontiguousarray(x) for name, x in inputs.items() if name != "L0_ffn_attention_mask"}
    arrays["L0_mix_temperature"] = arrays["L0_mix_temperature"].reshape(H)
    arrays.update(constants())
    a = {name: nc.dram_tensor(name, x.shape, mybir.dt.from_np(x.dtype), kind="ExternalInput").ap()
         for name, x in arrays.items()}
    out = nc.dram_tensor("out", (N, D), F32, kind="ExternalOutput").ap()
    program(nc, a, out)
    return run_bass_kernel_spmd(nc, [arrays], core_ids=[0]).results[0]["out"]
```

```python
from contextlib import ExitStack

import numpy as np

import concourse.bass as bass
from concourse import mybir

F32 = mybir.dt.float32
I32 = mybir.dt.int32
ALU = mybir.AluOpType
ACT = mybir.ActivationFunctionType
AX = mybir.AxisListType

P = 125
T = 25
N = P * T
TE = 425
E = P * TE
D = 256
KC = D // 128
H = 8
DH = D // H
B = 5
ITERS = T // B
HID = 1024
HC = HID // 128
GW = D + H

NQ = 17 * DH
NF = NQ + DH + 1
FC = 5
FW = FC * 128
V1 = DH + 1


def second_order_weights():
    scale = float(DH) ** 0.25
    w = np.zeros(FW, np.float64)
    w[:NQ] = 0.5 * np.where((np.arange(NQ) // DH > 0) & (np.arange(NQ) // DH < 16), 2.0, 1.0)
    w[NQ:NQ + DH] = scale ** 2
    w[NQ + DH] = scale ** 4
    return np.tile((w / N).reshape(FC, 128).T, (1, H)).astype(np.float32)


def constants():
    p = np.arange(P, dtype=np.float32)
    return {
        "c_ident": np.eye(128, dtype=np.float32),
        "c_node": (p[:, None] * T + np.arange(T, dtype=np.float32)).astype(np.float32),
        "c_column": np.tile(np.arange(T, dtype=np.float32), (P, 1)),
        "c_before": np.triu(np.ones((P, P), np.float32), 1).T.copy(),
        "c_after": np.triu(np.ones((P, P), np.float32), 1),
        "c_base": np.tile(p * T, (P, 1)).astype(np.float32),
        "c_reversed": np.tile(8.0 - np.arange(8, dtype=np.float32), (P, 1)).astype(np.float32),
        "c_second": second_order_weights(),
    }


class Core:

    def __init__(self, nc, a, stack):
        self.nc, self.a, self.stack = nc, a, stack
        self.count = 0

    def scope(self):
        return Scope(self)


class Scope:

    def __init__(self, core):
        self.core, self.nc = core, core.nc

    def __enter__(self):
        self.stack = ExitStack()
        self.stack.__enter__()
        self.sems = []
        return self

    def __exit__(self, *e):
        if self.sems and e[0] is None:
            sems = self.sems
            with self.nc.Block() as block:
                @block.gpsimd
                def _(pool):
                    for sem in sems:
                        pool.sem_clear(sem)
        return self.stack.__exit__(*e)

    def sb(self, name, shape, dt=F32):
        self.core.count += 1
        return self.stack.enter_context(self.nc.sbuf_tensor(f"{name}_{self.core.count}", shape, dt))

    def ps(self, name, shape, dt=F32):
        self.core.count += 1
        return self.stack.enter_context(self.nc.psum_tensor(f"{name}_{self.core.count}", shape, dt))

    def gather_sem(self, name):
        self.core.count += 1
        return self.core.stack.enter_context(self.nc.semaphore(f"{name}_{self.core.count}"))

    def sem(self, name):
        self.core.count += 1
        self.sems.append(self.stack.enter_context(self.nc.semaphore(f"{name}_{self.core.count}")))
        return self.sems[-1]


def node_rows(table):
    return table.rearrange("(p j) d -> p j d", p=P)


def row(vector, n):
    return vector.rearrange("(a d) -> a d", a=1).broadcast_to([n, vector.shape[0]])


def chunks(matrix):
    return matrix.rearrange("(k p) n -> p k n", p=128)


def bcast(ap, n):
    p, h = ap.shape
    return ap.unsqueeze(2).to_broadcast([p, h, n])


def node_stats(k, s, eps, var_ready, sd_ready):
    nc, v = k.nc, k.nc.vector
    with v.Fori(0, ITERS) as i:
        for b in range(B):
            v.bn_stats(s.stat[:, b, :], k.X[:, i * B + b, :])
        v.drain()
        for b in range(B):
            v.bn_aggr(s.mv[:, b, :], s.stat[:, b, :])
        v.drain()
        v.tensor_copy(k.MV[:, bass.ds(i * B, B), :], s.mv[:])
        v.drain()
    v.tensor_scalar(k.RSTD[:], k.MV[:, :, 1], eps, None, ALU.add).then_inc(var_ready, 1)
    v.wait_ge(sd_ready, 1)
    v.reciprocal(k.RSTD[:], k.SD[:])
    v.drain()


def stage_load(k):
    nc, a = k.nc, k.a
    with k.scope() as s:
        loaded = s.sem("loaded")
        with nc.Block() as block:
            @block.sync
            def _(sp):
                sp.dma_start(k.X[:], node_rows(a["x"])).then_inc(loaded, 16)
                sp.dma_start(k.IDENT[:], a["c_ident"]).then_inc(loaded, 16)
                sp.dma_start(k.NODE[:], a["c_node"]).then_inc(loaded, 16)
                sp.wait_ge(loaded, 48)


def stage_edges(k):
    nc, a = k.nc, k.a
    with k.scope() as s:
        dstf = s.sb("dstf", [P, TE])
        firstrow = s.sb("firstrow", [P, P])
        lastrow = s.sb("lastrow", [P, P])
        wide = s.sb("wide", [P, 2, P])
        nexti = s.sb("nexti", [P, 1], I32)
        nextf = s.sb("nextf", [P, 1])
        lc = s.sb("lc", [P, 1])
        before = s.sb("before", [P, P])
        after = s.sb("after", [P, P])
        scratch = s.sb("scratch", [P, TE])
        pc = s.sb("pc", [P, T])
        rowi = s.sb("rowi", [P, T], I32)
        drow = s.sb("drow", [P, B, TE], I32)
        stage_row = s.sb("stage_row", [P, B], I32)
        colc = s.sb("colc", [P, T])
        cnt = s.sb("cnt", [P, T])
        c5 = s.sb("c5", [P, B])
        h5 = s.sb("h5", [P, B])
        rows_ps = s.ps("rows_ps", [P, 2, 512])
        loaded, none, wide_ready, rows_ready = s.sem("loaded"), s.sem("none"), s.sem("wide_ready"), s.sem("rows_ready")
        row_index, staged, gathered, counted = s.sem("row_index"), s.sem("staged"), s.gather_sem("gathered"), s.sem("counted")
        with nc.Block() as block:
            @block.sync
            def _(sp):
                dst2 = a["dst"].rearrange("(p t) -> p t", p=P)
                sp.dma_start(k.SRC[:], a["src"].rearrange("(p t) -> p t", p=P)).then_inc(loaded, 16)
                sp.dma_start(k.DST[:], dst2).then_inc(loaded, 16)
                sp.dma_start(before[:], a["c_before"]).then_inc(loaded, 16)
                sp.dma_start(after[:], a["c_after"]).then_inc(loaded, 16)
                sp.dma_start(colc[:], a["c_column"]).then_inc(loaded, 16)
                sp.wait_ge(none, 1)
                sp.dma_start(nexti[0:P - 1, :], dst2[1:P, 0:1], allow_slow_non_contiguous=True).then_inc(loaded, 16)
                sp.wait_ge(loaded, 96)

            @block.tensor
            def _(pe):
                pe.wait_ge(wide_ready, 1)
                for r in range(2):
                    ins = nc.tensor.matmul(rows_ps[:, r, 0:P], wide[:, r, :], k.IDENT[0:P, 0:P], start=True, stop=True)
                ins.then_inc(rows_ready, 1)

            @block.vector
            def _(v):
                v.memset(nexti[:], -1).then_inc(none, 1)
                v.wait_ge(loaded, 96)
                v.tensor_copy(dstf[:], k.DST[:])
                v.tensor_copy(nextf[:], nexti[:])
                v.drain()
                v.tensor_copy(wide[:, 0, :], dstf[:, 0:1].to_broadcast([P, P]))
                v.tensor_copy(wide[:, 1, :], dstf[:, TE - 1:TE].to_broadcast([P, P])).then_inc(wide_ready, 1)
                v.memset(k.SAME[:, 0:1], 0.0)
                v.tensor_tensor(k.SAME[:, 1:TE], dstf[:, 1:TE], dstf[:, 0:TE - 1], ALU.is_equal)
                v.tensor_tensor(lc[:], dstf[:, TE - 1:TE], nextf[:], ALU.is_equal)
                v.tensor_scalar(cnt[:, 0:1], dstf[:, TE - 1:TE], 1.0, None, ALU.add)
                v.drain()
                v.tensor_tensor(lc[:], lc[:], cnt[:, 0:1], ALU.mult)
                v.drain()
                v.tensor_scalar(lc[:], lc[:], -1.0, None, ALU.add)
                v.drain()
                v.tensor_scalar(k.OPEN[:], colc[:], lc[:, 0:1], -1.0, ALU.subtract, ALU.mult)
                v.wait_ge(rows_ready, 1)
                v.tensor_copy(firstrow[:], rows_ps[:, 0, 0:P])
                v.tensor_copy(lastrow[:], rows_ps[:, 1, 0:P])
                v.drain()
                v.scalar_tensor_tensor(k.FROM_LEFT[:], lastrow[:], dstf[:, 0:1], before[:], ALU.is_equal, ALU.mult)
                v.scalar_tensor_tensor(k.FROM_RIGHT[:], firstrow[:], dstf[:, TE - 1:TE], after[:], ALU.is_equal, ALU.mult)
                for j in range(T):
                    v.tensor_scalar(scratch[:, 0:P], firstrow[:], k.NODE[:, j:j + 1], 0.0, ALU.is_le, ALU.add,
                                    accum_out=pc[:, j:j + 1])
                    v.drain()
                v.tensor_scalar(pc[:], pc[:], -1.0, 0.0, ALU.add, ALU.max)
                v.drain()
                v.tensor_copy(rowi[:], pc[:])
                v.drain()
                with v.Fori(0, ITERS) as i:
                    v.tensor_copy(stage_row[:], rowi[:, bass.ds(i * B, B)]).then_inc(staged, 1)
                    v.wait_ge(gathered, (i + 1) * 16 * B)
                    for b in range(B):
                        v.tensor_scalar(scratch[:], drow[:, b, :], k.NODE[:, bass.ds(i * B + b, 1)], 0.0, ALU.is_le, ALU.add,
                                        accum_out=c5[:, b:b + 1])
                        v.drain()
                        v.tensor_scalar(scratch[:], drow[:, b, :], k.NODE[:, bass.ds(i * B + b, 1)], 0.0, ALU.is_equal, ALU.max,
                                        accum_out=h5[:, b:b + 1])
                        v.drain()
                    v.tensor_copy(cnt[:, bass.ds(i * B, B)], c5[:])
                    v.tensor_copy(k.HAS[:, bass.ds(i * B, B)], h5[:])
                    v.drain()
                v.scalar_tensor_tensor(pc[:], pc[:], float(TE), cnt[:], ALU.mult, ALU.add)
                v.drain()
                v.tensor_scalar(pc[:], pc[:], -1.0, 0.0, ALU.add, ALU.max)
                v.drain()
                v.tensor_copy(k.LAST[:], pc[:])

            @block.gpsimd
            def _(pool):
                table = a["dst"].rearrange("(p t) -> p t", p=P)
                with pool.Fori(0, ITERS) as i:
                    pool.wait_ge(staged, i + 1)
                    pool.sem_inc(counted, 1)
                    for b in range(B):
                        nc.gpsimd.indirect_dma_start(out=drow[:, b, :], out_offset=None, in_=table,
                                                     in_offset=bass.IndirectOffsetOnAxis(ap=stage_row[:, b:b + 1], axis=0)
                                                     ).then_inc(gathered, 16)


def stage_weights0(k, s0, W):
    nc, a = k.nc, k.a
    with k.scope() as s:
        wq = s.sb("wq", [128, 6, D])
        wp = s.sb("wp", [128, 2, D])
        pt = s.ps("pt", [128, 8, 512])
        loaded, turned, taken = s.sem("loaded"), s.sem("turned"), s.sem("taken")
        with nc.Block() as block:
            @block.sync
            def _(sp):
                sp.dma_start(wq[:], chunks(a["L0_mix_Wqkv"])).then_inc(loaded, 16)
                sp.dma_start(wp[:], chunks(a["L0_mix_Wproj"])).then_inc(loaded, 16)
                sp.dma_start(W[:, :, 768:1024], chunks(a["L0_gnn_weight"])).then_inc(loaded, 16)
                sp.dma_start(s0.bias[:], row(a["L0_mix_bqkv"], P)).then_inc(loaded, 16)
                sp.dma_start(s0.second[:], a["c_second"]).then_inc(loaded, 16)
                sp.dma_start(s0.fac[:], row(a["L0_mix_temperature"], P)).then_inc(loaded, 16)
                sp.dma_start(s0.bsum[:, 0, :], row(a["L0_gnn_bias"], P)).then_inc(loaded, 16)
                sp.dma_start(s0.bsum[:, 1, :], row(a["L0_mix_bproj"], P)).then_inc(loaded, 16)
                sp.wait_ge(loaded, 128)

            @block.tensor
            def _(pe):
                pe.wait_ge(loaded, 128)
                for r in range(8):
                    src = wq[:, r, :] if r < 6 else wp[:, r - 6, :]
                    for c in range(KC):
                        ins = nc.tensor.transpose(pt[:, r, c * 128:c * 128 + 128], src[:, c * 128:c * 128 + 128], k.IDENT[:])
                    ins.then_inc(turned, 1)

            @block.vector
            def _(v):
                for r in range(8):
                    v.wait_ge(turned, r + 1)
                    out = W[:, :, r * 128:r * 128 + 128] if r < 6 else s0.WPT[:, :, (r - 6) * 128:(r - 5) * 128]
                    v.tensor_copy(out, pt[:, r, 0:256].rearrange("p (c n) -> p c n", c=KC))
                v.wait_ge(loaded, 128)
                v.tensor_scalar(s0.fac[:], s0.fac[:], float(DH) ** 0.5, None, ALU.mult)


def features(v, U, PHI, phi_ready):
    once = U[:, :, 0:DH].unsqueeze(2).to_broadcast([P, 4, 17, DH])
    shifted = bass.AP(U.tensor, U.offset, [list(U.ap[0]), list(U.ap[1]), [1, 17], [1, DH]])
    v.tensor_copy(PHI[:, :, NQ:NQ + DH], U[:, :, 0:DH])
    v.tensor_tensor(PHI[:, :, 0:NQ].rearrange("p h (o i) -> p h o i", i=DH), once, shifted, ALU.mult)
    v.drain().then_inc(phi_ready, 1)




CW = 17
STEPS = TE // CW
SUBS = ((0, 5), (5, 9), (9, 13), (13, 17))


def gather_rows(nc, pool, wanted, rows, may_fill, go):
    staged, go = go
    with pool.Fori(0, STEPS) as n:
        for s, (lo, hi) in enumerate(SUBS):
            may_fill(n, s)
            for numbers, idx, _, _ in wanted:
                nc.gpsimd.tensor_copy(idx[:, lo:hi], numbers[:, bass.ds(n * CW + lo, hi - lo)]).then_inc(staged, 1)
            pool.wait_ge(staged, (4 * n + s + 1) * len(wanted))
            pool.sem_inc(go, 1)
            for t in range(lo, hi):
                for _, idx, table, out in wanted:
                    nc.gpsimd.indirect_dma_start(out=out[:, t, 0:D], out_offset=None, in_=table,
                                                 in_offset=bass.IndirectOffsetOnAxis(ap=idx[:, t:t + 1], axis=0)
                                                 ).then_inc(rows[s], 16)


class EdgeSums:

    def __init__(self, k, s, table, run, G, idx, weights=None):
        self.k, self.nc, self.table, self.weights = k, k.nc, table, weights
        self.width = D if weights is None else GW
        self.G, self.idx = G, idx
        self.run = run.rearrange("(p t) d -> p t d", p=P)
        self.rows = [s.gather_sem(f"rows{b}") for b in range(len(SUBS))]
        self.out = [s.sem(f"sums_out{b}") for b in range(len(SUBS))]
        self.go = s.sem("staged"), s.sem("go")
        self.summed = s.sem("summed")

    def pool(self, pool):
        def may_fill(n, s):
            pool.wait_ge(self.out[s], 16 * n + 16)
            pool.wait_ge(self.summed, 4 * n + s + 2)
        gather_rows(self.nc, pool, [(self.k.SRC, self.idx, self.table, self.G)], self.rows, may_fill, self.go)

    def sync_begin(self, sp):
        for s in range(len(SUBS)):
            sp.sem_inc(self.out[s], 16)

    def sync_steps(self, sp, n0, count):
        with sp.Fori(0, count) as i:
            n = n0 + i
            for s, (lo, hi) in enumerate(SUBS):
                sp.wait_ge(self.summed, 4 * n + s + 5)
                sp.dma_start(self.run[:, bass.ds(n * CW + lo, hi - lo), :], self.G[:, lo:hi, :]).then_inc(self.out[s], 16)

    def sync_end(self, sp):
        for s in range(len(SUBS)):
            sp.wait_ge(self.out[s], 16 * (STEPS + 1))

    def begin(self, v):
        v.memset(self.G[:, CW - 1, :], 0.0)
        v.drain().then_inc(self.summed, 4)

    def sub(self, v, n, s):
        lo, hi = SUBS[s]
        G, k = self.G, self.k
        v.wait_ge(self.rows[s], (n + 1) * 16 * (hi - lo))
        if self.weights is not None:
            w = self.weights[:, :, bass.ds(n * CW + lo, hi - lo)].rearrange("p h t -> p t h")
            v.tensor_copy(G[:, lo:hi, D:GW], w)
            v.drain()
            g = G[:, lo:hi, 0:D].rearrange("p t (h d) -> p t h d", h=H)
            v.tensor_tensor(g, g, G[:, lo:hi, D:GW].unsqueeze(3).to_broadcast([P, hi - lo, H, DH]), ALU.mult)
            v.drain()
        for t in range(lo, hi):
            v.scalar_tensor_tensor(G[:, t, :], G[:, (t - 1) % CW, :], k.SAME[:, bass.ds(n * CW + t, 1)], G[:, t, :],
                                   ALU.mult, ALU.add)
            last = v.drain()
        last.then_inc(self.summed, 1)

    def end(self, v):
        v.tensor_copy(self.k.RLAST[:, 0:self.width], self.G[:, CW - 1, :])


def stage_layer0_mix(k, s0):
    nc, a = k.nc, k.a
    GROUPS = H * FC // 4
    HH = H // 2
    REST = NF - 512
    with k.scope() as s:
        RAW = s.sb("RAW", [P, B * H, DH])
        nrm = s.sb("nrm", [P, B * H])
        nsd = s.sb("nsd", [P, B * H])
        UW = s.sb("UW", [P, B * H, DH + 16])
        VV = s.sb("VV", [P, B * HH, V1])
        PHI = s.sb("PHI", [P, H, FW])
        PHT = s.sb("PHT", [128, H * FC, P])
        SUMS = PHT[:].rearrange("p q n -> p (q n)")[0:V1, 0:HH * FW]
        YS = s.sb("YS", [V1, H, P])
        YO = s.sb("YO", [P, 2, D])
        YT = s.sb("YT", [128, KC, P])
        rec = s.sb("rec", [P, H])
        G = s.sb("G", [P, CW, D])
        idx = s.sb("idx", [P, CW], I32)
        KVP = s.ps("KVP", [128, HH + 1, 512])
        PT = s.ps("PT", [128, 2, 512])
        PS, PY, PYT, PO = KVP[0:V1, 0:2, 0:4 * P], KVP[0:P, 2, :], KVP[:, 3, :], KVP[0:P, 4, :]
        sem = s.sem
        zeroed, norm_ready, root_ready = sem("zeroed"), sem("norm_ready"), sem("root_ready")
        phi_ready, phi_free, v_free = sem("phi_ready"), sem("phi_free"), sem("v_free")
        sums_ready, sums_kept, kv_turned, kv_ready = sem("sums_ready"), sem("sums_kept"), sem("kv_turned"), sem("kv_ready")
        pt_ready, pt_free, pht_ready, pht_free = sem("pt_ready"), sem("pt_free"), sem("pht_ready"), sem("pht_free")
        ys_summed, ys_ready, ys_free = sem("ys_summed"), sem("ys_ready"), sem("ys_free")
        y_ready, yo_ready = sem("y_ready"), sem("yo_ready")
        yt_turned, yt_ready, out_ready, out_free = sem("yt_turned"), sem("yt_ready"), sem("out_ready"), sem("out_free")
        edges = EdgeSums(k, s, k.sup, k.run0, G, idx)
        with nc.Block() as block:
            @block.gpsimd
            def _(pool):
                edges.pool(pool)

            @block.sync
            def _(sp):
                edges.sync_begin(sp)
                edges.sync_steps(sp, 0, STEPS)
                edges.sync_end(sp)

            @block.vector
            def _(v):
                def five(part, i, h0, nh):
                    lo = part * D + h0 * DH
                    return k.QKV[:, bass.ds(i * B, B), lo:lo + nh * DH]

                def bias(part, h0, nh):
                    lo = part * D + h0 * DH
                    return s0.bias[:, lo:lo + nh * DH]

                def scaled(part, i, h0, nh, item):
                    m = B * nh
                    raw, sq, nr = RAW[:, 0:m, :], UW[:, 0:m, 0:DH], nrm[:, 0:m]
                    v.tensor_tensor(raw.rearrange("p (b h) d -> p b (h d)", b=B), five(part, i, h0, nh),
                                    bias(part, h0, nh).unsqueeze(1).to_broadcast([P, B, nh * DH]), ALU.add)
                    v.drain()
                    v.tensor_tensor(sq, raw, raw, ALU.mult)
                    v.drain()
                    v.tensor_reduce(nr, sq, AX.X, ALU.add).then_inc(norm_ready, 1)
                    v.wait_ge(root_ready, item + 1)
                    v.tensor_scalar(nr, nsd[:, 0:m], float(DH) ** 0.25 if part == 0 else 1.0, 1e-12, ALU.mult, ALU.max)
                    v.drain()
                    v.reciprocal(nr, nr)
                    v.drain()
                    if part == 0:
                        v.tensor_tensor(nr.rearrange("p (b h) -> p b h", b=B), nr.rearrange("p (b h) -> p b h", b=B),
                                        s0.fac[:].unsqueeze(1).to_broadcast([P, B, H]), ALU.mult)
                    else:
                        v.tensor_scalar(nr, nr, float(DH) ** 0.25, None, ALU.mult)
                    v.drain()
                    v.tensor_tensor(sq, raw, bcast(nr, DH), ALU.mult)
                    v.tensor_tensor(UW[:, 0:m, DH:DH + 16], raw[:, :, 0:16], bcast(nr, 16), ALU.mult)
                    v.drain()

                v.memset(KVP[:], 0.0)
                v.memset(PHI[:, :, NQ + DH:FW], 0.0)
                v.memset(VV[:, :, 0:1], 1.0)
                v.drain()
                v.memset(PHI[:, :, NF - 1:NF], 1.0)
                v.drain().then_inc(zeroed, 1)
                edges.begin(v)
                for half in range(2):
                    with v.Fori(0, ITERS) as i:
                        j = half * ITERS + i
                        scaled(1, i, half * HH, HH, j)
                        v.wait_ge(v_free, j + 1)
                        v.tensor_tensor(VV[:, :, 1:V1].rearrange("p (b h) d -> p b h d", b=B),
                                        five(2, i, half * HH, HH).rearrange("p b (h d) -> p b h d", h=HH),
                                        bias(2, half * HH, HH).rearrange("p (h d) -> p h d", h=HH).unsqueeze(1)
                                        .to_broadcast([P, B, HH, DH]), ALU.add)
                        v.drain()
                        for b in range(B):
                            n = j * B + b
                            v.wait_ge(phi_free, n + (2 if b == 0 else 1))
                            features(v, UW[:, b * HH:(b + 1) * HH, :], PHI[:, (b % 2) * HH:(b % 2 + 1) * HH, :], phi_ready)
                            if b < 4:
                                edges.sub(v, j, b)
                    v.wait_ge(sums_ready, half + 1)
                    v.memset(SUMS, 0.0)
                    v.drain()
                    sums = SUMS.rearrange("p (h f) -> p h f", h=HH)
                    v.tensor_copy(sums[:, :, 0:512], KVP[0:V1, 0:HH, :])
                    v.tensor_copy(sums[:, :, 512:NF], KVP[0:V1, HH, 0:HH * REST].rearrange("p (h f) -> p h f", h=HH))
                    v.drain()
                    v.memset(KVP[:], 0.0)
                    v.drain().then_inc(sums_kept, 1)
                    v.wait_ge(kv_turned, half + 1)
                    for q in range(2):
                        lo = (2 * half + q) * 2 * FC
                        v.tensor_tensor(s0.KV[:, lo:lo + 2 * FC, :], PT[:, q, 0:2 * FC * V1].rearrange("p (g e) -> p g e", e=V1),
                                        bcast(s0.second[:, lo:lo + 2 * FC], V1), ALU.mult)
                    v.drain().then_inc(kv_ready, 1)
                v.sem_inc(out_free, 1)

                def divide(i, b):
                    v.wait_ge(y_ready, i * B + b + 1)
                    y = PY[:, 0:H * V1].rearrange("p (h e) -> p h e", e=V1)
                    v.reciprocal(rec[:], y[:, :, 0])
                    v.drain()
                    v.tensor_tensor(YO[:, b % 2, :].rearrange("p (h d) -> p h d", h=H), y[:, :, 1:V1], bcast(rec[:], DH), ALU.mult
                                    ).then_inc(yo_ready, 1)

                def add(i, b):
                    n = i * B + b
                    v.wait_ge(out_ready, n + 1)
                    v.tensor_tensor(k.X[:, n, :], PO[:, 0:D], k.X[:, n, :], ALU.add).then_inc(out_free, 1)

                def query_tiles(i, first):
                    scaled(0, i, 0, H, 2 * ITERS + i)
                    e = 0
                    for b in range(B):
                        for half in range(2):
                            v.wait_ge(phi_free, 2 * (T + i * B + b) + half + 1)
                            features(v, UW[:, b * H + half * HH:b * H + (half + 1) * HH, :],
                                     PHI[:, half * HH:(half + 1) * HH, :], phi_ready)
                            if half and (b or not first):
                                divide(*((i, b - 1) if b else (i - 1, B - 1)))
                            if not half and (b > 1 or not first):
                                add(*((i, b - 2) if b > 1 else (i - 1, B + b - 2)))
                            for _ in range(2 if half and b in (0, 2) else 1):
                                edges.sub(v, 10 + 3 * i + e // 4, e % 4)
                                e += 1

                query_tiles(0, True)
                with v.Fori(1, ITERS) as i:
                    query_tiles(i, False)
                add(ITERS - 1, B - 2)
                divide(ITERS - 1, B - 1)
                add(ITERS - 1, B - 1)
                edges.end(v)

            @block.tensor
            def _(pe):
                pe.sem_inc(v_free, 1)
                pe.sem_inc(phi_free, 2)
                pe.sem_inc(pht_free, 1)
                pe.sem_inc(ys_free, 1)
                pe.wait_ge(zeroed, 1)
                for half in range(2):
                    with pe.Fori(0, ITERS) as i:
                        for b in range(B):
                            pe.wait_ge(phi_ready, (half * ITERS + i) * B + b + 1)
                            for h in range(HH):
                                phi, values = PHI[:, (b % 2) * HH + h, :], VV[:, b * HH + h, :]
                                nc.tensor.matmul(KVP[0:V1, h, :], values, phi[:, 0:512],
                                                 start=False, stop=False, skip_group_check=True)
                                ins = nc.tensor.matmul(KVP[0:V1, HH, h * REST:(h + 1) * REST], values, phi[:, 512:NF],
                                                       start=False, stop=False, skip_group_check=True)
                            ins.then_inc(phi_free, 1)
                        pe.drain().then_inc(v_free, 1)
                    pe.drain().then_inc(sums_ready, 1)
                    pe.wait_ge(sums_kept, half + 1)
                    for q in range(HH * FC):
                        ins = nc.tensor.matmul(PT[:, q // 10, (q % 10) * V1:(q % 10 + 1) * V1], SUMS[:, q * 128:q * 128 + 128],
                                               k.IDENT[0:V1, 0:V1], start=True, stop=True)
                    ins.then_inc(kv_turned, 1)
                    pe.wait_ge(kv_ready, half + 1)

                def products(i, b, g):
                    pe.wait_ge(pht_ready, (i * B + b) * GROUPS + g + 1)
                    if g % 5 == 0:
                        pe.wait_ge(ys_ready, 2 * (i * B + b) + g // 5 + 1)
                    for q in range(4 * g, 4 * g + 4):
                        h, c = q // FC, q % FC
                        ins = nc.tensor.matmul(PS[:, h // 4, (h % 4) * P:(h % 4 + 1) * P], s0.KV[:, q, :], PHT[:, q, :],
                                               start=(c == 0), stop=(c == FC - 1))
                    if g % 5 == 4:
                        ins.then_inc(ys_summed, 1)

                def turn_back(i, b):
                    pe.wait_ge(ys_ready, 2 * (i * B + b) + 4)
                    for h in range(H):
                        ins = nc.tensor.matmul(PY[:, h * V1:(h + 1) * V1], YS[:, h, :], k.IDENT[0:V1, 0:V1], start=True, stop=True)
                    ins.then_inc(y_ready, 1)
                    pe.drain().then_inc(ys_free, 1)

                def turn(i, b):
                    pe.wait_ge(yo_ready, i * B + b + 1)
                    for c in range(KC):
                        ins = nc.tensor.transpose(PYT[:, c * P:c * P + P], YO[:, b % 2, c * 128:c * 128 + 128],
                                                  k.IDENT[0:P, 0:P])
                    ins.then_inc(yt_turned, 1)

                def project(i, b):
                    n = i * B + b
                    pe.wait_ge(yt_ready, n + 1)
                    pe.wait_ge(out_free, n + 1)
                    for c in range(KC):
                        ins = nc.tensor.matmul(PO[:, 0:D], YT[:, c, :], s0.WPT[:, c, :], start=(c == 0), stop=(c == KC - 1))
                    ins.then_inc(out_ready, 1)

                def query_tiles(i, first):
                    for b in range(B):
                        n = i * B + b
                        before = (i, b - 1) if b else (i - 1, B - 1)
                        for g in range(GROUPS):
                            if g % 5 == 0:
                                pe.wait_ge(phi_ready, 2 * (T + n) + g // 5 + 1)
                            pe.wait_ge(pt_free, n * GROUPS + g + 1)
                            for q in range(4):
                                h, c = (4 * g + q) // FC, (4 * g + q) % FC
                                ins = nc.tensor.transpose(PT[:, g % 2, q * P:q * P + P], PHI[:, h, c * 128:c * 128 + 128],
                                                          k.IDENT[0:P, 0:P])
                            ins.then_inc(pt_ready, 1)
                            if g % 5 == 4:
                                pe.drain().then_inc(phi_free, 1)
                            if g:
                                products(i, b, g - 1)
                            if b or not first:
                                if g == 2:
                                    turn_back(*before)
                                if g == 5:
                                    turn(*before)
                                if g == 8:
                                    project(*before)
                        products(i, b, GROUPS - 1)
                        pe.drain().then_inc(pht_free, 1)

                query_tiles(0, True)
                with pe.Fori(1, ITERS) as i:
                    query_tiles(i, False)
                last = (ITERS - 1, B - 1)
                turn_back(*last)
                turn(*last)
                project(*last)

            @block.scalar
            def _(act):
                act.sem_inc(pt_free, 2)
                act.sem_inc(ys_ready, 2)
                with act.Fori(0, 2 * ITERS) as i:
                    act.wait_ge(norm_ready, i + 1)
                    nc.scalar.activation(nsd[:, 0:B * HH], nrm[:, 0:B * HH], ACT.Sqrt).then_inc(root_ready, 1)

                def keep_sums(i, b, half):
                    act.wait_ge(ys_summed, 2 * (i * B + b) + half + 1)
                    if half == 0:
                        act.wait_ge(ys_free, i * B + b + 1)
                    nc.scalar.activation(YS[:, half * 4:half * 4 + 4, :], PS[:, half, :].rearrange("p (h n) -> p h n", h=4),
                                         ACT.Copy).then_inc(ys_ready, 1)

                def keep_y(i, b):
                    act.wait_ge(yt_turned, i * B + b + 1)
                    nc.scalar.activation(YT[:], PYT[:, 0:KC * P].rearrange("p (c n) -> p c n", c=KC), ACT.Copy
                                         ).then_inc(yt_ready, 1)

                def query_tiles(i, first):
                    act.wait_ge(norm_ready, 2 * ITERS + i + 1)
                    nc.scalar.activation(nsd[:], nrm[:], ACT.Sqrt).then_inc(root_ready, 1)
                    for b in range(B):
                        n = i * B + b
                        before = (i, b - 1) if b else (i - 1, B - 1)
                        act.wait_ge(pht_free, n + 1)
                        for g in range(GROUPS):
                            act.wait_ge(pt_ready, n * GROUPS + g + 1)
                            nc.scalar.activation(PHT[:, 4 * g:4 * g + 4, :],
                                                 PT[:, g % 2, 0:4 * P].rearrange("p (q n) -> p q n", n=P), ACT.Copy
                                                 ).then_inc(pht_ready, 1)
                            act.drain().then_inc(pt_free, 1)
                            if g == 0 and (b or not first):
                                keep_sums(*before, 1)
                            if g == 6:
                                keep_sums(i, b, 0)
                            if g == 6 and (b or not first):
                                keep_y(*before)

                query_tiles(0, True)
                with act.Fori(1, ITERS) as i:
                    query_tiles(i, False)
                keep_sums(ITERS - 1, B - 1, 1)
                keep_y(ITERS - 1, B - 1)


def open_nodes(v, k, out, base, n):
    return v.tensor_scalar(out, base, k.OPEN[:, bass.ds(n, 1)], None, ALU.is_equal)


def stage_layer0_nodes(k, s0):
    nc, a = k.nc, k.a
    with k.scope() as s:
        base = s.sb("base", [P, P])
        idx = s.sb("idx", [P, B], I32)
        G = s.sb("G", [P, B, D])
        GM = s.sb("GM", [P, B, P])
        bias = s.sb("bias", [P, D])
        PS = s.ps("PS", [P, B, 512])
        sem = s.sem
        loaded, staged, go, open_ready, sums_ready = (sem(x) for x in (
            "loaded", "staged", "go", "open_ready", "sums_ready"))
        rows = s.gather_sem("rows")
        with nc.Block() as block:
            @block.sync
            def _(sp):
                sp.dma_start(base[:], a["c_base"]).then_inc(loaded, 16)
                sp.wait_ge(loaded, 16)

            @block.gpsimd
            def _(pool):
                with pool.Fori(0, ITERS) as i:
                    pool.wait_ge(staged, i + 1)
                    pool.sem_inc(go, 1)
                    for b in range(B):
                        nc.gpsimd.indirect_dma_start(out=G[:, b, :], out_offset=None, in_=k.run0,
                                                     in_offset=bass.IndirectOffsetOnAxis(ap=idx[:, b:b + 1], axis=0)
                                                     ).then_inc(rows, 16)

            @block.tensor
            def _(pe):
                with pe.Fori(0, ITERS) as i:
                    for b in range(B):
                        pe.wait_ge(open_ready, i * B + b + 1)
                        nc.tensor.matmul(PS[:, b, 0:D], GM[:, b, :], k.RLAST[:, 0:D], start=True, stop=True
                                         ).then_inc(sums_ready, 1)

            @block.vector
            def _(v):
                v.wait_ge(loaded, 16)
                v.tensor_tensor(bias[:], s0.bsum[:, 0, :], s0.bsum[:, 1, :], ALU.add)
                with v.Fori(0, ITERS) as i:
                    v.drain()
                    v.tensor_copy(idx[:], k.LAST[:, bass.ds(i * B, B)]).then_inc(staged, 1)
                    for b in range(B):
                        open_nodes(v, k, GM[:, b, :], base[:], i * B + b).then_inc(open_ready, 1)
                    v.wait_ge(rows, (i + 1) * 16 * B)
                    for b in range(B):
                        n = i * B + b
                        v.wait_ge(sums_ready, n + 1)
                        v.tensor_tensor(G[:, b, :], G[:, b, :], PS[:, b, 0:D], ALU.add)
                        v.tensor_tensor(k.X[:, n, :], k.X[:, n, :], bias[:], ALU.add)
                        v.drain()
                        v.scalar_tensor_tensor(k.X[:, n, :], G[:, b, :], k.HAS[:, bass.ds(n, 1)], k.X[:, n, :],
                                               ALU.mult, ALU.add)




def stage_normalise(k, eps, XNT=None, ranked=None, XN=None, tables=None, W=None, KEPT=None):
    nc, a = k.nc, k.a
    with k.scope() as s:
        s.stat = s.sb("stat", [P, B, 6])
        s.mv = s.sb("mv", [P, B, 2])
        XS = s.sb("XS", [P, B, D])
        XT = s.sb("XT", [128, B, KC, P])
        PT = s.ps("PT", [128, 3, 512])
        nt = len(tables or ())
        if tables:
            kept = D * sum(table is None for _, table in tables)
            stored_tables = [table for _, table in tables if table is not None]
            ns = len(stored_tables)
            load_w = W is None
            W = s.sb("W", [128, KC, nt * D]) if load_w else W
            OUT = s.sb("OUT", [P, B, ns * D])
            PR = s.ps("PR", [P, 2, 512])
        if ranked:
            wr = s.sb("wr", [P, D])
            br = s.sb("br", [P, 1])
            prod = s.sb("prod", [P, D])
            w5 = s.sb("w5", [P, B])

        def pt(b):
            return PT[:, b % 3, 0:KC * P].rearrange("p (c n) -> p c n", c=KC)

        sem = s.sem
        loaded, var_ready, sd_ready = sem("loaded"), sem("var_ready"), sem("sd_ready")
        rows_ready, rows_free, rows_kept = sem("rows_ready"), sem("rows_free"), sem("rows_kept")
        turned_ready, turned_free = sem("turned_ready"), sem("turned_free")
        xt_ready, xt_free, xt_kept = sem("xt_ready"), sem("xt_free"), sem("xt_kept")
        proj_ready, pr_free = sem("proj_ready"), [sem("pr_free0"), sem("pr_free1")]
        out_ready, stored = sem("out_ready"), [sem(f"stored{b}") for b in range(B)]
        weights_ready = sem("weights_ready")
        nload = 16 * ((nt if tables and load_w else 0) + (2 if ranked else 0))
        with nc.Block() as block:
            @block.sync
            def _(sp):
                for m, (w, _) in enumerate(tables if tables and load_w else ()):
                    sp.dma_start(W[:, :, m * D:(m + 1) * D], chunks(w)).then_inc(loaded, 16)
                if ranked:
                    sp.dma_start(wr[:], row(a["L0_ffn_wr"].rearrange("d o -> (d o)"), P)).then_inc(loaded, 16)
                    sp.dma_start(br[:], row(a["L0_ffn_br"], P)).then_inc(loaded, 16)
                if tables:
                    for b in range(B):
                        sp.sem_inc(stored[b], 16)
                    with sp.Fori(0, ITERS) as i:
                        for b in range(B):
                            n = i * B + b
                            sp.wait_ge(out_ready, n + 1)
                            for m, table in enumerate(stored_tables):
                                sp.dma_start(node_rows(table)[:, n, :], OUT[:, b, m * D:(m + 1) * D]).then_inc(stored[b], 16)
                    for b in range(B):
                        sp.wait_ge(stored[b], 16 * (ns * ITERS + 1))
                if ranked:
                    sp.wait_ge(weights_ready, 1)
                    sp.dma_start(k.weights.rearrange("(p t) d -> p (t d)", p=P), ranked.selw[:]).then_inc(loaded, 16)
                    sp.wait_ge(loaded, nload + 16)

            @block.vector
            def _(v):
                node_stats(k, s, eps, var_ready, sd_ready)
                if ranked:
                    v.wait_ge(loaded, nload)
                with v.Fori(0, ITERS) as i:
                    for b in range(B):
                        n = i * B + b
                        v.wait_ge(rows_free, n + 1)
                        v.wait_ge(rows_kept, n + 1)
                        v.tensor_scalar(XS[:, b, :], k.X[:, n, :], k.MV[:, n, 0:1], k.RSTD[:, bass.ds(n, 1)],
                                        ALU.subtract, ALU.mult).then_inc(rows_ready, 1)
                        if ranked:
                            v.drain()
                            v.tensor_tensor_reduce(prod[:], XS[:, b, :], wr[:], 1.0, 0.0, ALU.mult, ALU.add,
                                                   w5[:, b:b + 1])
                    if ranked:
                        v.drain()
                        v.tensor_scalar(ranked.selw[:, bass.ds(i * B, B)], w5[:], br[:, 0:1], None, ALU.add)
                        v.drain()
                if ranked:
                    v.drain().then_inc(weights_ready, 1)

            @block.tensor
            def _(pe):
                pe.sem_inc(rows_free, B)
                pe.sem_inc(xt_free, B)
                if nload:
                    pe.wait_ge(loaded, nload)
                with pe.Fori(0, ITERS) as i:
                    for b in range(B):
                        n = i * B + b
                        pe.wait_ge(rows_ready, n + 1)
                        pe.wait_ge(turned_free, n + 1)
                        for c in range(KC):
                            ins = nc.tensor.transpose(pt(b)[:, c, :], XS[:, b, c * 128:c * 128 + 128], k.IDENT[0:P, 0:P])
                        ins.then_inc(turned_ready, 1)
                    for b in range(B if tables else 0):
                        n = i * B + b
                        pe.wait_ge(xt_ready, n + 1)
                        for half in range(2):
                            lo, hi = half * 512, min(half * 512 + 512, nt * D)
                            pe.wait_ge(pr_free[half], n + 1)
                            for c in range(KC):
                                ins = nc.tensor.matmul(PR[:, half, 0:hi - lo], XT[:, b, c, :], W[:, c, lo:hi],
                                                       start=(c == 0), stop=(c == KC - 1))
                            ins.then_inc(proj_ready, 1)
                        pe.drain().then_inc(xt_free, 1)

            @block.scalar
            def _(act):
                act.sem_inc(turned_free, 2)
                if tables:
                    act.sem_inc(pr_free[0], 1)
                    act.sem_inc(pr_free[1], 1)
                act.wait_ge(var_ready, 1)
                nc.scalar.activation(k.SD[:], k.RSTD[:], ACT.Sqrt).then_inc(sd_ready, 1)
                with act.Fori(0, ITERS) as i:
                    for b in range(B):
                        n = i * B + b
                        act.wait_ge(turned_ready, n + 1)
                        if tables:
                            act.wait_ge(xt_free, n + 1)
                            nc.scalar.activation(XT[:, b, :, :], pt(b), ACT.Copy).then_inc(xt_ready, 1)
                        if XNT is not None:
                            nc.scalar.activation(XNT[:, :, bass.ds(n * P, P)], pt(b), ACT.Copy)
                        act.sem_inc(rows_free, 1)
                        act.drain().then_inc(turned_free, 1)
                    for b in range(B if tables else 0):
                        n = i * B + b
                        act.wait_ge(stored[b], 16 * (ns * i + 1))
                        for half in range(2):
                            lo, hi = half * 512, min(half * 512 + 512, nt * D)
                            act.wait_ge(proj_ready, 2 * n + half + 1)
                            if lo < kept:
                                m = min(hi, kept)
                                ins = nc.scalar.activation(KEPT[:, n, lo:m], PR[:, half, 0:m - lo], ACT.Copy)
                            if hi > kept:
                                m = max(lo, kept)
                                ins = nc.scalar.activation(OUT[:, b, m - kept:hi - kept], PR[:, half, m - lo:hi - lo], ACT.Copy)
                            ins.then_inc(pr_free[half], 1)
                        act.drain().then_inc(out_ready, 1)

            @block.gpsimd
            def _(pool):
                pool.sem_inc(rows_kept, B)
                if XN is not None:
                    nc.gpsimd.memset(XN[:, :, D:D + 1], 1.0)
                if XN is not None or ranked:
                    with pool.Fori(0, ITERS) as i:
                        for b in range(B):
                            n = i * B + b
                            pool.wait_ge(rows_ready, n + 1)
                            if ranked:
                                nc.gpsimd.tensor_tensor(k.X[:, n, :], k.X[:, n, :], XS[:, b, :], ALU.add).then_inc(rows_kept, 1)
                            else:
                                nc.gpsimd.tensor_copy(XN[:, n, 0:D], XS[:, b, :]).then_inc(rows_kept, 1)
                else:
                    pool.sem_inc(rows_kept, T)


KEEP = int(0.5 * N) - 1


class Selection:

    def __init__(self, k, f, s, PS):
        self.k, self.f, self.PS = k, f, PS
        self.wrow = s.sb("wrow", [P, N])
        self.scratch = s.sb("scratch", [P, N])
        self.gt, self.ge, self.tie, self.ones, self.upto = (s.sb(x, [P, T]) for x in ("gt", "ge", "tie", "ones", "upto"))
        self.after = s.sb("after", [P, P])
        self.loaded, self.ties_ready, self.before_ready = s.sem("ranks_loaded"), s.sem("ties_ready"), s.sem("before_ready")

    def sync(self, sp):
        sp.dma_start(self.wrow[:], row(self.k.weights.rearrange("n d -> (n d)"), P)).then_inc(self.loaded, 16)
        sp.dma_start(self.after[:], self.k.a["c_after"]).then_inc(self.loaded, 16)

    def vector(self, v):
        gt, ge, tie, upto, selw = self.gt, self.ge, self.tie, self.upto, self.f.selw
        v.memset(self.ones[:], 1.0)
        v.wait_ge(self.loaded, 32)
        for out, op in ((gt, ALU.is_gt), (ge, ALU.is_ge)):
            for n in range(T):
                v.drain()
                v.tensor_scalar(self.scratch[:], self.wrow[:], selw[:, n:n + 1], 0.0, op, ALU.add,
                                accum_out=out[:, n:n + 1])
        v.drain()
        v.tensor_scalar(tie[:], gt[:], float(KEEP), None, ALU.is_lt)
        v.drain()
        v.scalar_tensor_tensor(tie[:], ge[:], float(KEEP), tie[:], ALU.is_gt, ALU.mult)
        v.drain()
        v.tensor_tensor_scan(upto[:], self.ones[:], tie[:], 0.0, ALU.mult, ALU.add).then_inc(self.ties_ready, 1)
        v.wait_ge(self.before_ready, 1)
        v.tensor_tensor(upto[:], upto[:], tie[:], ALU.subtract)
        v.drain()
        v.tensor_scalar(upto[:], upto[:], self.PS[:, 0:1], None, ALU.add)
        v.drain()
        v.tensor_tensor(upto[:], upto[:], tie[:], ALU.mult)
        v.drain()
        v.tensor_tensor(gt[:], gt[:], upto[:], ALU.add)
        v.drain()
        v.scalar_tensor_tensor(selw[:], gt[:], float(KEEP), selw[:], ALU.is_lt, ALU.mult)
        v.drain()

    def tensor(self, pe):
        pe.wait_ge(self.ties_ready, 1)
        self.k.nc.tensor.matmul(self.PS[:, 0:1], self.after[:], self.upto[:, T - 1:T], start=True, stop=True
                                ).then_inc(self.before_ready, 1)


PIECES = ((0, 3 * P), (3 * P, B * P))


def stage_layer0_ffn(k, f, XNT):
    nc, a = k.nc, k.a
    with k.scope() as s:
        W1 = s.sb("W1", [128, KC, HID])
        W2 = s.sb("W2", [128, HC, D])
        b1 = s.sb("b1", [128, HC])
        b2 = s.sb("b2", [P, D])
        HT = s.sb("HT", [128, HC, B * P])
        Y = s.sb("Y", [P, T, D])
        HP = s.ps("HP", [128, 4, 512])
        YP = s.ps("YP", [P, 3, 512])
        PS = s.ps("PS", [P, 512])
        selection = Selection(k, f, s, PS)
        sem = s.sem
        loaded, h_ready, h_free, ht_ready, ht_free, y_ready, y_free, y_kept = (sem(x) for x in (
            "loaded", "h_ready", "h_free", "ht_ready", "ht_free", "y_ready", "y_free", "y_kept"))
        with nc.Block() as block:
            @block.sync
            def _(sp):
                selection.sync(sp)
                sp.dma_start(W1[:], chunks(a["L0_ffn_w1"])).then_inc(loaded, 16)
                sp.dma_start(W2[:], chunks(a["L0_ffn_w2"])).then_inc(loaded, 16)
                sp.dma_start(b1[:], a["L0_ffn_b1"].rearrange("(c p) -> p c", p=128), allow_slow_non_contiguous=True).then_inc(loaded, 16)
                sp.dma_start(b2[:], row(a["L0_ffn_b2"], P)).then_inc(loaded, 16)
                sp.wait_ge(loaded, 64)

            @block.tensor
            def _(pe):
                pe.sem_inc(ht_free, 1)
                pe.wait_ge(loaded, 64)
                with pe.Fori(0, ITERS) as i:
                    for c in range(HC):
                        for q, (lo, hi) in enumerate(PIECES):
                            m = 2 * c + q
                            pe.wait_ge(h_free, i * 2 * HC + m + 1)
                            for kc in range(KC):
                                ins = nc.tensor.matmul(HP[:, m % 4, 0:hi - lo], W1[:, kc, c * 128:c * 128 + 128],
                                                       XNT[:, kc, bass.ds(i * B * P + lo, hi - lo)],
                                                       start=(kc == 0), stop=(kc == KC - 1))
                            ins.then_inc(h_ready, 1)
                    pe.wait_ge(ht_ready, (i + 1) * 2 * HC)
                    for b in range(B):
                        pe.wait_ge(y_free, i * B + b + 1)
                        for c in range(HC):
                            ins = nc.tensor.matmul(YP[:, b % 3, 0:D], HT[:, c, b * P:b * P + P], W2[:, c, :],
                                                   start=(c == 0), stop=(c == HC - 1))
                        ins.then_inc(y_ready, 1)
                    pe.drain().then_inc(ht_free, 1)
                selection.tensor(pe)

            @block.scalar
            def _(act):
                act.sem_inc(h_free, 4)
                act.sem_inc(y_free, 2)
                act.wait_ge(loaded, 64)
                with act.Fori(0, ITERS) as i:
                    act.wait_ge(ht_free, i + 1)
                    for c in range(HC):
                        for q, (lo, hi) in enumerate(PIECES):
                            m = 2 * c + q
                            act.wait_ge(h_ready, i * 2 * HC + m + 1)
                            nc.scalar.activation(HT[:, c, lo:hi], HP[:, m % 4, 0:hi - lo], ACT.Gelu_apprx_tanh,
                                                 bias=b1[:, c:c + 1]).then_inc(h_free, 1)
                    act.drain().then_inc(ht_ready, 2 * HC)
                    for b in range(B):
                        act.wait_ge(y_ready, i * B + b + 1)
                        nc.scalar.activation(Y[:, i * B + b, :], YP[:, b % 3, 0:D], ACT.Copy).then_inc(y_free, 1)
                act.drain().then_inc(y_kept, 1)

            @block.vector
            def _(v):
                selection.vector(v)
                v.wait_ge(loaded, 64)
                v.wait_ge(y_kept, 1)
                with v.Fori(0, ITERS) as i:
                    rows = Y[:, bass.ds(i * B, B), :]
                    v.tensor_tensor(rows, rows, b2[:].unsqueeze(1).to_broadcast([P, B, D]), ALU.add)
                    v.drain()
                    for b in range(B):
                        n = i * B + b
                        v.scalar_tensor_tensor(k.X[:, n, :], Y[:, n, :], f.selw[:, bass.ds(n, 1)], k.X[:, n, :],
                                               ALU.mult, ALU.add)


def stage_experts(k, XNT, out):
    nc, a = k.nc, k.a
    NE = 8
    with k.scope() as s:
        W1 = s.sb("W1", [128, KC, HID])
        WG = s.sb("WG", [128, HC, NE])
        WD = s.sb("WD", [128, HC, NE, D])
        BD = s.sb("BD", [B * NE, B, D])
        b1 = s.sb("b1", [128, HC])
        bg = s.sb("bg", [P, NE])
        rev = s.sb("rev", [P, NE])
        HT = s.sb("HT", [128, HC, B * P])
        lg = s.sb("lg", [P, B, NE])
        key = s.sb("key", [P, B, NE])
        one = s.sb("one", [P, B])
        coef = s.sb("coef", [P, 16, NE])
        CT = s.sb("CT", [B * NE, P])
        HP = s.ps("HP", [128, 2, 512])
        YP = s.ps("YP", [P, 4, 512])
        LG = s.ps("LG", [P, 512])
        CB = s.ps("CB", [128, 512])
        sem = s.sem
        (loaded, zeroed, h_ready, h_free, ht_ready, ht_free, lg_ready, lg_free, coef_ready, ct_ready, ct_kept, bd_ready,
         bd_free, y_ready, y_free, x_ready, shifted, exp_ready, stored) = (sem(x) for x in (
             "loaded", "zeroed", "h_ready", "h_free", "ht_ready", "ht_free", "lg_ready", "lg_free", "coef_ready", "ct_ready",
             "ct_kept", "bd_ready", "bd_free", "y_ready", "y_free", "x_ready", "shifted", "exp_ready", "stored"))
        NL = 16 * (5 + NE + B)
        with nc.Block() as block:
            @block.sync
            def _(sp):
                sp.dma_start(W1[:], chunks(a["L1_ffn_W1"])).then_inc(loaded, 16)
                sp.dma_start(b1[:], a["L1_ffn_b1"].rearrange("(c p) -> p c", p=128), allow_slow_non_contiguous=True).then_inc(loaded, 16)
                sp.dma_start(WG[:], chunks(a["L1_ffn_Wg"])).then_inc(loaded, 16)
                sp.dma_start(bg[:], row(a["L1_ffn_bg"], P)).then_inc(loaded, 16)
                sp.dma_start(rev[:], a["c_reversed"]).then_inc(loaded, 16)
                for e in range(NE):
                    sp.dma_start(WD[:, :, e, :], chunks(a["L1_ffn_Wd"][e])).then_inc(loaded, 16)
                sp.wait_ge(zeroed, 1)
                for b in range(B):
                    sp.dma_start(BD[b * NE:(b + 1) * NE, b, :], a["L1_ffn_bd"]).then_inc(loaded, 16)
                sp.wait_ge(loaded, NL)
                with sp.Fori(0, T) as n:
                    sp.wait_ge(x_ready, n + 1)
                    sp.dma_start(node_rows(out)[:, n, :], k.X[:, n, :]).then_inc(stored, 16)
                sp.wait_ge(stored, 16 * T)

            @block.tensor
            def _(pe):
                pe.sem_inc(ht_free, 1)
                pe.wait_ge(loaded, NL)
                with pe.Fori(0, ITERS) as i:
                    for c in range(HC):
                        for q, (lo, hi) in enumerate(PIECES):
                            pe.wait_ge(h_free, i * 2 * HC + 2 * c + q + 1)
                            for kc in range(KC):
                                ins = nc.tensor.matmul(HP[:, q, 0:hi - lo], W1[:, kc, c * 128:c * 128 + 128],
                                                       XNT[:, kc, bass.ds(i * B * P + lo, hi - lo)],
                                                       start=(kc == 0), stop=(kc == KC - 1))
                            ins.then_inc(h_ready, 1)
                    pe.wait_ge(ht_ready, i + 1)
                    pe.wait_ge(lg_free, i + 1)
                    for b in range(B):
                        for c in range(HC):
                            ins = nc.tensor.matmul(LG[:, b * NE:(b + 1) * NE], HT[:, c, b * P:b * P + P], WG[:, c, :],
                                                   start=(c == 0), stop=(c == HC - 1))
                    ins.then_inc(lg_ready, 1)
                    for b in range(B):
                        for q in range(NE // 2):
                            pe.wait_ge(y_free, (i * B + b) * 4 + q + 1)
                            for c in range(HC):
                                ins = nc.tensor.matmul(YP[:, q, :], HT[:, c, b * P:b * P + P],
                                                       WD[:, c, 2 * q:2 * q + 2, :], start=(c == 0), stop=(c == HC - 1))
                            ins.then_inc(y_ready, 1)
                        if b == 0:
                            pe.wait_ge(coef_ready, i + 1)
                            pe.wait_ge(bd_free, i * B + 1)
                            nc.tensor.transpose(CB[:, D:D + P], coef[:].rearrange("p b e -> p (b e)"),
                                                k.IDENT[0:P, 0:P]).then_inc(ct_ready, 1)
                            pe.wait_ge(ct_kept, i + 1)
                        pe.wait_ge(bd_free, i * B + b + 1)
                        nc.tensor.matmul(CB[0:P, 0:D], CT[:], BD[:, b, :], start=True, stop=True).then_inc(bd_ready, 1)
                    pe.drain().then_inc(ht_free, 1)

            @block.scalar
            def _(act):
                act.sem_inc(h_free, 2)
                act.wait_ge(loaded, NL)
                with act.Fori(0, ITERS) as i:
                    act.wait_ge(ht_free, i + 1)
                    for c in range(HC):
                        for q, (lo, hi) in enumerate(PIECES):
                            act.wait_ge(h_ready, i * 2 * HC + 2 * c + q + 1)
                            nc.scalar.activation(HT[:, c, lo:hi], HP[:, q, 0:hi - lo], ACT.Gelu,
                                                 bias=b1[:, c:c + 1]).then_inc(h_free, 1)
                    act.drain().then_inc(ht_ready, 1)
                    act.wait_ge(shifted, i + 1)
                    nc.scalar.activation(lg[:], lg[:], ACT.Exp).then_inc(exp_ready, 1)
                    act.wait_ge(ct_ready, i + 1)
                    nc.scalar.activation(CT[:], CB[0:B * NE, D:D + P], ACT.Copy).then_inc(ct_kept, 1)

            @block.vector
            def _(v):
                v.memset(coef[:], 0.0)
                v.memset(BD[:], 0.0).then_inc(zeroed, 1)
                v.sem_inc(lg_free, 1)
                v.sem_inc(bd_free, 1)
                v.sem_inc(y_free, 4)
                v.wait_ge(loaded, NL)
                with v.Fori(0, ITERS) as i:
                    v.wait_ge(lg_ready, i + 1)
                    v.tensor_tensor(lg[:], LG[:, 0:B * NE].rearrange("p (b e) -> p b e", b=B),
                                    bg[:].unsqueeze(1).to_broadcast([P, B, NE]), ALU.add)
                    v.drain().then_inc(lg_free, 1)
                    v.tensor_reduce(one[:], lg[:], AX.X, ALU.max)
                    v.drain()
                    v.tensor_tensor(lg[:], lg[:], bcast(one[:], NE), ALU.subtract).then_inc(shifted, 1)
                    v.wait_ge(exp_ready, i + 1)
                    v.tensor_reduce(one[:], lg[:], AX.X, ALU.add)
                    v.drain()
                    v.reciprocal(one[:], one[:])
                    v.drain()
                    v.tensor_tensor(lg[:], lg[:], bcast(one[:], NE), ALU.mult)
                    v.drain()
                    v.tensor_reduce(one[:], lg[:], AX.X, ALU.max)
                    v.drain()
                    v.tensor_tensor(key[:], lg[:], bcast(one[:], NE), ALU.is_equal)
                    v.drain()
                    v.tensor_tensor(key[:], key[:], rev[:].unsqueeze(1).to_broadcast([P, B, NE]), ALU.mult)
                    v.drain()
                    v.tensor_reduce(one[:], key[:], AX.X, ALU.max)
                    v.drain()
                    v.tensor_tensor(key[:], key[:], bcast(one[:], NE), ALU.is_equal)
                    v.drain()
                    v.tensor_tensor(coef[:, 0:B, :], key[:], lg[:], ALU.mult).then_inc(coef_ready, 1)
                    v.drain()
                    for b in range(B):
                        n = i * B + b
                        for q in range(NE // 2):
                            v.wait_ge(y_ready, n * 4 + q + 1)
                            for e in range(2):
                                v.scalar_tensor_tensor(k.X[:, n, :], YP[:, q, e * D:(e + 1) * D],
                                                       coef[:, b, 2 * q + e:2 * q + e + 1], k.X[:, n, :], ALU.mult, ALU.add)
                                last = v.drain()
                            last.then_inc(y_free, 1)
                        v.wait_ge(bd_ready, n + 1)
                        v.tensor_tensor(k.X[:, n, :], k.X[:, n, :], CB[0:P, 0:D], ALU.add).then_inc(x_ready, 1)
                        v.drain().then_inc(bd_free, 1)


SCALE1 = DH ** -0.5
KD = 256
QSCALE = KD ** -0.25
EPS_ATT = 1e-6
LN_SQRT_M = float(0.5 * np.log(256.0))


class EdgeScores:

    def __init__(self, k, s, S, GK, GQ, ki, qi):
        self.k, self.nc, self.S, self.GK, self.GQ, self.ki, self.qi = k, k.nc, S, GK, GQ, ki, qi
        self.rows = [s.gather_sem(f"rows{b}") for b in range(len(SUBS))]
        self.go = s.sem("staged"), s.sem("go")
        self.used = s.sem("used")

    def pool(self, pool):
        def may_fill(n, b):
            pool.wait_ge(self.used, 4 * n + b + 1)
        gather_rows(self.nc, pool, [(self.k.SRC, self.ki, self.k.keys, self.GK), (self.k.DST, self.qi, self.k.queries, self.GQ)],
                    self.rows, may_fill, self.go)

    def begin(self, v):
        v.sem_inc(self.used, 4)

    def sub(self, v, n, b):
        lo, hi = SUBS[b]
        v.wait_ge(self.rows[b], (n + 1) * 32 * (hi - lo))
        v.tensor_tensor(self.GK[:, lo:hi, :], self.GK[:, lo:hi, :], self.GQ[:, lo:hi, :], ALU.mult)
        v.drain()
        v.tensor_reduce(self.S[:, :, bass.ds(n * CW + lo, hi - lo)].rearrange("p h t -> p t h"),
                        self.GK[:, lo:hi, :].rearrange("p t (h d) -> p t h d", h=H), AX.X, ALU.add).then_inc(self.used, 1)


def stage_edge_weights(k, S):
    nc, a = k.nc, k.a
    with k.scope() as s:
        F = s.sb("F", [P, H, TE])
        R = s.sb("R", [P, H, TE])
        forward = s.sb("forward", [P, TE])
        backward = s.sb("backward", [P, TE])
        ends = s.sb("ends", [P, H, P])
        masked = s.sb("masked", [P, H, P])
        ones = s.sb("ones", [P, P])
        carry = s.sb("carry", [P, 2, H])
        PS = s.ps("PS", [P, 2, 512])
        scaled, less, ends_ready, spread = s.sem("scaled"), s.sem("less"), s.sem("ends_ready"), s.sem("spread")
        with nc.Block() as block:
            @block.scalar
            def _(act):
                nc.scalar.activation(S[:], S[:], ACT.Copy, scale=SCALE1).then_inc(scaled, 1)
                act.wait_ge(less, 1)
                nc.scalar.activation(S[:], S[:], ACT.Exp)

            @block.tensor
            def _(pe):
                for r in range(2):
                    pe.wait_ge(ends_ready, r + 1)
                    for q in range(2):
                        ins = nc.tensor.matmul(PS[:, q, 0:4 * P], ones[:], ends[:, 4 * q:4 * q + 4, :], start=True, stop=True)
                    ins.then_inc(spread, 1)

            @block.vector
            def _(v):
                v.memset(ones[:], 1.0)
                v.tensor_copy(forward[:, 1:TE], k.SAME[:, 1:TE])
                v.memset(forward[:, 0:1], 1.0)
                v.tensor_copy(backward[:, 0:TE - 1], k.SAME[:, 1:TE])
                v.memset(backward[:, TE - 1:TE], 1.0)
                v.drain()
                v.wait_ge(scaled, 1)

                def scans(first):
                    for h in range(H):
                        start = (0.0, 0.0) if first else (carry[:, 0, h:h + 1], carry[:, 1, h:h + 1])
                        v.tensor_tensor_scan(F[:, h, :], forward[:], S[:, h, :], start[0], ALU.mult, ALU.max)
                        v.tensor_tensor_scan(R[:, h, ::-1], backward[:, ::-1], S[:, h, ::-1], start[1], ALU.mult, ALU.max)
                    v.drain()
                scans(True)
                for r, (edge, mask) in enumerate(((F[:, :, TE - 1], k.FROM_LEFT), (R[:, :, 0], k.FROM_RIGHT))):
                    v.tensor_tensor(ends[:], k.IDENT[0:P, 0:P].unsqueeze(1).to_broadcast([P, H, P]),
                                    bcast(edge, P), ALU.mult).then_inc(ends_ready, 1)
                    v.wait_ge(spread, r + 1)
                    for q in range(2):
                        v.tensor_tensor(masked[:, 4 * q:4 * q + 4, :], PS[:, q, 0:4 * P].rearrange("p (h n) -> p h n", h=4),
                                        mask[:].unsqueeze(1).to_broadcast([P, 4, P]), ALU.mult)
                    v.drain()
                    v.tensor_reduce(carry[:, r, :], masked[:], AX.X, ALU.max)
                    v.drain()
                scans(False)
                v.tensor_tensor(F[:], F[:], R[:], ALU.max)
                v.drain()
                v.tensor_tensor(S[:], S[:], F[:], ALU.subtract).then_inc(less, 1)


def stage_post(k, ones, fetch_blocks, nh, act_func, w1, bb1, w2, bb2, g1, be1, g2, be2, eps, graph, XN, add0):
    nc, a = k.nc, k.a
    with k.scope() as s:
        W1 = s.sb("W1", [128, KC, nh * 128])
        W2 = s.sb("W2", [128, nh, D])
        b1 = s.sb("b1", [128, nh])
        vec = s.sb("vec", [P, 6, D])
        R = s.sb("R", [P, B, D])
        RT = s.sb("RT", [128, KC, B, P])
        HT = s.sb("HT", [128, nh, B * P])
        stat = s.sb("stat", [P, B, 6])
        mv = s.sb("mv", [P, B, 2])
        var = s.sb("var", [P, B])
        sd = s.sb("sd", [P, B])
        PT = s.ps("PT", [128, 3, 512])
        PY = s.ps("PY", [P, 3, 512])
        HP = s.ps("HP", [128, 2, 512])
        if graph:
            WO = s.sb("WO", [128, KC, D])
            base = s.sb("base", [P, P])
            idx = s.sb("idx", [P, B], I32)
            G = s.sb("G", [P, B, GW])
            GM = s.sb("GM", [P, B, P])
        sem = s.sem
        (loaded, staged, go, open_ready, sums_ready, a_ready, at_ready, att_ready, n_var, n_sd, r_ready, rt_turned,
         rt_ready, h_ready, h_free, ht_ready, y_ready, msg_turned, sums_used) = (sem(x) for x in (
             "loaded", "staged", "go", "open_ready", "sums_ready", "a_ready", "at_ready", "att_ready", "n_var", "n_sd",
             "r_ready", "rt_turned", "rt_ready", "h_ready", "h_free", "ht_ready", "y_ready", "msg_turned", "sums_used"))
        rows = s.gather_sem("rows")
        NL = 16 * (9 + (2 if graph else 0))

        def pty(ps, b, w):
            return ps[:, b // 2, (b % 2) * 256:(b % 2) * 256 + w]

        with nc.Block() as block:
            @block.sync
            def _(sp):
                sp.dma_start(W1[:], chunks(w1)).then_inc(loaded, 16)
                sp.dma_start(W2[:], chunks(w2)).then_inc(loaded, 16)
                sp.dma_start(b1[:], bb1.rearrange("(c p) -> p c", p=128), allow_slow_non_contiguous=True).then_inc(loaded, 16)
                for m, x in enumerate((add0, g1, be1, bb2, g2, be2)):
                    sp.dma_start(vec[:, m, :], row(x, P)).then_inc(loaded, 16)
                if graph:
                    sp.dma_start(WO[:], chunks(a["L1_gnn_Wo_w"])).then_inc(loaded, 16)
                    sp.dma_start(base[:], a["c_base"]).then_inc(loaded, 16)
                sp.wait_ge(loaded, NL)

            if graph:
                @block.gpsimd
                def _(pool):
                    with pool.Fori(0, ITERS) as i:
                        pool.wait_ge(staged, i + 1)
                        pool.sem_inc(go, 1)
                        for b in range(B):
                            nc.gpsimd.indirect_dma_start(out=G[:, b, :], out_offset=None, in_=k.run,
                                                         in_offset=bass.IndirectOffsetOnAxis(ap=idx[:, b:b + 1], axis=0)
                                                         ).then_inc(rows, 16)

            def turn(pe, src, ready):
                for b in range(B):
                    for c in range(KC):
                        ins = nc.tensor.transpose(pty(PT, b, 250)[:, c * P:c * P + P], src[:, b, c * 128:c * 128 + 128],
                                                  k.IDENT[0:P, 0:P])
                ins.then_inc(ready, 1)

            def keep_turned(act, ready):
                for b in range(B):
                    ins = nc.scalar.activation(RT[:, :, b, :], pty(PT, b, 250).rearrange("p (c n) -> p c n", c=KC), ACT.Copy)
                ins.then_inc(ready, 1)

            @block.tensor
            def _(pe):
                pe.wait_ge(loaded, NL)
                with pe.Fori(0, ITERS) as i:
                    if graph:
                        for b in range(B):
                            pe.wait_ge(open_ready, i * B + b + 1)
                            pe.wait_ge(sums_used, i * B + b + 1)
                            nc.tensor.matmul(HP[0:P, b % 2, 0:GW], GM[:, b, :], k.RLAST[:], start=True, stop=True
                                             ).then_inc(sums_ready, 1)
                        pe.wait_ge(a_ready, i + 1)
                        turn(pe, G, msg_turned)
                        pe.wait_ge(at_ready, i + 1)
                        for b in range(B):
                            for c in range(KC):
                                ins = nc.tensor.matmul(pty(PY, b, D), RT[:, c, b, :], WO[:, c, :], start=(c == 0), stop=(c == KC - 1))
                        ins.then_inc(att_ready, 1)
                    pe.wait_ge(r_ready, i + 1)
                    turn(pe, R, rt_turned)
                    pe.wait_ge(rt_ready, i + 1)
                    for c in range(nh):
                        for q, (lo, hi) in enumerate(PIECES):
                            pe.wait_ge(h_free, i * 2 * nh + 2 * c + q + 1)
                            for kc in range(KC):
                                ins = nc.tensor.matmul(HP[:, q, 0:hi - lo], W1[:, kc, c * 128:c * 128 + 128],
                                                       RT[:, kc, lo // P:hi // P, :], start=(kc == 0), stop=(kc == KC - 1))
                            ins.then_inc(h_ready, 1)
                    pe.wait_ge(ht_ready, i + 1)
                    for b in range(B):
                        for c in range(nh):
                            ins = nc.tensor.matmul(pty(PY, b, D), HT[:, c, b * P:b * P + P], W2[:, c, :],
                                                   start=(c == 0), stop=(c == nh - 1))
                    ins.then_inc(y_ready, 1)

            @block.scalar
            def _(act):
                act.sem_inc(h_free, 2)
                act.wait_ge(loaded, NL)
                with act.Fori(0, ITERS) as i:
                    if graph:
                        act.wait_ge(msg_turned, i + 1)
                        keep_turned(act, at_ready)
                    act.wait_ge(n_var, 2 * i + 1)
                    nc.scalar.activation(sd[:], var[:], ACT.Sqrt).then_inc(n_sd, 1)
                    act.wait_ge(rt_turned, i + 1)
                    keep_turned(act, rt_ready)
                    for c in range(nh):
                        for q, (lo, hi) in enumerate(PIECES):
                            act.wait_ge(h_ready, i * 2 * nh + 2 * c + q + 1)
                            nc.scalar.activation(HT[:, c, lo:hi], HP[:, q, 0:hi - lo], act_func,
                                                 bias=b1[:, c:c + 1]).then_inc(h_free, 1)
                    act.drain().then_inc(ht_ready, 1)
                    act.wait_ge(n_var, 2 * i + 2)
                    nc.scalar.activation(sd[:], var[:], ACT.Sqrt).then_inc(n_sd, 1)

            def wide(m):
                return vec[:, m, :].unsqueeze(1).to_broadcast([P, B, D])

            @block.vector
            def _(v):
                def layernorm(i, which, gm):
                    for b in range(B):
                        v.bn_stats(stat[:, b, :], R[:, b, :])
                    v.drain()
                    for b in range(B):
                        v.bn_aggr(mv[:, b, :], stat[:, b, :])
                    v.drain()
                    v.tensor_scalar(var[:], mv[:, :, 1], eps, None, ALU.add).then_inc(n_var, 1)
                    v.wait_ge(n_sd, 2 * i + which + 1)
                    v.reciprocal(var[:], sd[:])
                    v.drain()
                    for b in range(B):
                        v.tensor_scalar(R[:, b, :], R[:, b, :], mv[:, b, 0:1], var[:, b:b + 1], ALU.subtract, ALU.mult)
                    v.drain()
                    v.tensor_tensor(R[:], R[:], wide(gm), ALU.mult)
                    v.drain()
                    v.tensor_tensor(R[:], R[:], wide(gm + 1), ALU.add)
                    return v.drain()

                v.sem_inc(sums_used, 2)
                v.wait_ge(loaded, NL)
                with v.Fori(0, ITERS) as i:
                    if graph:
                        v.tensor_copy(idx[:], k.LAST[:, bass.ds(i * B, B)]).then_inc(staged, 1)
                        for b in range(B):
                            open_nodes(v, k, GM[:, b, :], base[:], i * B + b).then_inc(open_ready, 1)
                        v.wait_ge(rows, (i + 1) * 16 * B)
                        for b in range(B):
                            v.wait_ge(sums_ready, i * B + b + 1)
                            v.tensor_tensor(G[:, b, :], G[:, b, :], HP[0:P, b % 2, 0:GW], ALU.add)
                            v.drain().then_inc(sums_used, 1)
                        v.tensor_scalar(G[:, :, D:GW], G[:, :, D:GW], 1e-8, None, ALU.add)
                        v.drain()
                        v.reciprocal(G[:, :, D:GW], G[:, :, D:GW])
                        v.drain()
                        for b in range(B):
                            g = G[:, b, 0:D].rearrange("p (h d) -> p h d", h=H)
                            v.tensor_tensor(g, g, bcast(G[:, b, D:GW], DH), ALU.mult)
                        v.drain()
                        for b in range(B):
                            v.tensor_scalar(G[:, b, 0:D], G[:, b, 0:D], k.HAS[:, bass.ds(i * B + b, 1)], None, ALU.mult)
                        v.drain().then_inc(a_ready, 1)
                        v.wait_ge(att_ready, i + 1)
                        for b in range(B):
                            v.tensor_tensor(R[:, b, :], pty(PY, b, D), XN[:, i * B + b, 0:D], ALU.add)
                    else:
                        v.tensor_tensor(R[:], k.ACC[:, bass.ds(i * B, B), :], XN[:, bass.ds(i * B, B), 0:D], ALU.add)
                    v.drain()
                    v.tensor_tensor(R[:], R[:], wide(0), ALU.add)
                    v.drain()
                    layernorm(i, 0, 1).then_inc(r_ready, 1)
                    v.wait_ge(y_ready, i + 1)
                    for b in range(B):
                        v.tensor_tensor(R[:, b, :], R[:, b, :], pty(PY, b, D), ALU.add)
                    v.drain()
                    v.tensor_tensor(R[:], R[:], wide(3), ALU.add)
                    v.drain()
                    layernorm(i, 1, 4)
                    v.tensor_tensor(k.X[:, bass.ds(i * B, B), :], k.X[:, bass.ds(i * B, B), :], R[:], ALU.add)
                    v.drain()


def stage_linear_attention(k, XN, XNT, S, h0, heads, with_scores):
    nc, a = k.nc, k.a
    CB = B * P
    with k.scope() as s:
        WQ = s.sb("WQ", [128, KC, KD])
        WK = s.sb("WK", [128, KC, KD])
        WV = s.sb("WV", [128, KC, KD])
        WO = s.sb("WO", [128, KC, D])
        bv = s.sb("bv", [1, KD])
        PR = s.sb("PR", [128, 2, KD])
        PJ = s.sb("PJ", [128, KC, KD])
        bqk = s.sb("bqk", [128, 2, H, KC])
        bcur = s.sb("bcur", [128, 2, KC])
        half = s.sb("half", [128, 128])
        shift = s.sb("shift", [128, 1])
        QT = s.sb("QT", [128, KC, CB])
        SQ = s.sb("SQ", [128, KC, CB])
        PH = s.sb("PH", [128, 2, CB])
        PK = s.sb("PK", [P, B, KD])
        nb = s.sb("nb", [P, B])
        AS = s.sb("AS", [128, 2, D + 1])
        AT = s.sb("AT", [128, KC, KD])
        AL = s.sb("AL", [1, KD])
        KVT = s.sb("KVT", [128, KC, KD])
        KO = s.sb("KO", [128, 2, D + 1])
        rz = s.sb("rz", [P, 3])
        CP = s.ps("CP", [128, 2, 512])
        UP = s.ps("UP", [128, 3, 512])
        AP = s.ps("AP", [128, 2, 512])
        TP = s.ps("TP", [128, 512])
        sem = s.sem
        (loaded, proj_turned, proj_kept, ready0, wk_loaded, wq_loaded, wvo_loaded, k_used, q_used, vo_used,
         c_ready, c_free, qt_ready, qt_free, sq_ready, u_ready, u_read, pk_exp, pk_ready, a_zeroed, a_ready, as_ready,
         t_ready, t_kept, kv_ready, kv_kept, ko_ready, ko_kept, c_u_free, ph_exp, ph_ready, ph_free, o_ready, nb_ready,
         pk_free, u_free, begun) = (
            sem(x) for x in (
                "loaded", "proj_turned", "proj_kept", "ready0", "wk_loaded", "wq_loaded", "wvo_loaded", "k_used", "q_used",
                "vo_used", "c_ready", "c_free", "qt_ready", "qt_free", "sq_ready", "u_ready", "u_read", "pk_exp", "pk_ready",
                "a_zeroed", "a_ready", "as_ready", "t_ready", "t_kept", "kv_ready", "kv_kept", "ko_ready", "ko_kept", "c_u_free",
                "ph_exp", "ph_ready", "ph_free", "o_ready", "nb_ready", "pk_free", "u_free", "begun"))
        if with_scores:
            edges = EdgeScores(k, s, S, s.sb("GK", [P, CW, D]), s.sb("GQ", [P, CW, D]), s.sb("ki", [P, CW], I32),
                               s.sb("qi", [P, CW], I32))
            assert STEPS == heads * ITERS
        else:
            edges = EdgeSums(k, s, k.sup, k.run, s.sb("G", [P, CW, GW]), s.sb("idx", [P, CW], I32), S)
            assert STEPS == (2 * heads - 1) * ITERS
        QTS, CPS = 2 * ITERS, 4 * ITERS + 8 * ITERS

        with nc.Block() as block:
            @block.sync
            def _(sp):
                sp.dma_start(PR[:], chunks(a["L1_mix_proj"])).then_inc(loaded, 16)
                for m, x in enumerate((a["L1_mix_bq"], a["L1_mix_bk"])):
                    for c in range(KC):
                        sp.dma_start(bqk[:, m, :, c], x.rearrange("h (c p) -> c p h", p=128)[c],
                                     allow_slow_non_contiguous=True).then_inc(loaded, 16)

                def load_k(h):
                    sp.wait_ge(k_used, h + 1)
                    sp.dma_start(WK[:], chunks(a["L1_mix_Wk"].rearrange("p h n -> p (h n)"))[:, :, bass.ds((h0 + h) * KD, KD)]).then_inc(wk_loaded, 16)

                def load_vo(h):
                    sp.wait_ge(vo_used, h + 1)
                    sp.dma_start(WV[:], chunks(a["L1_mix_Wv"].rearrange("p h n -> p (h n)"))[:, :, bass.ds((h0 + h) * KD, KD)]).then_inc(wvo_loaded, 16)
                    sp.dma_start(WO[:], a["L1_mix_Wo"].rearrange("h (c p) n -> h p c n", p=128)[h0 + h]).then_inc(wvo_loaded, 16)
                    sp.dma_start(bv[:], a["L1_mix_bv"][bass.ds(h0 + h, 1), :]).then_inc(wvo_loaded, 16)

                def load_q(h):
                    sp.wait_ge(q_used, h + 1)
                    sp.dma_start(WQ[:], chunks(a["L1_mix_Wq"].rearrange("p h n -> p (h n)"))[:, :, bass.ds((h0 + h) * KD, KD)]).then_inc(wq_loaded, 16)

                if with_scores:
                    with sp.Fori(0, heads) as h:
                        load_k(h)
                        load_vo(h)
                        load_q(h)
                else:
                    load_k(0)
                    load_vo(0)
                    load_q(0)
                    edges.sync_begin(sp)
                    with sp.Fori(0, heads - 1) as h:
                        edges.sync_steps(sp, 2 * h * ITERS, ITERS)
                        load_k(h + 1)
                        load_vo(h + 1)
                        edges.sync_steps(sp, (2 * h + 1) * ITERS, ITERS)
                        load_q(h + 1)
                    edges.sync_steps(sp, 2 * (heads - 1) * ITERS, ITERS)
                    edges.sync_end(sp)
                sp.wait_ge(wq_loaded, 16 * heads)

            @block.gpsimd
            def _(pool):
                edges.pool(pool)

            @block.tensor
            def _(pe):
                for free in (qt_free, k_used, vo_used, q_used):
                    pe.sem_inc(free, 1)
                pe.sem_inc(pk_free, B)
                pe.sem_inc(ph_free, 1)
                pe.wait_ge(loaded, 80)
                for r in range(2):
                    for c in range(KC):
                        ins = nc.tensor.transpose(AP[:, r, c * 128:c * 128 + 128], PR[:, r, c * 128:c * 128 + 128], k.IDENT[:])
                ins.then_inc(proj_turned, 1)
                pe.wait_ge(ready0, 1)

                def turned(W, base_c, i):
                    for c in range(KC):
                        for q, (lo, hi) in enumerate(PIECES):
                            pe.wait_ge(c_free, base_c + 2 * c + q + 1)
                            for kc in range(KC):
                                ins = nc.tensor.matmul(CP[:, q, 0:hi - lo], W[:, kc, c * 128:c * 128 + 128],
                                                       XNT[:, kc, bass.ds(i * CB + lo, hi - lo)],
                                                       start=(kc == 0), stop=(kc == KC - 1))
                            ins.then_inc(c_ready, 1)

                def key_sums(h, i, b):
                    pe.wait_ge(pk_ready, h * T + i * B + b + 1)
                    for r in range(2):
                        ins = nc.tensor.matmul(AP[:, r, 0:D + 1], PK[:, b, r * 128:r * 128 + 128], XN[:, i * B + b, :],
                                               start=False, stop=False, skip_group_check=True)
                    ins.then_inc(pk_free, 1)

                def key_item(h, i, first):
                    turned(WK, h * CPS + i * 4, i)
                    if not first:
                        key_sums(h, i - 1, B - 2)
                        key_sums(h, i - 1, B - 1)
                    pe.wait_ge(sq_ready, h * QTS + i + 1)
                    for b in range(B):
                        pe.wait_ge(u_free, h * 2 * T + i * B + b + 1)
                        for kc in range(KC):
                            nc.tensor.matmul(UP[0:P, b % 3, 0:KD], QT[:, kc, b * P:b * P + P], PJ[:, kc, :],
                                             start=(kc == 0), stop=(kc == KC - 1))
                        nc.tensor.matmul(UP[0:P, b % 3, KD:KD + 1], SQ[:, 0, b * P:b * P + P], half[:, 0:1],
                                         start=True, stop=True).then_inc(u_ready, 1)
                        if b >= 2:
                            key_sums(h, i, b - 2)
                    pe.drain().then_inc(qt_free, 1)

                def phi_q(h, i):
                    for r in range(2):
                        for q, (lo, hi) in enumerate(PIECES):
                            pe.wait_ge(c_free, h * CPS + 4 * ITERS + i * 8 + 4 + 2 * r + q + 1)
                            for kc in range(KC):
                                nc.tensor.matmul(CP[:, q, 0:hi - lo], PJ[:, kc, r * 128:r * 128 + 128], QT[:, kc, lo:hi],
                                                 start=(kc == 0), stop=False)
                            if r == 0 and q == 0:
                                pe.wait_ge(sq_ready, h * QTS + ITERS + i + 1)
                            nc.tensor.matmul(CP[:, q, 0:hi - lo], half[:], SQ[:, 0, lo:hi],
                                             start=False, stop=True).then_inc(c_ready, 1)
                    pe.drain().then_inc(qt_free, 1)

                def outputs(h, i):
                    pe.wait_ge(ph_ready, h * ITERS + i + 1)
                    for b in range(B):
                        pe.wait_ge(u_free, h * 2 * T + T + i * B + b + 1)
                        for r in range(2):
                            ins = nc.tensor.matmul(UP[0:P, b % 3, 0:D + 1], PH[:, r, b * P:b * P + P], KO[:, r, :],
                                                   start=(r == 0), stop=(r == 1))
                        ins.then_inc(o_ready, 1)
                    pe.drain().then_inc(ph_free, 1)

                def query_turned(h, i):
                    turned(WQ, h * CPS + 4 * ITERS + i * 8, i)

                with pe.Fori(0, heads) as h:
                    pe.wait_ge(wk_loaded, 16 * h + 16)
                    pe.wait_ge(a_zeroed, h + 1)
                    pe.sem_inc(begun, 1)
                    key_item(h, 0, True)
                    with pe.Fori(1, ITERS) as i:
                        key_item(h, i, False)
                    key_sums(h, ITERS - 1, B - 2)
                    key_sums(h, ITERS - 1, B - 1)
                    pe.drain().then_inc(a_ready, 1)
                    pe.sem_inc(k_used, 1)
                    pe.wait_ge(wq_loaded, 16 * h + 16)
                    query_turned(h, 0)
                    pe.wait_ge(as_ready, h + 1)
                    for c in range(KC):
                        for r in range(2):
                            ins = nc.tensor.transpose(TP[:, c * 256 + r * 128:c * 256 + r * 128 + 128],
                                                      AS[:, r, c * 128:c * 128 + 128], k.IDENT[:])
                    ins.then_inc(t_ready, 1)
                    pe.wait_ge(qt_ready, h * QTS + ITERS + 1)
                    phi_q(h, 0)
                    pe.wait_ge(t_kept, 2 * h + 1)
                    for r in range(2):
                        ins = nc.tensor.transpose(TP[0:1, r * 128:r * 128 + 128], AS[:, r, D:D + 1], k.IDENT[:])
                    ins.then_inc(t_ready, 1)
                    pe.wait_ge(t_kept, 2 * h + 2)
                    pe.wait_ge(wvo_loaded, 48 * h + 48)
                    for c in range(KC):
                        for kc in range(KC):
                            nc.tensor.matmul(TP[:, c * 256:c * 256 + 256], WV[:, kc, c * 128:c * 128 + 128], AT[:, kc, :],
                                             start=(kc == 0), stop=False)
                        ins = nc.tensor.matmul(TP[:, c * 256:c * 256 + 256], bv[:, c * 128:c * 128 + 128], AL[:],
                                               start=False, stop=True)
                    ins.then_inc(kv_ready, 1)
                    pe.wait_ge(kv_kept, h + 1)
                    for r in range(2):
                        for kc in range(KC):
                            ins = nc.tensor.matmul(TP[:, r * 256:r * 256 + 256], KVT[:, kc, r * 128:r * 128 + 128], WO[:, kc, :],
                                                   start=(kc == 0), stop=(kc == KC - 1))
                    ins.then_inc(ko_ready, 1)
                    pe.drain().then_inc(vo_used, 1)
                    pe.wait_ge(ko_kept, h + 1)
                    pe.sem_inc(begun, 1)
                    with pe.Fori(1, ITERS) as i:
                        query_turned(h, i)
                        outputs(h, i - 1)
                        pe.wait_ge(qt_ready, h * QTS + ITERS + i + 1)
                        phi_q(h, i)
                    outputs(h, ITERS - 1)
                    pe.sem_inc(q_used, 1)

            @block.scalar
            def _(act):
                act.sem_inc(c_free, 2)
                act.wait_ge(ready0, 1)

                def turned(m, item, cbase):
                    act.wait_ge(qt_free, item + 1)
                    for c in range(KC):
                        for q, (lo, hi) in enumerate(PIECES):
                            act.wait_ge(c_ready, cbase + 2 * c + q + 1)
                            nc.scalar.activation(QT[:, c, lo:hi], CP[:, q, 0:hi - lo], ACT.Identity, scale=QSCALE,
                                                 bias=bcur[:, m, c:c + 1])
                            nc.scalar.activation(SQ[:, c, lo:hi], CP[:, q, 0:hi - lo], ACT.Square, scale=QSCALE,
                                                 bias=bcur[:, m, c:c + 1]).then_inc(c_free, 1)
                    act.drain().then_inc(qt_ready, 1)

                def key_item(h, i):
                    turned(1, h * QTS + i, h * CPS + i * 4)
                    for b in range(B):
                        n = h * T + i * B + b
                        act.wait_ge(pk_free, n + 1)
                        act.wait_ge(nb_ready, n + 1)
                        nc.scalar.activation(PK[:, b, :], UP[0:P, b % 3, 0:KD], ACT.Exp, bias=nb[:, b:b + 1]
                                             ).then_inc(pk_exp, 1)

                def query_turned(h, i):
                    turned(0, h * QTS + ITERS + i, h * CPS + 4 * ITERS + i * 8)

                def phi_q(h, i):
                    act.wait_ge(ph_free, h * ITERS + i + 1)
                    for r in range(2):
                        for q, (lo, hi) in enumerate(PIECES):
                            act.wait_ge(c_ready, h * CPS + 4 * ITERS + i * 8 + 4 + 2 * r + q + 1)
                            nc.scalar.activation(PH[:, r, lo:hi], CP[:, q, 0:hi - lo], ACT.Exp, bias=shift[:, 0:1]
                                                 ).then_inc(c_free, 1)
                    act.drain().then_inc(ph_exp, 1)

                with act.Fori(0, heads) as h:
                    nc.scalar.activation(bcur[:], bqk[:, :, h0 + h, :], ACT.Copy)
                    act.drain()
                    with act.Fori(0, ITERS) as i:
                        key_item(h, i)
                    act.wait_ge(a_ready, h + 1)
                    nc.scalar.activation(AS[:], AP[:, :, 0:D + 1], ACT.Copy).then_inc(as_ready, 1)
                    query_turned(h, 0)
                    act.wait_ge(t_ready, 2 * h + 1)
                    nc.scalar.activation(AT[:], TP[:].rearrange("p (c m) -> p c m", c=KC), ACT.Copy).then_inc(t_kept, 1)
                    phi_q(h, 0)
                    act.wait_ge(t_ready, 2 * h + 2)
                    nc.scalar.activation(AL[:], TP[0:1, 0:KD], ACT.Copy).then_inc(t_kept, 1)
                    act.wait_ge(kv_ready, h + 1)
                    nc.scalar.activation(KVT[:], TP[:].rearrange("p (c m) -> p c m", c=KC), ACT.Copy).then_inc(kv_kept, 1)
                    act.wait_ge(ko_ready, h + 1)
                    nc.scalar.activation(KO[:, :, 0:D], TP[:].rearrange("p (c m) -> p c m", c=2), ACT.Copy)
                    nc.scalar.activation(KO[:, :, D:D + 1], AS[:, :, D:D + 1], ACT.Copy)
                    act.drain().then_inc(ko_kept, 1)
                    with act.Fori(1, ITERS) as i:
                        query_turned(h, i)
                        phi_q(h, i)

            @block.vector
            def _(v):
                v.memset(half[:], -0.5)
                v.memset(shift[:], -LN_SQRT_M)
                v.wait_ge(proj_turned, 1)
                v.tensor_copy(PJ[:].rearrange("p c (r m) -> p r c m", r=2), AP[:, :, 0:256].rearrange("p r (c m) -> p r c m", c=KC))
                v.tensor_scalar(bqk[:], bqk[:], QSCALE, None, ALU.mult)
                v.drain()
                v.memset(AP[:], 0.0)
                if h0 == 0:
                    v.memset(k.ACC[:], 0.0)
                edges.begin(v)
                v.sem_inc(u_free, 2)
                v.sem_inc(a_zeroed, 1)
                v.drain().then_inc(ready0, 1)

                def edge_part(h, phase, i, at):
                    if not with_scores:
                        if at < 4:
                            edges.sub(v, (2 * h + phase) * ITERS + i, at)
                    elif at in (1, 3):
                        u = 2 * (phase * ITERS + i) + at // 2
                        edges.sub(v, h * ITERS + u // 4, u % 4)

                def squares(item):
                    v.wait_ge(qt_ready, item + 1)
                    v.tensor_tensor(SQ[:, 0, :], SQ[:, 0, :], SQ[:, 1, :], ALU.add).then_inc(sq_ready, 1)

                def key_item(h, i):
                    squares(h * QTS + i)
                    for b in range(B):
                        n = h * T + i * B + b
                        v.wait_ge(u_ready, n + 1)
                        v.tensor_scalar(nb[:, b:b + 1], UP[0:P, b % 3, KD:KD + 1], -LN_SQRT_M, None, ALU.add
                                        ).then_inc(nb_ready, 1)
                        v.wait_ge(pk_exp, n + 1)
                        v.sem_inc(u_free, 1)
                        v.tensor_scalar(PK[:, b, :], PK[:, b, :], EPS_ATT, None, ALU.add).then_inc(pk_ready, 1)
                        edge_part(h, 0, i, b)

                def add_outputs(h, i, edges_of=None):
                    for b in range(B):
                        v.wait_ge(o_ready, h * T + i * B + b + 1)
                        v.reciprocal(rz[:, b % 3:b % 3 + 1], UP[0:P, b % 3, D:D + 1])
                        v.drain()
                        v.scalar_tensor_tensor(k.ACC[:, i * B + b, :], UP[0:P, b % 3, 0:D], rz[:, b % 3:b % 3 + 1],
                                               k.ACC[:, i * B + b, :], ALU.mult, ALU.add).then_inc(u_free, 1)
                        if edges_of is not None and b in (1, 3):
                            edge_part(h, 1, edges_of, b // 2)

                def query_item(h, i, first, with_edges=True):
                    squares(h * QTS + ITERS + i)
                    if not first:
                        add_outputs(h, i - 1, i if with_edges else None)
                    elif with_edges:
                        edge_part(h, 1, i, 0)
                        edge_part(h, 1, i, 1)
                    v.wait_ge(ph_exp, h * ITERS + i + 1)
                    v.tensor_scalar(PH[:], PH[:], EPS_ATT, None, ALU.add).then_inc(ph_ready, 1)
                    if with_edges:
                        edge_part(h, 1, i, 2)
                        edge_part(h, 1, i, 3)

                def between(h):
                    v.wait_ge(as_ready, h + 1)
                    v.memset(AP[:], 0.0).then_inc(a_zeroed, 1)

                if with_scores:
                    with v.Fori(0, heads) as h:
                        for i in range(ITERS):
                            key_item(h, i)
                        between(h)
                        for i in range(ITERS):
                            query_item(h, i, i == 0)
                        add_outputs(h, ITERS - 1)
                else:
                    last = heads - 1
                    with v.Fori(0, last) as h:
                        with v.Fori(0, ITERS) as i:
                            key_item(h, i)
                        between(h)
                        query_item(h, 0, True)
                        with v.Fori(1, ITERS) as i:
                            query_item(h, i, False)
                        add_outputs(h, ITERS - 1)
                    with v.Fori(0, ITERS) as i:
                        key_item(last, i)
                    edges.end(v)
                    between(last)
                    query_item(last, 0, True, False)
                    with v.Fori(1, ITERS) as i:
                        query_item(last, i, False, False)
                    add_outputs(last, ITERS - 1)


def layer1_mix(k):
    a = k.a
    with k.scope() as f:
        k.ACC = f.sb("ACC", [P, T, D])
        XN = f.sb("XN", [P, T, D + 1])
        with k.scope() as g:
            XNT = g.sb("XNT", [128, KC, N])
            stage_normalise(k, 1e-5, XNT, XN=XN, tables=(
                (a["L1_gnn_Wq"], k.queries), (a["L1_gnn_Wk"], k.keys), (a["L1_gnn_Wv"], k.sup)))
            S = g.sb("S", [P, H, TE])
            stage_linear_attention(k, XN, XNT, S, 0, 5, True)
            stage_edge_weights(k, S)
            stage_linear_attention(k, XN, XNT, S, 5, 3, False)
        stage_post(k, None, None, 2, ACT.Relu, a["L1_mix_W1"], a["L1_mix_bias1"], a["L1_mix_W2"], a["L1_mix_bias2"],
                   a["L1_mix_g1"], a["L1_mix_beta1"], a["L1_mix_g2"], a["L1_mix_beta2"], 1e-6, False, XN, a["L1_mix_bo"])
        stage_post(k, None, None, 4, ACT.Gelu, a["L1_gnn_ffn_w1"], a["L1_gnn_ffn_b1"], a["L1_gnn_ffn_w2"], a["L1_gnn_ffn_b2"],
                   a["L1_gnn_ln1_g"], a["L1_gnn_ln1_b"], a["L1_gnn_ln2_g"], a["L1_gnn_ln2_b"], 1e-5, True, XN, a["L1_gnn_Wo_b"])
def program(nc, a, out):
    with ExitStack() as stack:
        k = Core(nc, a, stack)
        keep = stack.enter_context(k.scope())
        k.X = keep.sb("X", [P, T, D])
        k.IDENT = keep.sb("IDENT", [128, 128])
        k.NODE = keep.sb("NODE", [P, T])
        k.MV = keep.sb("MV", [P, T, 2])
        k.RSTD = keep.sb("RSTD", [P, T])
        k.SD = keep.sb("SD", [P, T])
        k.SRC = keep.sb("SRC", [P, TE], I32)
        k.DST = keep.sb("DST", [P, TE], I32)
        k.SAME = keep.sb("SAME", [P, TE])
        k.FROM_LEFT = keep.sb("FROM_LEFT", [P, P])
        k.FROM_RIGHT = keep.sb("FROM_RIGHT", [P, P])
        k.OPEN = keep.sb("OPEN", [P, T])
        k.LAST = keep.sb("LAST", [P, T], I32)
        k.HAS = keep.sb("HAS", [P, T])
        k.RLAST = keep.sb("RLAST", [P, GW])
        k.keys = nc.dram_tensor("keys", [N, D], F32, kind="Internal").ap()
        k.queries = nc.dram_tensor("queries", [N, D], F32, kind="Internal").ap()
        k.weights = nc.dram_tensor("router_weights", [N, 1], F32, kind="Internal").ap()
        k.sup = nc.dram_tensor("support", [N, D], F32, kind="Internal").ap()
        k.run = nc.dram_tensor("running_sums", [E, GW], F32, kind="Internal").ap()
        k.run0 = nc.dram_tensor("running_sums0", [E, D], F32, kind="Internal").ap()
        stage_load(k)
        stage_edges(k)
        with k.scope() as s0:
            s0.WPT = s0.sb("WPT", [128, KC, D])
            s0.bias = s0.sb("bias", [P, 3 * D])
            s0.second = s0.sb("second", [128, H * FC])
            s0.fac = s0.sb("fac", [P, H])
            s0.bsum = s0.sb("bsum", [P, 2, D])
            s0.KV = s0.sb("KV", [128, H * FC, V1])
            k.QKV = s0.sb("QKV", [P, T, 3 * D])
            with k.scope() as w:
                W = w.sb("W", [128, KC, 4 * D])
                stage_weights0(k, s0, W)
                stage_normalise(k, 1e-5, tables=[(None, None)] * 3 + [(None, k.sup)], W=W, KEPT=k.QKV)
            stage_layer0_mix(k, s0)
            stage_layer0_nodes(k, s0)
        with k.scope() as f:
            XNT = f.sb("XNT", [128, KC, N])
            f.selw = f.sb("selw", [P, T])
            stage_normalise(k, 1e-5, XNT, ranked=f)
            stage_layer0_ffn(k, f, XNT)
        layer1_mix(k)
        with k.scope() as f:
            XNT = f.sb("XNT", [128, KC, N])
            stage_normalise(k, 1e-5, XNT)
            stage_experts(k, XNT, out)


def kernel(**inputs):
    import concourse.bacc as bacc
    from concourse.bass_utils import run_bass_kernel_spmd

    nc = bacc.Bacc("TRN2", target_bir_lowering=False, num_devices=1)
    arrays = {name: np.ascontiguousarray(x) for name, x in inputs.items() if name != "L0_ffn_attention_mask"}
    arrays["L0_mix_temperature"] = arrays["L0_mix_temperature"].reshape(H)
    arrays.update(constants())
    a = {name: nc.dram_tensor(name, x.shape, mybir.dt.from_np(x.dtype), kind="ExternalInput").ap()
         for name, x in arrays.items()}
    out = nc.dram_tensor("out", (N, D), F32, kind="ExternalOutput").ap()
    program(nc, a, out)
    return run_bass_kernel_spmd(nc, [arrays], core_ids=[0]).results[0]["out"]
```

```python
from contextlib import ExitStack

import numpy as np

import concourse.bass as bass
from concourse import mybir

F32 = mybir.dt.float32
I32 = mybir.dt.int32
ALU = mybir.AluOpType
ACT = mybir.ActivationFunctionType
AX = mybir.AxisListType

P = 125
T = 25
N = P * T
TE = 425
E = P * TE
D = 256
KC = D // 128
H = 8
DH = D // H
B = 5
ITERS = T // B
HID = 1024
HC = HID // 128
GW = D + H

NQ = 17 * DH
NF = NQ + DH + 1
FC = 5
FW = FC * 128
V1 = DH + 1


def second_order_weights():
    scale = float(DH) ** 0.25
    w = np.zeros(FW, np.float64)
    w[:NQ] = 0.5 * np.where((np.arange(NQ) // DH > 0) & (np.arange(NQ) // DH < 16), 2.0, 1.0)
    w[NQ:NQ + DH] = scale ** 2
    w[NQ + DH] = scale ** 4
    return np.tile((w / N).reshape(FC, 128).T, (1, H)).astype(np.float32)


def constants():
    p = np.arange(P, dtype=np.float32)
    return {
        "c_ident": np.eye(128, dtype=np.float32),
        "c_node": (p[:, None] * T + np.arange(T, dtype=np.float32)).astype(np.float32),
        "c_column": np.tile(np.arange(T, dtype=np.float32), (P, 1)),
        "c_before": np.triu(np.ones((P, P), np.float32), 1).T.copy(),
        "c_after": np.triu(np.ones((P, P), np.float32), 1),
        "c_base": np.tile(p * T, (P, 1)).astype(np.float32),
        "c_reversed": np.tile(8.0 - np.arange(8, dtype=np.float32), (P, 1)).astype(np.float32),
        "c_second": second_order_weights(),
        "c_route": np.concatenate([np.tile(P * np.arange(T), (128, 1)), np.tile(np.arange(SLOTS), (128, 1)),
                                   np.arange(128)[:, None]], axis=1).astype(np.float32),
    }


class Core:

    def __init__(self, nc, a, stack):
        self.nc, self.a, self.stack = nc, a, stack
        self.count = 0

    def scope(self):
        return Scope(self)


class Scope:

    def __init__(self, core):
        self.core, self.nc = core, core.nc

    def __enter__(self):
        self.stack = ExitStack()
        self.stack.__enter__()
        self.sems = []
        return self

    def __exit__(self, *e):
        if self.sems and e[0] is None:
            sems = self.sems
            with self.nc.Block() as block:
                @block.gpsimd
                def _(pool):
                    for sem in sems:
                        pool.sem_clear(sem)
        return self.stack.__exit__(*e)

    def sb(self, name, shape, dt=F32):
        self.core.count += 1
        return self.stack.enter_context(self.nc.sbuf_tensor(f"{name}_{self.core.count}", shape, dt))

    def ps(self, name, shape, dt=F32):
        self.core.count += 1
        return self.stack.enter_context(self.nc.psum_tensor(f"{name}_{self.core.count}", shape, dt))

    def gather_sem(self, name):
        self.core.count += 1
        return self.core.stack.enter_context(self.nc.semaphore(f"{name}_{self.core.count}"))

    def sem(self, name):
        self.core.count += 1
        self.sems.append(self.stack.enter_context(self.nc.semaphore(f"{name}_{self.core.count}")))
        return self.sems[-1]


def node_rows(table):
    return table.rearrange("(p j) d -> p j d", p=P)


def row(vector, n):
    return vector.rearrange("(a d) -> a d", a=1).broadcast_to([n, vector.shape[0]])


def chunks(matrix):
    return matrix.rearrange("(k p) n -> p k n", p=128)


def bcast(ap, n):
    p, h = ap.shape
    return ap.unsqueeze(2).to_broadcast([p, h, n])


def node_stats(k, s, eps, var_ready, sd_ready):
    nc, v = k.nc, k.nc.vector
    with v.Fori(0, ITERS) as i:
        for b in range(B):
            v.bn_stats(s.stat[:, b, :], k.X[:, i * B + b, :])
        v.drain()
        for b in range(B):
            v.bn_aggr(s.mv[:, b, :], s.stat[:, b, :])
        v.drain()
        v.tensor_copy(k.MV[:, bass.ds(i * B, B), :], s.mv[:])
        v.drain()
    v.tensor_scalar(k.RSTD[:], k.MV[:, :, 1], eps, None, ALU.add).then_inc(var_ready, 1)
    v.wait_ge(sd_ready, 1)
    v.reciprocal(k.RSTD[:], k.SD[:])
    v.drain()


class LastEdges:

    def __init__(self, k, s):
        self.k = k
        self.firstrow = s.sb("firstrow", [P, P])
        self.scratch = s.sb("scratch", [P, TE])
        self.pc = s.sb("pc", [P, T])
        self.rowi = s.sb("rowi", [P, T + B], I32)
        self.drow = s.sb("drow", [P, B, TE], I32)
        self.stage_row = s.sb("stage_row", [P, B], I32)
        self.cnt = s.sb("cnt", [P, T])
        self.c5 = s.sb("c5", [P, B])
        self.h5 = s.sb("h5", [P, B])
        self.staged, self.go, self.gathered = s.sem("rows_staged"), s.sem("rows_go"), s.gather_sem("gathered")

    def prepare(self, v):
        pc = self.pc
        for j in range(T):
            v.tensor_scalar(self.scratch[:, 0:P], self.firstrow[:], self.k.NODE[:, j:j + 1], 0.0, ALU.is_le, ALU.add,
                            accum_out=pc[:, j:j + 1])
            v.drain()
        v.tensor_scalar(pc[:], pc[:], -1.0, 0.0, ALU.add, ALU.max)
        v.drain()
        v.tensor_copy(self.rowi[:, 0:T], pc[:])
        v.memset(self.rowi[:, T:T + B], 0)
        v.drain()
        v.tensor_copy(self.stage_row[:], self.rowi[:, 0:B]).then_inc(self.staged, 1)

    def item(self, v, i):
        k, scratch, drow = self.k, self.scratch, self.drow
        v.wait_ge(self.gathered, (i + 1) * 16 * B)
        for b in range(B):
            node = k.NODE[:, bass.ds(i * B + b, 1)]
            v.tensor_scalar(scratch[:], drow[:, b, :], node, 0.0, ALU.is_le, ALU.add, accum_out=self.c5[:, b:b + 1])
            v.drain()
            v.tensor_scalar(scratch[:], drow[:, b, :], node, 0.0, ALU.is_equal, ALU.max, accum_out=self.h5[:, b:b + 1])
            v.drain()
        v.tensor_copy(self.cnt[:, bass.ds(i * B, B)], self.c5[:])
        v.tensor_copy(k.HAS[:, bass.ds(i * B, B)], self.h5[:])
        v.tensor_copy(self.stage_row[:], self.rowi[:, bass.ds(i * B + B, B)]).then_inc(self.staged, 1)
        v.drain()

    def finish(self, v):
        pc = self.pc
        v.scalar_tensor_tensor(pc[:], pc[:], float(TE), self.cnt[:], ALU.mult, ALU.add)
        v.drain()
        v.tensor_scalar(pc[:], pc[:], -1.0, 0.0, ALU.add, ALU.max)
        v.drain()
        v.tensor_copy(self.k.LAST[:], pc[:])

    def pool(self, pool):
        nc = self.k.nc
        table = self.k.a["dst"].rearrange("(p t) -> p t", p=P)
        with pool.Fori(0, ITERS) as i:
            pool.wait_ge(self.staged, i + 1)
            pool.sem_inc(self.go, 1)
            for b in range(B):
                nc.gpsimd.indirect_dma_start(out=self.drow[:, b, :], out_offset=None, in_=table,
                                             in_offset=bass.IndirectOffsetOnAxis(ap=self.stage_row[:, b:b + 1], axis=0)
                                             ).then_inc(self.gathered, 16)


def stage_edges(k, firstrow):
    nc, a = k.nc, k.a
    with k.scope() as s:
        dstf = s.sb("dstf", [P, TE])
        lastrow = s.sb("lastrow", [P, P])
        wide = s.sb("wide", [P, 2, P])
        nexti = s.sb("nexti", [P, 1], I32)
        nextf = s.sb("nextf", [P, 1])
        lc = s.sb("lc", [P, 1])
        before = s.sb("before", [P, P])
        after = s.sb("after", [P, P])
        colc = s.sb("colc", [P, T])
        cnt = s.sb("cnt", [P, 1])
        rows_ps = s.ps("rows_ps", [P, 2, 512])
        x_loaded = s.sem("x_loaded")
        loaded, none, wide_ready, rows_ready = s.sem("loaded"), s.sem("none"), s.sem("wide_ready"), s.sem("rows_ready")
        with nc.Block() as block:
            @block.sync
            def _(sp):
                dst2 = a["dst"].rearrange("(p t) -> p t", p=P)
                sp.dma_start(k.SRC[:], a["src"].rearrange("(p t) -> p t", p=P)).then_inc(loaded, 16)
                sp.dma_start(k.DST[:], dst2).then_inc(loaded, 16)
                sp.dma_start(before[:], a["c_before"]).then_inc(loaded, 16)
                sp.dma_start(after[:], a["c_after"]).then_inc(loaded, 16)
                sp.dma_start(colc[:], a["c_column"]).then_inc(loaded, 16)
                sp.dma_start(k.IDENT[:], a["c_ident"]).then_inc(loaded, 16)
                sp.dma_start(k.NODE[:], a["c_node"]).then_inc(loaded, 16)
                sp.wait_ge(none, 1)
                sp.dma_start(nexti[0:P - 1, :], dst2[1:P, 0:1], allow_slow_non_contiguous=True).then_inc(loaded, 16)
                sp.dma_start(k.X[:], node_rows(a["x"])).then_inc(x_loaded, 16)
                sp.wait_ge(loaded, 128)
                sp.wait_ge(x_loaded, 16)

            @block.tensor
            def _(pe):
                pe.wait_ge(wide_ready, 1)
                for r in range(2):
                    ins = nc.tensor.matmul(rows_ps[:, r, 0:P], wide[:, r, :], k.IDENT[0:P, 0:P], start=True, stop=True)
                ins.then_inc(rows_ready, 1)

            @block.vector
            def _(v):
                v.memset(nexti[:], -1).then_inc(none, 1)
                v.wait_ge(loaded, 128)
                v.tensor_copy(dstf[:], k.DST[:])
                v.tensor_copy(nextf[:], nexti[:])
                v.drain()
                v.tensor_copy(wide[:, 0, :], dstf[:, 0:1].to_broadcast([P, P]))
                v.tensor_copy(wide[:, 1, :], dstf[:, TE - 1:TE].to_broadcast([P, P])).then_inc(wide_ready, 1)
                v.memset(k.SAME[:, 0:1], 0.0)
                v.tensor_tensor(k.SAME[:, 1:TE], dstf[:, 1:TE], dstf[:, 0:TE - 1], ALU.is_equal)
                v.tensor_tensor(lc[:], dstf[:, TE - 1:TE], nextf[:], ALU.is_equal)
                v.tensor_scalar(cnt[:], dstf[:, TE - 1:TE], 1.0, None, ALU.add)
                v.drain()
                v.tensor_tensor(lc[:], lc[:], cnt[:], ALU.mult)
                v.drain()
                v.tensor_scalar(lc[:], lc[:], -1.0, None, ALU.add)
                v.drain()
                v.tensor_scalar(k.OPEN[:], colc[:], lc[:, 0:1], -1.0, ALU.subtract, ALU.mult)
                v.wait_ge(rows_ready, 1)
                v.tensor_copy(firstrow[:], rows_ps[:, 0, 0:P])
                v.tensor_copy(lastrow[:], rows_ps[:, 1, 0:P])
                v.drain()
                v.scalar_tensor_tensor(k.FROM_LEFT[:], lastrow[:], dstf[:, 0:1], before[:], ALU.is_equal, ALU.mult)
                v.scalar_tensor_tensor(k.FROM_RIGHT[:], firstrow[:], dstf[:, TE - 1:TE], after[:], ALU.is_equal, ALU.mult)


def stage_weights0(k, s0, W):
    nc, a = k.nc, k.a
    with k.scope() as s:
        wq = s.sb("wq", [128, 6, D])
        wp = s.sb("wp", [128, 2, D])
        pt = s.ps("pt", [128, 8, 512])
        loaded, turned, taken = s.sem("loaded"), s.sem("turned"), s.sem("taken")
        with nc.Block() as block:
            @block.sync
            def _(sp):
                sp.dma_start(wq[:], chunks(a["L0_mix_Wqkv"])).then_inc(loaded, 16)
                sp.dma_start(wp[:], chunks(a["L0_mix_Wproj"])).then_inc(loaded, 16)
                sp.dma_start(W[:, :, 768:1024], chunks(a["L0_gnn_weight"])).then_inc(loaded, 16)
                sp.dma_start(s0.bias[:], row(a["L0_mix_bqkv"], P)).then_inc(loaded, 16)
                sp.dma_start(s0.second[:], a["c_second"]).then_inc(loaded, 16)
                sp.dma_start(s0.fac[:], row(a["L0_mix_temperature"], P)).then_inc(loaded, 16)
                sp.dma_start(s0.bsum[:, 0, :], row(a["L0_gnn_bias"], P)).then_inc(loaded, 16)
                sp.dma_start(s0.bsum[:, 1, :], row(a["L0_mix_bproj"], P)).then_inc(loaded, 16)
                sp.wait_ge(loaded, 128)

            @block.tensor
            def _(pe):
                pe.wait_ge(loaded, 128)
                for r in range(8):
                    src = wq[:, r, :] if r < 6 else wp[:, r - 6, :]
                    for c in range(KC):
                        ins = nc.tensor.transpose(pt[:, r, c * 128:c * 128 + 128], src[:, c * 128:c * 128 + 128], k.IDENT[:])
                    ins.then_inc(turned, 1)

            @block.vector
            def _(v):
                for r in range(8):
                    v.wait_ge(turned, r + 1)
                    out = W[:, :, r * 128:r * 128 + 128] if r < 6 else s0.WPT[:, :, (r - 6) * 128:(r - 5) * 128]
                    v.tensor_copy(out, pt[:, r, 0:256].rearrange("p (c n) -> p c n", c=KC))
                v.wait_ge(loaded, 128)
                v.tensor_scalar(s0.fac[:], s0.fac[:], float(DH) ** 0.5, None, ALU.mult)


def features(v, U, PHI, phi_ready):
    once = U[:, :, 0:DH].unsqueeze(2).to_broadcast([P, 4, 17, DH])
    shifted = bass.AP(U.tensor, U.offset, [list(U.ap[0]), list(U.ap[1]), [1, 17], [1, DH]])
    v.tensor_copy(PHI[:, :, NQ:NQ + DH], U[:, :, 0:DH])
    v.tensor_tensor(PHI[:, :, 0:NQ].rearrange("p h (o i) -> p h o i", i=DH), once, shifted, ALU.mult)
    v.drain().then_inc(phi_ready, 1)




CW = 17
STEPS = TE // CW
SUBS = ((0, 5), (5, 9), (9, 13), (13, 17))


def gather_rows(nc, pool, wanted, rows, may_fill, go, beside=None):
    staged, go = go
    with pool.Fori(0, STEPS) as n:
        for s, (lo, hi) in enumerate(SUBS):
            may_fill(n, s)
            for numbers, idx, _, _ in wanted:
                nc.gpsimd.tensor_copy(idx[:, lo:hi], numbers[:, bass.ds(n * CW + lo, hi - lo)]).then_inc(staged, 1)
            if beside is not None:
                beside(n, s).then_inc(staged, 1)
            copies = len(wanted) + (beside is not None)
            pool.wait_ge(staged, (4 * n + s + 1) * copies)
            pool.sem_inc(go, 1)
            for t in range(lo, hi):
                for _, idx, table, out in wanted:
                    nc.gpsimd.indirect_dma_start(out=out[:, t, 0:D], out_offset=None, in_=table,
                                                 in_offset=bass.IndirectOffsetOnAxis(ap=idx[:, t:t + 1], axis=0)
                                                 ).then_inc(rows[s], 16)


class EdgeSums:

    def __init__(self, k, s, table, run, G, idx, weights=None):
        self.k, self.nc, self.table, self.weights = k, k.nc, table, weights
        self.width = D if weights is None else GW
        self.G, self.idx = G, idx
        self.run = run.rearrange("(p t) d -> p t d", p=P)
        self.rows = [s.gather_sem(f"rows{b}") for b in range(len(SUBS))]
        self.out = [s.sem(f"sums_out{b}") for b in range(len(SUBS))]
        self.go = s.sem("staged"), s.sem("go")
        self.summed = s.sem("summed")

    def pool(self, pool):
        def may_fill(n, s):
            pool.wait_ge(self.out[s], 16 * n + 16)
            pool.wait_ge(self.summed, 4 * n + s + 2)

        def weights(n, s):
            lo, hi = SUBS[s]
            w = self.weights[:, :, bass.ds(n * CW + lo, hi - lo)].rearrange("p h t -> p t h")
            return self.nc.gpsimd.tensor_copy(self.G[:, lo:hi, D:GW], w)
        gather_rows(self.nc, pool, [(self.k.SRC, self.idx, self.table, self.G)], self.rows, may_fill, self.go,
                    None if self.weights is None else weights)

    def sync_begin(self, sp):
        for s in range(len(SUBS)):
            sp.sem_inc(self.out[s], 16)

    def sync_steps(self, sp, n0, count):
        with sp.Fori(0, count) as i:
            n = n0 + i
            for s, (lo, hi) in enumerate(SUBS):
                sp.wait_ge(self.summed, 4 * n + s + 5)
                sp.dma_start(self.run[:, bass.ds(n * CW + lo, hi - lo), :], self.G[:, lo:hi, :]).then_inc(self.out[s], 16)

    def sync_end(self, sp):
        for s in range(len(SUBS)):
            sp.wait_ge(self.out[s], 16 * (STEPS + 1))

    def begin(self, v):
        v.memset(self.G[:, CW - 1, :], 0.0)
        v.drain().then_inc(self.summed, 4)

    def sub(self, v, n, s):
        lo, hi = SUBS[s]
        G, k = self.G, self.k
        v.wait_ge(self.rows[s], (n + 1) * 16 * (hi - lo))
        if self.weights is not None:
            g = G[:, lo:hi, 0:D].rearrange("p t (h d) -> p t h d", h=H)
            v.tensor_tensor(g, g, G[:, lo:hi, D:GW].unsqueeze(3).to_broadcast([P, hi - lo, H, DH]), ALU.mult)
            v.drain()
        for t in range(lo, hi):
            v.scalar_tensor_tensor(G[:, t, :], G[:, (t - 1) % CW, :], k.SAME[:, bass.ds(n * CW + t, 1)], G[:, t, :],
                                   ALU.mult, ALU.add)
            last = v.drain()
        last.then_inc(self.summed, 1)

    def end(self, v):
        v.tensor_copy(self.k.RLAST[:, 0:self.width], self.G[:, CW - 1, :])


def stage_layer0_mix(k, s0):
    nc, a = k.nc, k.a
    GROUPS = H * FC // 4
    HH = H // 2
    REST = NF - 512
    with k.scope() as s:
        RAW = s.sb("RAW", [P, B * H, DH])
        nrm = s.sb("nrm", [P, B * H])
        nsd = s.sb("nsd", [P, B * H])
        UW = s.sb("UW", [P, B * H, DH + 16])
        VV = s.sb("VV", [P, B * HH, V1])
        PHI = s.sb("PHI", [P, H, FW])
        PHT = s.sb("PHT", [128, H * FC, P])
        SPARE = PHT[:].rearrange("p q n -> p (q n)")[:, 0:HH * FW]
        KEYS = [PHI[:, 0:HH, :], PHI[:, HH:H, :], SPARE[0:P, :].rearrange("p (h f) -> p h f", h=HH)]
        SUMS = SPARE[0:V1, :]
        YS = s.sb("YS", [V1, H, P])
        YO = s.sb("YO", [P, 2, D])
        YT = s.sb("YT", [128, KC, P])
        rec = s.sb("rec", [P, H])
        G = s.sb("G", [P, CW, D])
        idx = s.sb("idx", [P, CW], I32)
        KVP = s.ps("KVP", [128, HH + 1, 512])
        PT = s.ps("PT", [128, 2, 512])
        PS, PY, PYT, PO = KVP[0:V1, 0:2, 0:4 * P], KVP[0:P, 2, :], KVP[:, 3, :], KVP[0:P, 4, :]
        sem = s.sem
        zeroed, norm_ready, root_ready = sem("zeroed"), sem("norm_ready"), sem("root_ready")
        phi_ready, phi_free, v_ready, v_free = sem("phi_ready"), sem("phi_free"), sem("v_ready"), sem("v_free")
        sums_ready, sums_kept, kv_turned, kv_ready = sem("sums_ready"), sem("sums_kept"), sem("kv_turned"), sem("kv_ready")
        pt_ready, pt_free, pht_ready, pht_free = sem("pt_ready"), sem("pt_free"), sem("pht_ready"), sem("pht_free")
        ys_summed, ys_ready, ys_free = sem("ys_summed"), sem("ys_ready"), sem("ys_free")
        y_ready, yo_ready = sem("y_ready"), sem("yo_ready")
        yt_turned, yt_ready, out_ready, out_free = sem("yt_turned"), sem("yt_ready"), sem("out_ready"), sem("out_free")
        edges = EdgeSums(k, s, k.sup, k.run0, G, idx)
        with nc.Block() as block:
            @block.gpsimd
            def _(pool):
                edges.pool(pool)

            @block.sync
            def _(sp):
                edges.sync_begin(sp)
                edges.sync_steps(sp, 0, STEPS)
                edges.sync_end(sp)

            @block.vector
            def _(v):
                def five(part, i, h0, nh):
                    lo = part * D + h0 * DH
                    return k.QKV[:, bass.ds(i * B, B), lo:lo + nh * DH]

                def bias(part, h0, nh):
                    lo = part * D + h0 * DH
                    return s0.bias[:, lo:lo + nh * DH]

                def scaled(part, i, h0, nh, item, at=0):
                    m = B * nh
                    raw, sq, nr = RAW[:, 0:m, :], UW[:, at:at + m, 0:DH], nrm[:, 0:m]
                    v.tensor_tensor(raw.rearrange("p (b h) d -> p b (h d)", b=B), five(part, i, h0, nh),
                                    bias(part, h0, nh).unsqueeze(1).to_broadcast([P, B, nh * DH]), ALU.add)
                    v.drain()
                    v.tensor_tensor(sq, raw, raw, ALU.mult)
                    v.drain()
                    v.tensor_reduce(nr, sq, AX.X, ALU.add).then_inc(norm_ready, 1)
                    v.wait_ge(root_ready, item + 1)
                    v.tensor_scalar(nr, nsd[:, 0:m], float(DH) ** 0.25 if part == 0 else 1.0, 1e-12, ALU.mult, ALU.max)
                    v.drain()
                    v.reciprocal(nr, nr)
                    v.drain()
                    if part == 0:
                        v.tensor_tensor(nr.rearrange("p (b h) -> p b h", b=B), nr.rearrange("p (b h) -> p b h", b=B),
                                        s0.fac[:].unsqueeze(1).to_broadcast([P, B, H]), ALU.mult)
                    else:
                        v.tensor_scalar(nr, nr, float(DH) ** 0.25, None, ALU.mult)
                    v.drain()
                    v.tensor_tensor(sq, raw, bcast(nr, DH), ALU.mult)
                    v.tensor_tensor(UW[:, at:at + m, DH:DH + 16], raw[:, :, 0:16], bcast(nr, 16), ALU.mult)
                    v.drain()

                v.memset(KVP[:], 0.0)
                v.memset(VV[:, :, 0:1], 1.0)

                def constant_features(PHI):
                    v.memset(PHI[:, :, NQ + DH:FW], 0.0)
                    v.drain()
                    v.memset(PHI[:, :, NF - 1:NF], 1.0)
                    v.drain()

                constant_features(PHI)
                v.sem_inc(zeroed, 1)
                edges.begin(v)
                def keys_scaled(j):
                    scaled(1, j % ITERS, j // ITERS * HH, HH, j, j % 2 * B * HH)

                keys_scaled(0)
                for half in range(2):
                    constant_features(KEYS[2])
                    for i in range(ITERS):
                        j = half * ITERS + i
                        for b in range(B):
                            n = j * B + b
                            v.wait_ge(phi_free, n + 1)
                            u = (j % 2 * B + b) * HH
                            features(v, UW[:, u:u + HH, :], KEYS[b % 3], phi_ready)
                            if b == 0:
                                v.wait_ge(v_free, j + 1)
                                v.tensor_tensor(VV[:, :, 1:V1].rearrange("p (b h) d -> p b h d", b=B),
                                                five(2, i, half * HH, HH).rearrange("p b (h d) -> p b h d", h=HH),
                                                bias(2, half * HH, HH).rearrange("p (h d) -> p h d", h=HH).unsqueeze(1)
                                                .to_broadcast([P, B, HH, DH]), ALU.add).then_inc(v_ready, 1)
                            if half == 0 and b < 4:
                                edges.sub(v, i, b)
                            if b == 2 and j + 1 < 2 * ITERS:
                                keys_scaled(j + 1)
                    v.wait_ge(sums_ready, half + 1)
                    v.memset(SUMS, 0.0)
                    v.drain()
                    sums = SUMS.rearrange("p (h f) -> p h f", h=HH)
                    v.tensor_copy(sums[:, :, 0:512], KVP[0:V1, 0:HH, :])
                    v.tensor_copy(sums[:, :, 512:NF], KVP[0:V1, HH, 0:HH * REST].rearrange("p (h f) -> p h f", h=HH))
                    v.drain()
                    v.memset(KVP[:], 0.0)
                    v.drain().then_inc(sums_kept, 1)
                    v.wait_ge(kv_turned, half + 1)
                    for q in range(2):
                        lo = (2 * half + q) * 2 * FC
                        v.tensor_tensor(s0.KV[:, lo:lo + 2 * FC, :], PT[:, q, 0:2 * FC * V1].rearrange("p (g e) -> p g e", e=V1),
                                        bcast(s0.second[:, lo:lo + 2 * FC], V1), ALU.mult)
                    v.drain().then_inc(kv_ready, 1)
                v.sem_inc(out_free, 1)

                def divide(i, b):
                    v.wait_ge(y_ready, i * B + b + 1)
                    y = PY[:, 0:H * V1].rearrange("p (h e) -> p h e", e=V1)
                    v.reciprocal(rec[:], y[:, :, 0])
                    v.drain()
                    v.tensor_tensor(YO[:, b % 2, :].rearrange("p (h d) -> p h d", h=H), y[:, :, 1:V1], bcast(rec[:], DH), ALU.mult
                                    ).then_inc(yo_ready, 1)

                def add(i, b):
                    n = i * B + b
                    v.wait_ge(out_ready, n + 1)
                    v.tensor_tensor(k.X[:, n, :], PO[:, 0:D], k.X[:, n, :], ALU.add).then_inc(out_free, 1)

                def query_tiles(i, first):
                    scaled(0, i, 0, H, 2 * ITERS + i)
                    e = 0
                    for b in range(B):
                        for half in range(2):
                            v.wait_ge(phi_free, 2 * (T + i * B + b) + half + 1)
                            features(v, UW[:, b * H + half * HH:b * H + (half + 1) * HH, :],
                                     PHI[:, half * HH:(half + 1) * HH, :], phi_ready)
                            if half and (b or not first):
                                divide(*((i, b - 1) if b else (i - 1, B - 1)))
                            if not half and (b > 1 or not first):
                                add(*((i, b - 2) if b > 1 else (i - 1, B + b - 2)))
                            for _ in range(2 if half or b == 0 else 1):
                                edges.sub(v, ITERS + 4 * i + e // 4, e % 4)
                                e += 1

                query_tiles(0, True)
                with v.Fori(1, ITERS) as i:
                    query_tiles(i, False)
                add(ITERS - 1, B - 2)
                divide(ITERS - 1, B - 1)
                add(ITERS - 1, B - 1)
                edges.end(v)

            @block.tensor
            def _(pe):
                pe.sem_inc(v_free, 1)
                pe.sem_inc(phi_free, 2)
                pe.sem_inc(pht_free, 1)
                pe.sem_inc(ys_free, 1)
                pe.wait_ge(zeroed, 1)
                for half in range(2):
                    with pe.Fori(0, ITERS) as i:
                        pe.wait_ge(v_ready, half * ITERS + i + 1)
                        for b in range(B):
                            pe.wait_ge(phi_ready, (half * ITERS + i) * B + b + 1)
                            for h in range(HH):
                                phi, values = KEYS[b % 3][:, h, :], VV[:, b * HH + h, :]
                                nc.tensor.matmul(KVP[0:V1, h, :], values, phi[:, 0:512],
                                                 start=False, stop=False, skip_group_check=True)
                                ins = nc.tensor.matmul(KVP[0:V1, HH, h * REST:(h + 1) * REST], values, phi[:, 512:NF],
                                                       start=False, stop=False, skip_group_check=True)
                            ins.then_inc(phi_free, 1)
                        pe.drain().then_inc(v_free, 1)
                    pe.drain().then_inc(sums_ready, 1)
                    pe.wait_ge(sums_kept, half + 1)
                    for q in range(HH * FC):
                        ins = nc.tensor.matmul(PT[:, q // 10, (q % 10) * V1:(q % 10 + 1) * V1], SUMS[:, q * 128:q * 128 + 128],
                                               k.IDENT[0:V1, 0:V1], start=True, stop=True)
                    ins.then_inc(kv_turned, 1)
                    pe.wait_ge(kv_ready, half + 1)

                def products(i, b, g):
                    pe.wait_ge(pht_ready, (i * B + b) * GROUPS + g + 1)
                    if g % 5 == 0:
                        pe.wait_ge(ys_ready, 2 * (i * B + b) + g // 5 + 1)
                    for q in range(4 * g, 4 * g + 4):
                        h, c = q // FC, q % FC
                        ins = nc.tensor.matmul(PS[:, h // 4, (h % 4) * P:(h % 4 + 1) * P], s0.KV[:, q, :], PHT[:, q, :],
                                               start=(c == 0), stop=(c == FC - 1))
                    if g % 5 == 4:
                        ins.then_inc(ys_summed, 1)

                def turn_back(i, b):
                    pe.wait_ge(ys_ready, 2 * (i * B + b) + 4)
                    for h in range(H):
                        ins = nc.tensor.matmul(PY[:, h * V1:(h + 1) * V1], YS[:, h, :], k.IDENT[0:V1, 0:V1], start=True, stop=True)
                    ins.then_inc(y_ready, 1)
                    pe.drain().then_inc(ys_free, 1)

                def turn(i, b):
                    pe.wait_ge(yo_ready, i * B + b + 1)
                    for c in range(KC):
                        ins = nc.tensor.transpose(PYT[:, c * P:c * P + P], YO[:, b % 2, c * 128:c * 128 + 128],
                                                  k.IDENT[0:P, 0:P])
                    ins.then_inc(yt_turned, 1)

                def project(i, b):
                    n = i * B + b
                    pe.wait_ge(yt_ready, n + 1)
                    pe.wait_ge(out_free, n + 1)
                    for c in range(KC):
                        ins = nc.tensor.matmul(PO[:, 0:D], YT[:, c, :], s0.WPT[:, c, :], start=(c == 0), stop=(c == KC - 1))
                    ins.then_inc(out_ready, 1)

                def query_tiles(i, first):
                    for b in range(B):
                        n = i * B + b
                        before = (i, b - 1) if b else (i - 1, B - 1)
                        for g in range(GROUPS):
                            if g % 5 == 0:
                                pe.wait_ge(phi_ready, 2 * (T + n) + g // 5 + 1)
                            pe.wait_ge(pt_free, n * GROUPS + g + 1)
                            for q in range(4):
                                h, c = (4 * g + q) // FC, (4 * g + q) % FC
                                ins = nc.tensor.transpose(PT[:, g % 2, q * P:q * P + P], PHI[:, h, c * 128:c * 128 + 128],
                                                          k.IDENT[0:P, 0:P])
                            ins.then_inc(pt_ready, 1)
                            if g % 5 == 4:
                                pe.drain().then_inc(phi_free, 1)
                            if g:
                                products(i, b, g - 1)
                            if b or not first:
                                if g == 2:
                                    turn_back(*before)
                                if g == 5:
                                    turn(*before)
                                if g == 8:
                                    project(*before)
                        products(i, b, GROUPS - 1)
                        pe.drain().then_inc(pht_free, 1)

                query_tiles(0, True)
                with pe.Fori(1, ITERS) as i:
                    query_tiles(i, False)
                last = (ITERS - 1, B - 1)
                turn_back(*last)
                turn(*last)
                project(*last)

            @block.scalar
            def _(act):
                act.sem_inc(pt_free, 2)
                act.sem_inc(ys_ready, 2)
                with act.Fori(0, 2 * ITERS) as i:
                    act.wait_ge(norm_ready, i + 1)
                    nc.scalar.activation(nsd[:, 0:B * HH], nrm[:, 0:B * HH], ACT.Sqrt).then_inc(root_ready, 1)

                def keep_sums(i, b, half):
                    act.wait_ge(ys_summed, 2 * (i * B + b) + half + 1)
                    if half == 0:
                        act.wait_ge(ys_free, i * B + b + 1)
                    nc.scalar.activation(YS[:, half * 4:half * 4 + 4, :], PS[:, half, :].rearrange("p (h n) -> p h n", h=4),
                                         ACT.Copy).then_inc(ys_ready, 1)

                def keep_y(i, b):
                    act.wait_ge(yt_turned, i * B + b + 1)
                    nc.scalar.activation(YT[:], PYT[:, 0:KC * P].rearrange("p (c n) -> p c n", c=KC), ACT.Copy
                                         ).then_inc(yt_ready, 1)

                def query_tiles(i, first):
                    act.wait_ge(norm_ready, 2 * ITERS + i + 1)
                    nc.scalar.activation(nsd[:], nrm[:], ACT.Sqrt).then_inc(root_ready, 1)
                    for b in range(B):
                        n = i * B + b
                        before = (i, b - 1) if b else (i - 1, B - 1)
                        act.wait_ge(pht_free, n + 1)
                        for g in range(GROUPS):
                            act.wait_ge(pt_ready, n * GROUPS + g + 1)
                            nc.scalar.activation(PHT[:, 4 * g:4 * g + 4, :],
                                                 PT[:, g % 2, 0:4 * P].rearrange("p (q n) -> p q n", n=P), ACT.Copy
                                                 ).then_inc(pht_ready, 1)
                            act.drain().then_inc(pt_free, 1)
                            if g == 0 and (b or not first):
                                keep_sums(*before, 1)
                            if g == 6:
                                keep_sums(i, b, 0)
                            if g == 6 and (b or not first):
                                keep_y(*before)

                query_tiles(0, True)
                with act.Fori(1, ITERS) as i:
                    query_tiles(i, False)
                keep_sums(ITERS - 1, B - 1, 1)
                keep_y(ITERS - 1, B - 1)


def open_nodes(v, k, out, base, n):
    return v.tensor_scalar(out, base, k.OPEN[:, bass.ds(n, 1)], None, ALU.is_equal)


def stage_layer0_nodes(k, s0):
    nc, a = k.nc, k.a
    with k.scope() as s:
        base = s.sb("base", [P, P])
        G = k.QKV[:, :, 0:D]
        GM = s.sb("GM", [P, B, P])
        bias = s.sb("bias", [P, D])
        PS = s.ps("PS", [P, 8, 512])
        sem = s.sem
        loaded, open_ready, sums_ready, sums_used = (sem(x) for x in ("loaded", "open_ready", "sums_ready", "sums_used"))
        rows = [s.gather_sem(f"rows{i}") for i in range(ITERS)]
        with nc.Block() as block:
            @block.sync
            def _(sp):
                sp.dma_start(base[:], a["c_base"]).then_inc(loaded, 16)
                sp.wait_ge(loaded, 16)

            @block.gpsimd
            def _(pool):
                for n in range(T):
                    nc.gpsimd.indirect_dma_start(out=G[:, n, :], out_offset=None, in_=k.run0,
                                                 in_offset=bass.IndirectOffsetOnAxis(ap=k.LAST[:, n:n + 1], axis=0)
                                                 ).then_inc(rows[n // B], 16)

            @block.tensor
            def _(pe):
                with pe.Fori(0, ITERS) as i:
                    for b in range(B):
                        pe.wait_ge(open_ready, i * B + b + 1)
                        pe.wait_ge(sums_used, i * B + b + 1)
                        nc.tensor.matmul(PS[:, b, 0:D], GM[:, b, :], k.RLAST[:, 0:D], start=True, stop=True
                                         ).then_inc(sums_ready, 1)

            @block.vector
            def _(v):
                v.wait_ge(loaded, 16)
                v.sem_inc(sums_used, B)
                v.tensor_tensor(bias[:], s0.bsum[:, 0, :], s0.bsum[:, 1, :], ALU.add)
                for i in range(ITERS):
                    v.drain()
                    for b in range(B):
                        open_nodes(v, k, GM[:, b, :], base[:], i * B + b).then_inc(open_ready, 1)
                    x = k.X[:, i * B:(i + 1) * B, :]
                    v.tensor_tensor(x, x, bias[:].unsqueeze(1).to_broadcast([P, B, D]), ALU.add)
                    v.wait_ge(rows[i], 16 * B)
                    v.wait_ge(sums_ready, (i + 1) * B)
                    for b in range(B):
                        v.tensor_tensor(G[:, i * B + b, :], G[:, i * B + b, :], PS[:, b, 0:D], ALU.add)
                    v.drain().then_inc(sums_used, B)
                    for b in range(B):
                        n = i * B + b
                        v.scalar_tensor_tensor(k.X[:, n, :], G[:, n, :], k.HAS[:, n:n + 1], k.X[:, n, :], ALU.mult, ALU.add)



def stage_normalise(k, eps, XNT=None, ranked=None, XN=None, tables=None, W=None, KEPT=None, beside=None):
    nc, a = k.nc, k.a
    with k.scope() as s:
        s.stat = s.sb("stat", [P, B, 6])
        s.mv = s.sb("mv", [P, B, 2])
        XS = s.sb("XS", [P, B, D])
        XT = s.sb("XT", [128, B, KC, P])
        PT = s.ps("PT", [128, 3, 512])
        nt = len(tables or ())
        if tables:
            kept = D * sum(table is None for _, table in tables)
            stored_tables = [table for _, table in tables if table is not None]
            ns = len(stored_tables)
            load_w = W is None
            W = s.sb("W", [128, KC, nt * D]) if load_w else W
            OUT = s.sb("OUT", [P, B, ns * D])
            PR = s.ps("PR", [P, 2, 512])
        if ranked:
            wr = s.sb("wr", [P, D])
            br = s.sb("br", [P, 1])
            prod = s.sb("prod", [P, D])
            w5 = s.sb("w5", [P, B])

        def pt(b):
            return PT[:, b % 3, 0:KC * P].rearrange("p (c n) -> p c n", c=KC)

        sem = s.sem
        loaded, var_ready, sd_ready = sem("loaded"), sem("var_ready"), sem("sd_ready")
        rows_ready, rows_free, rows_kept = sem("rows_ready"), sem("rows_free"), sem("rows_kept")
        turned_ready, turned_free = sem("turned_ready"), sem("turned_free")
        xt_ready, xt_free = sem("xt_ready"), sem("xt_free")
        proj_ready, pr_free = sem("proj_ready"), [sem("pr_free0"), sem("pr_free1")]
        out_ready, stored = sem("out_ready"), [sem(f"stored{b}") for b in range(B)]
        weights_ready = sem("weights_ready")
        nload = 16 * ((nt if tables and load_w else 0) + (2 if ranked else 0))
        with nc.Block() as block:
            @block.sync
            def _(sp):
                for m, (w, _) in enumerate(tables if tables and load_w else ()):
                    sp.dma_start(W[:, :, m * D:(m + 1) * D], chunks(w)).then_inc(loaded, 16)
                if ranked:
                    sp.dma_start(wr[:], row(a["L0_ffn_wr"].rearrange("d o -> (d o)"), P)).then_inc(loaded, 16)
                    sp.dma_start(br[:], row(a["L0_ffn_br"], P)).then_inc(loaded, 16)
                if tables:
                    for b in range(B):
                        sp.sem_inc(stored[b], 16)
                    with sp.Fori(0, ITERS) as i:
                        for b in range(B):
                            n = i * B + b
                            sp.wait_ge(out_ready, n + 1)
                            for m, table in enumerate(stored_tables):
                                sp.dma_start(node_rows(table)[:, n, :], OUT[:, b, m * D:(m + 1) * D]).then_inc(stored[b], 16)
                    for b in range(B):
                        sp.wait_ge(stored[b], 16 * (ns * ITERS + 1))
                if ranked:
                    sp.wait_ge(weights_ready, 1)
                    sp.dma_start(k.weights.rearrange("(p t) d -> p (t d)", p=P), ranked.selw[:]).then_inc(loaded, 16)
                    sp.wait_ge(loaded, nload + 16)

            @block.vector
            def _(v):
                if beside is not None:
                    beside.prepare(v)
                node_stats(k, s, eps, var_ready, sd_ready)
                if ranked:
                    v.wait_ge(loaded, nload)
                with v.Fori(0, ITERS) as i:
                    for b in range(B):
                        n = i * B + b
                        v.wait_ge(rows_free, n + 1)
                        v.wait_ge(rows_kept, n + 1)
                        v.tensor_scalar(XS[:, b, :], k.X[:, n, :], k.MV[:, n, 0:1], k.RSTD[:, bass.ds(n, 1)],
                                        ALU.subtract, ALU.mult).then_inc(rows_ready, 1)
                        if ranked:
                            v.drain()
                            v.tensor_tensor_reduce(prod[:], XS[:, b, :], wr[:], 1.0, 0.0, ALU.mult, ALU.add,
                                                   w5[:, b:b + 1])
                    if ranked:
                        v.drain()
                        v.tensor_scalar(ranked.selw[:, bass.ds(i * B, B)], w5[:], br[:, 0:1], None, ALU.add)
                        v.drain()
                    if beside is not None:
                        beside.item(v, i)
                if ranked:
                    v.drain().then_inc(weights_ready, 1)
                if beside is not None:
                    beside.finish(v)

            @block.tensor
            def _(pe):
                pe.sem_inc(rows_free, B)
                pe.sem_inc(xt_free, B)
                if nload:
                    pe.wait_ge(loaded, nload)
                with pe.Fori(0, ITERS) as i:
                    for b in range(B):
                        n = i * B + b
                        pe.wait_ge(rows_ready, n + 1)
                        pe.wait_ge(turned_free, n + 1)
                        for c in range(KC):
                            ins = nc.tensor.transpose(pt(b)[:, c, :], XS[:, b, c * 128:c * 128 + 128], k.IDENT[0:P, 0:P])
                        ins.then_inc(turned_ready, 1)
                    for b in range(B if tables else 0):
                        n = i * B + b
                        pe.wait_ge(xt_ready, n + 1)
                        for half in range(2):
                            lo, hi = half * 512, min(half * 512 + 512, nt * D)
                            pe.wait_ge(pr_free[half], n + 1)
                            for c in range(KC):
                                ins = nc.tensor.matmul(PR[:, half, 0:hi - lo], XT[:, b, c, :], W[:, c, lo:hi],
                                                       start=(c == 0), stop=(c == KC - 1))
                            ins.then_inc(proj_ready, 1)
                        pe.drain().then_inc(xt_free, 1)

            @block.scalar
            def _(act):
                act.sem_inc(turned_free, 2)
                if tables:
                    act.sem_inc(pr_free[0], 1)
                    act.sem_inc(pr_free[1], 1)
                act.wait_ge(var_ready, 1)
                nc.scalar.activation(k.SD[:], k.RSTD[:], ACT.Sqrt).then_inc(sd_ready, 1)
                with act.Fori(0, ITERS) as i:
                    for b in range(B):
                        n = i * B + b
                        act.wait_ge(turned_ready, n + 1)
                        if tables:
                            act.wait_ge(xt_free, n + 1)
                            nc.scalar.activation(XT[:, b, :, :], pt(b), ACT.Copy).then_inc(xt_ready, 1)
                        if XNT is not None:
                            nc.scalar.activation(XNT[:, :, bass.ds(n * P, P)], pt(b), ACT.Copy)
                        act.sem_inc(rows_free, 1)
                        act.drain().then_inc(turned_free, 1)
                    for b in range(B if tables else 0):
                        n = i * B + b
                        act.wait_ge(stored[b], 16 * (ns * i + 1))
                        for half in range(2):
                            lo, hi = half * 512, min(half * 512 + 512, nt * D)
                            act.wait_ge(proj_ready, 2 * n + half + 1)
                            if lo < kept:
                                m = min(hi, kept)
                                ins = nc.scalar.activation(KEPT[:, n, lo:m], PR[:, half, 0:m - lo], ACT.Copy)
                            if hi > kept:
                                m = max(lo, kept)
                                ins = nc.scalar.activation(OUT[:, b, m - kept:hi - kept], PR[:, half, m - lo:hi - lo], ACT.Copy)
                            ins.then_inc(pr_free[half], 1)
                        act.drain().then_inc(out_ready, 1)

            @block.gpsimd
            def _(pool):
                pool.sem_inc(rows_kept, B)
                if XN is not None:
                    nc.gpsimd.memset(XN[:, :, D:D + 1], 1.0)
                if XN is not None or ranked:
                    with pool.Fori(0, ITERS) as i:
                        for b in range(B):
                            n = i * B + b
                            pool.wait_ge(rows_ready, n + 1)
                            if ranked:
                                nc.gpsimd.tensor_tensor(k.X[:, n, :], k.X[:, n, :], XS[:, b, :], ALU.add).then_inc(rows_kept, 1)
                            else:
                                nc.gpsimd.tensor_copy(XN[:, n, 0:D], XS[:, b, :]).then_inc(rows_kept, 1)
                else:
                    pool.sem_inc(rows_kept, T)
                if beside is not None:
                    beside.pool(pool)


KEEP = int(0.5 * N) - 1


class Selection:

    def __init__(self, k, f, s, PS):
        self.k, self.f, self.PS = k, f, PS
        self.wrow = s.sb("wrow", [P, N])
        self.scratch = s.sb("scratch", [P, N])
        self.gt, self.ge, self.tie, self.ones, self.upto = (s.sb(x, [P, T]) for x in ("gt", "ge", "tie", "ones", "upto"))
        self.after = s.sb("after", [P, P])
        self.loaded, self.ties_ready, self.before_ready = s.sem("ranks_loaded"), s.sem("ties_ready"), s.sem("before_ready")

    def sync(self, sp):
        sp.dma_start(self.wrow[:], row(self.k.weights.rearrange("n d -> (n d)"), P)).then_inc(self.loaded, 16)
        sp.dma_start(self.after[:], self.k.a["c_after"]).then_inc(self.loaded, 16)

    def vector(self, v):
        gt, ge, tie, upto, selw = self.gt, self.ge, self.tie, self.upto, self.f.selw
        v.memset(self.ones[:], 1.0)
        v.wait_ge(self.loaded, 32)
        for out, op in ((gt, ALU.is_gt), (ge, ALU.is_ge)):
            for n in range(T):
                v.drain()
                v.tensor_scalar(self.scratch[:], self.wrow[:], selw[:, n:n + 1], 0.0, op, ALU.add,
                                accum_out=out[:, n:n + 1])
        v.drain()
        v.tensor_scalar(tie[:], gt[:], float(KEEP), None, ALU.is_lt)
        v.drain()
        v.scalar_tensor_tensor(tie[:], ge[:], float(KEEP), tie[:], ALU.is_gt, ALU.mult)
        v.drain()
        v.tensor_tensor_scan(upto[:], self.ones[:], tie[:], 0.0, ALU.mult, ALU.add).then_inc(self.ties_ready, 1)
        v.wait_ge(self.before_ready, 1)
        v.tensor_tensor(upto[:], upto[:], tie[:], ALU.subtract)
        v.drain()
        v.tensor_scalar(upto[:], upto[:], self.PS[:, 0:1], None, ALU.add)
        v.drain()
        v.tensor_tensor(upto[:], upto[:], tie[:], ALU.mult)
        v.drain()
        v.tensor_tensor(gt[:], gt[:], upto[:], ALU.add)
        v.drain()
        v.scalar_tensor_tensor(selw[:], gt[:], float(KEEP), selw[:], ALU.is_lt, ALU.mult)
        v.drain()

    def tensor(self, pe):
        pe.wait_ge(self.ties_ready, 1)
        self.k.nc.tensor.matmul(self.PS[:, 0:1], self.after[:], self.upto[:, T - 1:T], start=True, stop=True
                                ).then_inc(self.before_ready, 1)


PIECES = ((0, 3 * P), (3 * P, B * P))


def stage_layer0_ffn(k, f, XNT):
    nc, a = k.nc, k.a
    with k.scope() as s:
        W1 = s.sb("W1", [128, KC, HID])
        W2 = s.sb("W2", [128, HC, D])
        b1 = s.sb("b1", [128, HC])
        b2 = s.sb("b2", [P, D])
        HT = s.sb("HT", [128, HC, B * P])
        Y = s.sb("Y", [P, T, D])
        HP = s.ps("HP", [128, 4, 512])
        YP = s.ps("YP", [P, 3, 512])
        PS = s.ps("PS", [P, 512])
        selection = Selection(k, f, s, PS)
        sem = s.sem
        loaded, h_ready, h_free, ht_ready, ht_free, y_ready, y_free, y_kept, go, y_biased = (sem(x) for x in (
            "loaded", "h_ready", "h_free", "ht_ready", "ht_free", "y_ready", "y_free", "y_kept", "go", "y_biased"))
        with nc.Block() as block:
            @block.sync
            def _(sp):
                selection.sync(sp)
                sp.dma_start(W1[:], chunks(a["L0_ffn_w1"])).then_inc(loaded, 16)
                sp.dma_start(W2[:], chunks(a["L0_ffn_w2"])).then_inc(loaded, 16)
                sp.dma_start(b1[:], a["L0_ffn_b1"].rearrange("(c p) -> p c", p=128), allow_slow_non_contiguous=True).then_inc(loaded, 16)
                sp.dma_start(b2[:], row(a["L0_ffn_b2"], P)).then_inc(loaded, 16)
                sp.wait_ge(loaded, 64)

            @block.tensor
            def _(pe):
                pe.sem_inc(ht_free, 1)
                pe.wait_ge(loaded, 64)
                with pe.Fori(0, ITERS) as i:
                    for c in range(HC):
                        for q, (lo, hi) in enumerate(PIECES):
                            m = 2 * c + q
                            pe.wait_ge(h_free, i * 2 * HC + m + 1)
                            for kc in range(KC):
                                ins = nc.tensor.matmul(HP[:, m % 4, 0:hi - lo], W1[:, kc, c * 128:c * 128 + 128],
                                                       XNT[:, kc, bass.ds(i * B * P + lo, hi - lo)],
                                                       start=(kc == 0), stop=(kc == KC - 1))
                            ins.then_inc(h_ready, 1)
                    pe.wait_ge(ht_ready, (i + 1) * 2 * HC)
                    for b in range(B):
                        pe.wait_ge(y_free, i * B + b + 1)
                        for c in range(HC):
                            ins = nc.tensor.matmul(YP[:, b % 3, 0:D], HT[:, c, b * P:b * P + P], W2[:, c, :],
                                                   start=(c == 0), stop=(c == HC - 1))
                        ins.then_inc(y_ready, 1)
                    pe.drain().then_inc(ht_free, 1)
                selection.tensor(pe)

            @block.scalar
            def _(act):
                act.sem_inc(h_free, 4)
                act.sem_inc(y_free, 2)
                act.wait_ge(loaded, 64)
                with act.Fori(0, ITERS) as i:
                    act.wait_ge(ht_free, i + 1)
                    for c in range(HC):
                        for q, (lo, hi) in enumerate(PIECES):
                            m = 2 * c + q
                            act.wait_ge(h_ready, i * 2 * HC + m + 1)
                            nc.scalar.activation(HT[:, c, lo:hi], HP[:, m % 4, 0:hi - lo], ACT.Gelu_apprx_tanh,
                                                 bias=b1[:, c:c + 1]).then_inc(h_free, 1)
                    act.drain().then_inc(ht_ready, 2 * HC)
                    for b in range(B):
                        act.wait_ge(y_ready, i * B + b + 1)
                        nc.scalar.activation(Y[:, i * B + b, :], YP[:, b % 3, 0:D], ACT.Copy).then_inc(y_free, 1)
                    act.drain().then_inc(y_kept, 1)

            @block.gpsimd
            def _(pool):
                pool.wait_ge(loaded, 64)
                with pool.Fori(0, ITERS) as i:
                    rows = Y[:, bass.ds(i * B, B), :]
                    pool.wait_ge(y_kept, i + 1)
                    pool.sem_inc(go, 1)
                    nc.gpsimd.tensor_tensor(rows, rows, b2[:].unsqueeze(1).to_broadcast([P, B, D]), ALU.add).then_inc(y_biased, 1)

            @block.vector
            def _(v):
                selection.vector(v)
                with v.Fori(0, ITERS) as i:
                    v.wait_ge(y_biased, i + 1)
                    for b in range(B):
                        n = i * B + b
                        v.scalar_tensor_tensor(k.X[:, n, :], Y[:, n, :], f.selw[:, bass.ds(n, 1)], k.X[:, n, :],
                                               ALU.mult, ALU.add)


NE = 8
SLOTS = T + NE - 1
SG = 4
SP_COLS = SG * P


def stage_gate(k, r, XNT, XN):
    nc, a = k.nc, k.a
    with k.scope() as s:
        W1 = s.sb("W1", [128, KC, HID])
        zeros = s.sb("zeros", [P, SG, D])
        WG = s.sb("WG", [128, HC, NE])
        bg = s.sb("bg", [P, NE])
        rev = s.sb("rev", [P, NE])
        after = s.sb("after", [P, P])
        route = s.sb("route", [128, T + SLOTS + 1])
        HT = s.sb("HT", [128, 4, B * P])
        LS = s.sb("LS", [NE, B * P])
        ones = s.sb("ones", [P, 128])
        lg = s.sb("lg", [P, T, NE])
        key = s.sb("key", [P, T, NE])
        run = s.sb("run", [P, T, NE])
        one = s.sb("one", [P, T])
        cnt = s.sb("cnt", [P, NE])
        base = s.sb("base", [P, NE])
        total = s.sb("total", [128, NE])
        tiles = s.sb("tiles", [128, NE])
        end = s.sb("end", [128, NE])
        more = s.sb("more", [128, NE, T])
        past = s.sb("past", [128, SLOTS, NE - 1])
        es = s.sb("es", [128, SLOTS])
        HP = s.ps("HP", [128, 4, 512])
        LP = s.ps("LP", [NE, 2, 512])
        LT = s.ps("LT", [P, 512])
        PS = s.ps("PS", [128, 512])
        sem = s.sem
        (loaded, w_ready, zeroed, cleared, h_ready, h_free, ht_ready, ht_free, l_ready, l_kept, lg_ready, shifted, exp_ready,
         counted, spread, placed, go) = (sem(x) for x in (
             "loaded", "w_ready", "zeroed", "cleared", "h_ready", "h_free", "ht_ready", "ht_free", "l_ready", "l_kept", "lg_ready",
             "shifted", "exp_ready", "counted", "spread", "placed", "go"))
        scattered = s.gather_sem("scattered")
        NL = 16 * 7
        with nc.Block() as block:
            @block.sync
            def _(sp):
                sp.dma_start(W1[:], chunks(a["L1_ffn_W1"])).then_inc(loaded, 16)
                sp.dma_start(r.b1[:], a["L1_ffn_b1"].rearrange("(p c) -> p c", c=HC)).then_inc(loaded, 16)
                sp.dma_start(WG[:], a["L1_ffn_Wg"].rearrange("(p c) e -> p c e", c=HC)).then_inc(loaded, 16)
                sp.dma_start(bg[:], row(a["L1_ffn_bg"], P)).then_inc(loaded, 16)
                sp.dma_start(rev[:], a["c_reversed"]).then_inc(loaded, 16)
                sp.dma_start(after[:], a["c_after"]).then_inc(loaded, 16)
                sp.dma_start(route[:], a["c_route"]).then_inc(loaded, 16)
                sp.wait_ge(zeroed, 1)
                for g in range(SLOTS // SG):
                    sp.dma_start(k.by_expert.rearrange("(p s) d -> p s d", p=P)[:, g * SG:(g + 1) * SG, :], zeros[:]
                                 ).then_inc(cleared, 16)
                sp.wait_ge(loaded, NL)
                sp.wait_ge(cleared, 16 * (SLOTS // SG))

            @block.gpsimd
            def _(pool):
                pool.wait_ge(cleared, 16 * (SLOTS // SG))
                pool.wait_ge(placed, 1)
                pool.sem_inc(go, 1)
                for n in range(T):
                    nc.gpsimd.indirect_dma_start(out=k.by_expert, out_offset=bass.IndirectOffsetOnAxis(ap=r.pos[:, n:n + 1], axis=0),
                                                 in_=XN[:, n, 0:D], in_offset=None).then_inc(scattered, 16)
                pool.wait_ge(scattered, 16 * T)

            @block.tensor
            def _(pe):
                pe.wait_ge(w_ready, 1)

                def gate(i, c):
                    pe.wait_ge(ht_ready, i * HC + c + 1)
                    for q, (lo, hi) in enumerate(PIECES):
                        ins = nc.tensor.matmul(LP[:, q, 0:hi - lo], WG[:, c, :], HT[:, c % 4, lo:hi],
                                               start=(c == 0), stop=(c == HC - 1))
                    if c == HC - 1:
                        ins.then_inc(l_ready, 1)
                    pe.drain().then_inc(ht_free, 1)

                with pe.Fori(0, ITERS) as i:
                    for c in range(HC):
                        for q, (lo, hi) in enumerate(PIECES):
                            pe.wait_ge(h_free, i * 2 * HC + 2 * c + q + 1)
                            for kc in range(KC):
                                ins = nc.tensor.matmul(HP[:, (2 * c + q) % 4, 0:hi - lo], r.W1[:, kc, c, :],
                                                       XNT[:, kc, bass.ds(i * B * P + lo, hi - lo)],
                                                       start=(kc == 0), stop=(kc == KC - 1))
                            ins.then_inc(h_ready, 1)
                        if c >= 2:
                            gate(i, c - 2)
                    gate(i, HC - 2)
                    gate(i, HC - 1)
                    pe.wait_ge(l_kept, i + 1)
                    for b in range(B):
                        ins = nc.tensor.matmul(LT[:, bass.ds((i * B + b) * NE, NE)], LS[:, b * P:b * P + P],
                                               k.IDENT[0:NE, 0:NE], start=True, stop=True)
                    ins.then_inc(lg_ready, 1)
                pe.wait_ge(counted, 1)
                nc.tensor.matmul(PS[:, 0:NE], ones[:], cnt[:], start=True, stop=True)
                nc.tensor.matmul(PS[0:P, NE:2 * NE], after[:], cnt[:], start=True, stop=True).then_inc(spread, 1)

            @block.scalar
            def _(act):
                act.sem_inc(h_free, 4)
                act.sem_inc(ht_free, 4)
                act.wait_ge(loaded, NL)
                with act.Fori(0, ITERS) as i:
                    for c in range(HC):
                        act.wait_ge(ht_free, i * HC + c + 1)
                        for q, (lo, hi) in enumerate(PIECES):
                            act.wait_ge(h_ready, i * 2 * HC + 2 * c + q + 1)
                            nc.scalar.activation(HT[:, c % 4, lo:hi], HP[:, (2 * c + q) % 4, 0:hi - lo], ACT.Gelu,
                                                 bias=r.b1[:, c:c + 1]).then_inc(h_free, 1)
                        act.drain().then_inc(ht_ready, 1)
                    act.wait_ge(l_ready, i + 1)
                    for q, (lo, hi) in enumerate(PIECES):
                        ins = nc.scalar.activation(LS[:, lo:hi], LP[:, q, 0:hi - lo], ACT.Copy)
                    ins.then_inc(l_kept, 1)
                act.wait_ge(shifted, 1)
                nc.scalar.activation(lg[:], lg[:], ACT.Exp).then_inc(exp_ready, 1)

            @block.vector
            def _(v):
                v.memset(zeros[:], 0.0).then_inc(zeroed, 1)
                v.memset(ones[:], 1.0)
                v.wait_ge(loaded, NL)
                for kc in range(KC):
                    v.tensor_copy(r.W1[:, kc, :, :], W1[:, kc, :].rearrange("p (m c) -> p c m", c=HC))
                v.drain().then_inc(w_ready, 1)
                v.wait_ge(lg_ready, ITERS)
                v.tensor_tensor(lg[:], LT[:, 0:T * NE].rearrange("p (t e) -> p t e", e=NE),
                                bg[:].unsqueeze(1).to_broadcast([P, T, NE]), ALU.add)
                v.drain()
                v.tensor_reduce(one[:], lg[:], AX.X, ALU.max)
                v.drain()
                v.tensor_tensor(lg[:], lg[:], bcast(one[:], NE), ALU.subtract).then_inc(shifted, 1)
                v.wait_ge(exp_ready, 1)
                v.tensor_reduce(one[:], lg[:], AX.X, ALU.add)
                v.drain()
                v.reciprocal(one[:], one[:])
                v.drain()
                v.tensor_tensor(lg[:], lg[:], bcast(one[:], NE), ALU.mult)
                v.drain()
                v.tensor_reduce(r.prob[:], lg[:], AX.X, ALU.max)
                v.drain()
                v.tensor_tensor(key[:], lg[:], bcast(r.prob[:], NE), ALU.is_equal)
                v.drain()
                v.tensor_tensor(key[:], key[:], rev[:].unsqueeze(1).to_broadcast([P, T, NE]), ALU.mult)
                v.drain()
                v.tensor_reduce(one[:], key[:], AX.X, ALU.max)
                v.drain()
                v.tensor_tensor(key[:], key[:], bcast(one[:], NE), ALU.is_equal)
                v.drain()
                v.tensor_reduce(cnt[:], key[:].rearrange("p t e -> p e t"), AX.X, ALU.add).then_inc(counted, 1)
                for e in range(NE):
                    v.tensor_tensor_scan(run[:, :, e], ones[:, 0:T], key[:, :, e], 0.0, ALU.mult, ALU.add)
                v.wait_ge(spread, 1)
                v.tensor_copy(total[:], PS[:, 0:NE])
                v.tensor_copy(base[:], PS[0:P, NE:2 * NE])
                v.drain()
                v.tensor_tensor(more[:], bcast(total[:], T), route[:, 0:T].unsqueeze(1).to_broadcast([128, NE, T]), ALU.is_gt)
                v.drain()
                v.tensor_reduce(tiles[:], more[:], AX.X, ALU.add)
                v.memset(es[:], 1.0)
                v.drain()
                v.tensor_tensor_scan(end[:], es[:, 0:NE], tiles[:], 0.0, ALU.mult, ALU.add)
                v.drain()
                v.tensor_tensor(tiles[:], end[:], tiles[:], ALU.subtract)
                v.drain()
                v.scalar_tensor_tensor(base[:], tiles[0:P, :], float(P), base[:], ALU.mult, ALU.add)
                v.drain()
                v.tensor_tensor(run[:], run[:], base[:].unsqueeze(1).to_broadcast([P, T, NE]), ALU.add)
                v.drain()
                v.tensor_tensor(run[:], run[:], key[:], ALU.mult)
                v.drain()
                v.tensor_reduce(one[:], run[:], AX.X, ALU.add)
                v.drain()
                v.tensor_scalar(one[:], one[:], -1.0, None, ALU.add)
                v.drain()
                v.tensor_copy(r.pos[:], one[:])
                v.drain().then_inc(placed, 1)
                v.tensor_tensor(past[:], bcast(route[:, T:T + SLOTS], NE - 1),
                                end[:, 0:NE - 1].unsqueeze(1).to_broadcast([128, SLOTS, NE - 1]), ALU.is_ge)
                v.drain()
                v.tensor_reduce(es[:], past[:], AX.X, ALU.add)
                v.drain()
                v.tensor_copy(r.bias_row[:], es[0:P, :])
                v.drain()
                v.tensor_scalar(es[:], es[:], 128.0, route[:, T + SLOTS:T + SLOTS + 1], ALU.mult, ALU.add)
                v.drain()
                v.tensor_copy(r.weight_row[:], es[:])


def stage_experts(k, r):
    nc, a = k.nc, k.a
    GS = SLOTS // SG
    with k.scope() as s:
        XR = s.sb("XR", [P, SG, D])
        XT = s.sb("XT", [128, KC, SG, P])
        HT = s.sb("HT", [128, HC, SP_COLS])
        WE = s.sb("WE", [128, SG, HC * D])
        BE = s.sb("BE", [P, SG, D])
        Y = s.sb("Y", [P, SG, D])
        wi = s.sb("wi", [128, SG], I32)
        bi = s.sb("bi", [P, SG], I32)
        PT = s.ps("PT", [128, 2, 512])
        HP = s.ps("HP", [128, 3, 512])
        YP = s.ps("YP", [P, 2, 512])
        sem = s.sem
        (row_load, rows_free, turned, xt_ready, xt_free, h_ready, h_free, ht_ready, ht_free, y_ready, y_free, y_kept, w_free,
         staged, go) = (sem(x) for x in (
             "row_load", "rows_free", "turned", "xt_ready", "xt_free", "h_ready", "h_free", "ht_ready", "ht_free", "y_ready",
             "y_free", "y_kept", "w_free", "staged", "go"))
        stored = [sem(f"stored{b}") for b in range(SG)]
        weights = [s.gather_sem(f"weights{b}") for b in range(SG)]
        slot_rows = k.by_expert.rearrange("(s p) d -> p s d", p=P)
        slot_out = k.expert_out.rearrange("(s p) d -> p s d", p=P)
        with nc.Block() as block:
            @block.sync
            def _(sp):
                with sp.Fori(0, GS) as g:
                    sp.wait_ge(rows_free, g + 1)
                    sp.dma_start(XR[:], slot_rows[:, bass.ds(g * SG, SG), :]).then_inc(row_load, 16)
                sp.wait_ge(row_load, 16 * GS)

            @block.scalar
            def _(act):
                act.sem_inc(h_free, 3)

                def keep_turned(g):
                    act.wait_ge(turned, g + 1)
                    act.wait_ge(xt_free, g + 1)
                    for q in range(2):
                        ins = nc.scalar.activation(XT[:, :, 2 * q:2 * q + 2, :],
                                                   PT[:, q, 0:4 * P].rearrange("p (b c n) -> p c b n", b=2, c=KC), ACT.Copy)
                    ins.then_inc(xt_ready, 1)

                keep_turned(0)

                def hidden(g):
                    act.wait_ge(ht_free, g + 1)
                    for c in range(HC):
                        act.wait_ge(h_ready, g * HC + c + 1)
                        nc.scalar.activation(HT[:, c, :], HP[:, c % 3, 0:SP_COLS], ACT.Gelu, bias=r.b1[:, c:c + 1]
                                             ).then_inc(h_free, 1)
                    act.drain().then_inc(ht_ready, 1)

                def results(g):
                    for b in range(SG):
                        act.wait_ge(y_kept, g * SG + b + 1)
                        act.dma_start(slot_out[:, g * SG + b, :], Y[:, b, :]).then_inc(stored[b], 16)

                with act.Fori(0, GS - 1) as g:
                    hidden(g)
                    keep_turned(g + 1)
                    results(g)
                hidden(GS - 1)
                results(GS - 1)
                for b in range(SG):
                    act.wait_ge(stored[b], 16 * (GS + 1))

            @block.gpsimd
            def _(pool):
                with pool.Fori(0, GS) as g:
                    for b in range(SG):
                        pool.wait_ge(w_free, g * SG + b + 1)
                        nc.gpsimd.tensor_copy(wi[:, b:b + 1], r.weight_row[:, bass.ds(g * SG + b, 1)]).then_inc(staged, 1)
                        nc.gpsimd.tensor_copy(bi[:, b:b + 1], r.bias_row[:, bass.ds(g * SG + b, 1)]).then_inc(staged, 1)
                        pool.wait_ge(staged, (g * SG + b) * 2 + 2)
                        pool.sem_inc(go, 1)
                        nc.gpsimd.indirect_dma_start(out=WE[:, b, :], out_offset=None,
                                                     in_=a["L1_ffn_Wd"].rearrange("e (p c) n -> (e p) (c n)", c=HC),
                                                     in_offset=bass.IndirectOffsetOnAxis(ap=wi[:, b:b + 1], axis=0)
                                                     ).then_inc(weights[b], 16)
                        nc.gpsimd.indirect_dma_start(out=BE[:, b, :], out_offset=None, in_=a["L1_ffn_bd"],
                                                     in_offset=bass.IndirectOffsetOnAxis(ap=bi[:, b:b + 1], axis=0)
                                                     ).then_inc(weights[b], 16)

            @block.tensor
            def _(pe):
                pe.sem_inc(rows_free, 1)
                pe.sem_inc(xt_free, 1)
                pe.sem_inc(ht_free, 1)

                def turn(g):
                    pe.wait_ge(row_load, 16 * g + 16)
                    for b in range(SG):
                        for c in range(KC):
                            ins = nc.tensor.transpose(PT[:, b // 2, (b % 2 * KC + c) * P:(b % 2 * KC + c + 1) * P],
                                                      XR[:, b, c * 128:c * 128 + 128], k.IDENT[0:P, 0:P])
                    ins.then_inc(turned, 1)
                    pe.drain().then_inc(rows_free, 1)

                def hidden(g):
                    pe.wait_ge(xt_ready, g + 1)
                    for c in range(HC):
                        pe.wait_ge(h_free, g * HC + c + (1 if c >= 2 else 2))
                        for kc in range(KC):
                            ins = nc.tensor.matmul(HP[:, c % 3, 0:SP_COLS], r.W1[:, kc, c, :], XT[:, kc, :, :],
                                                   start=(kc == 0), stop=(kc == KC - 1))
                        ins.then_inc(h_ready, 1)
                    pe.drain().then_inc(xt_free, 1)

                def outputs(g):
                    pe.wait_ge(ht_ready, g + 1)
                    for b in range(SG):
                        pe.wait_ge(weights[b], 32 * g + 32)
                        pe.wait_ge(y_free, g * SG + b + 1)
                        for c in range(HC):
                            ins = nc.tensor.matmul(YP[:, b % 2, 0:D], HT[:, c, b * P:b * P + P], WE[:, b, c * D:(c + 1) * D],
                                                   start=(c == 0), stop=(c == HC - 1))
                        ins.then_inc(y_ready, 1)
                    pe.drain().then_inc(ht_free, 1)

                turn(0)
                with pe.Fori(0, GS - 1) as g:
                    hidden(g)
                    turn(g + 1)
                    outputs(g)
                hidden(GS - 1)
                outputs(GS - 1)

            @block.vector
            def _(v):
                v.sem_inc(y_free, 2)
                v.sem_inc(w_free, SG)
                for b in range(SG):
                    v.sem_inc(stored[b], 16)
                with v.Fori(0, GS) as g:
                    for b in range(SG):
                        v.wait_ge(y_ready, g * SG + b + 1)
                        v.wait_ge(stored[b], 16 * g + 16)
                        v.tensor_tensor(Y[:, b, :], YP[:, b % 2, 0:D], BE[:, b, :], ALU.add).then_inc(y_kept, 1)
                        v.drain().then_inc(y_free, 1)
                        v.sem_inc(w_free, 1)


def stage_combine(k, r, out):
    nc = k.nc
    with k.scope() as s:
        Y = s.sb("Y", [P, T, D])
        x_ready, stored = s.sem("x_ready"), s.sem("stored")
        rows = [s.gather_sem(f"rows{g}") for g in range(ITERS)]
        with nc.Block() as block:
            @block.gpsimd
            def _(pool):
                for n in range(T):
                    nc.gpsimd.indirect_dma_start(out=Y[:, n, :], out_offset=None, in_=k.expert_out,
                                                 in_offset=bass.IndirectOffsetOnAxis(ap=r.pos[:, n:n + 1], axis=0)
                                                 ).then_inc(rows[n // B], 16)

            @block.vector
            def _(v):
                for n in range(T):
                    if n % B == 0:
                        v.wait_ge(rows[n // B], 16 * B)
                    ins = v.scalar_tensor_tensor(k.X[:, n, :], Y[:, n, :], r.prob[:, n:n + 1], k.X[:, n, :], ALU.mult, ALU.add)
                    if n % B == B - 1:
                        ins.then_inc(x_ready, 1)

            @block.sync
            def _(sp):
                for g in range(ITERS):
                    sp.wait_ge(x_ready, g + 1)
                    sp.dma_start(node_rows(out)[:, g * B:(g + 1) * B, :], k.X[:, g * B:(g + 1) * B, :]).then_inc(stored, 16)
                sp.wait_ge(stored, 16 * ITERS)




SCALE1 = DH ** -0.5
KD = 256
QSCALE = KD ** -0.25
EPS_ATT = 1e-6
LN_SQRT_M = float(0.5 * np.log(256.0))


class EdgeScores:

    def __init__(self, k, s, S, GK, GQ, ki, qi):
        self.k, self.nc, self.S, self.GK, self.GQ, self.ki, self.qi = k, k.nc, S, GK, GQ, ki, qi
        self.rows = [s.gather_sem(f"rows{b}") for b in range(len(SUBS))]
        self.go = s.sem("staged"), s.sem("go")
        self.used = s.sem("used")

    def pool(self, pool):
        def may_fill(n, b):
            pool.wait_ge(self.used, 4 * n + b + 1)
        gather_rows(self.nc, pool, [(self.k.SRC, self.ki, self.k.keys, self.GK), (self.k.DST, self.qi, self.k.queries, self.GQ)],
                    self.rows, may_fill, self.go)

    def begin(self, v):
        v.sem_inc(self.used, 4)

    def sub(self, v, n, b):
        lo, hi = SUBS[b]
        v.wait_ge(self.rows[b], (n + 1) * 32 * (hi - lo))
        v.tensor_tensor(self.GK[:, lo:hi, :], self.GK[:, lo:hi, :], self.GQ[:, lo:hi, :], ALU.mult)
        v.drain()
        v.tensor_reduce(self.S[:, :, bass.ds(n * CW + lo, hi - lo)].rearrange("p h t -> p t h"),
                        self.GK[:, lo:hi, :].rearrange("p t (h d) -> p t h d", h=H), AX.X, ALU.add).then_inc(self.used, 1)


def stage_edge_weights(k, S):
    nc, a = k.nc, k.a
    with k.scope() as s:
        F = s.sb("F", [P, H, TE])
        R = s.sb("R", [P, H, TE])
        forward = s.sb("forward", [P, TE])
        backward = s.sb("backward", [P, TE])
        ends = s.sb("ends", [P, H, P])
        masked = s.sb("masked", [P, H, P])
        ones = s.sb("ones", [P, P])
        carry = s.sb("carry", [P, 2, H])
        PS = s.ps("PS", [P, 2, 512])
        less, ends_ready, spread = s.sem("less"), s.sem("ends_ready"), s.sem("spread")
        with nc.Block() as block:
            @block.scalar
            def _(act):
                for half in range(2):
                    act.wait_ge(less, half + 1)
                    part = S[:, 4 * half:4 * half + 4, :]
                    nc.scalar.activation(part, part, ACT.Exp, scale=SCALE1)

            @block.tensor
            def _(pe):
                for r in range(2):
                    pe.wait_ge(ends_ready, r + 1)
                    for q in range(2):
                        ins = nc.tensor.matmul(PS[:, q, 0:4 * P], ones[:], ends[:, 4 * q:4 * q + 4, :], start=True, stop=True)
                    ins.then_inc(spread, 1)

            @block.vector
            def _(v):
                v.memset(ones[:], 1.0)
                v.tensor_copy(forward[:, 1:TE], k.SAME[:, 1:TE])
                v.memset(forward[:, 0:1], 1.0)
                v.tensor_copy(backward[:, 0:TE - 1], k.SAME[:, 1:TE])
                v.memset(backward[:, TE - 1:TE], 1.0)
                v.drain()

                def scans(first):
                    for h in range(H):
                        start = (0.0, 0.0) if first else (carry[:, 0, h:h + 1], carry[:, 1, h:h + 1])
                        v.tensor_tensor_scan(F[:, h, :], forward[:], S[:, h, :], start[0], ALU.mult, ALU.max)
                        v.tensor_tensor_scan(R[:, h, ::-1], backward[:, ::-1], S[:, h, ::-1], start[1], ALU.mult, ALU.max)
                    v.drain()
                scans(True)
                for r, (edge, mask) in enumerate(((F[:, :, TE - 1], k.FROM_LEFT), (R[:, :, 0], k.FROM_RIGHT))):
                    v.tensor_tensor(ends[:], k.IDENT[0:P, 0:P].unsqueeze(1).to_broadcast([P, H, P]),
                                    bcast(edge, P), ALU.mult).then_inc(ends_ready, 1)
                    v.wait_ge(spread, r + 1)
                    for q in range(2):
                        v.tensor_tensor(masked[:, 4 * q:4 * q + 4, :], PS[:, q, 0:4 * P].rearrange("p (h n) -> p h n", h=4),
                                        mask[:].unsqueeze(1).to_broadcast([P, 4, P]), ALU.mult)
                    v.drain()
                    v.tensor_reduce(carry[:, r, :], masked[:], AX.X, ALU.max)
                    v.drain()
                scans(False)
                for half in range(2):
                    part = slice(4 * half, 4 * half + 4)
                    v.tensor_tensor(F[:, part, :], F[:, part, :], R[:, part, :], ALU.max)
                    v.drain()
                    v.tensor_tensor(S[:, part, :], S[:, part, :], F[:, part, :], ALU.subtract).then_inc(less, 1)


class Post:

    def __init__(self, k, s, HP, name, nh, func, eps, w1, b1, w2, bias, g1, be1, b2, g2, be2):
        self.k, self.nc, self.nh, self.func, self.eps = k, k.nc, nh, func, eps
        sb, sem = (lambda x, *r: s.sb(name + x, *r)), (lambda x: s.sem(name + x))
        self.w1, self.w2, self.bb1, self.vectors = w1, w2, b1, (bias, g1, be1, b2, g2, be2)
        self.W1 = sb("W1", [128, KC, nh * 128])
        self.W2 = sb("W2", [128, nh, D])
        self.b1 = sb("b1", [128, nh])
        self.vec = sb("vec", [P, 6, D])
        self.R = sb("R", [P, B, D])
        self.RT = sb("RT", [128, KC, B, P])
        self.HT = sb("HT", [128, nh, B * P])
        self.Y = sb("Y", [P, B, D])
        self.stat = sb("stat", [P, B, 6])
        self.mv = sb("mv", [P, B, 2])
        self.var = sb("var", [P, B])
        self.sd = sb("sd", [P, B])
        self.PTY = s.ps(name + "PTY", [128, 3, 512])
        self.HP = HP
        (self.n_var, self.n_sd, self.r_ready, self.rt_turned, self.rt_ready, self.h_ready, self.h_free, self.ht_ready,
         self.y_ready, self.y_kept, self.done, self.adding, self.added) = (sem(x) for x in (
             "n_var", "n_sd", "r_ready", "rt_turned", "rt_ready", "h_ready", "h_free", "ht_ready", "y_ready", "y_kept",
             "done", "adding", "added"))
        self.loads = 9

    def tile(self, b, w):
        return self.PTY[:, b // 2, (b % 2) * 256:(b % 2) * 256 + w]

    def wide(self, m):
        return self.vec[:, m, :].unsqueeze(1).to_broadcast([P, B, D])

    def sync(self, sp, loaded):
        sp.dma_start(self.W1[:], chunks(self.w1)).then_inc(loaded, 16)
        sp.dma_start(self.W2[:], chunks(self.w2)).then_inc(loaded, 16)
        sp.dma_start(self.b1[:], self.bb1.rearrange("(c p) -> p c", p=128), allow_slow_non_contiguous=True).then_inc(loaded, 16)
        for m, x in enumerate(self.vectors):
            sp.dma_start(self.vec[:, m, :], row(x, P)).then_inc(loaded, 16)

    def turn(self, pe, src, ready, i):
        pe.wait_ge(self.y_kept, i + 1)
        for b in range(B):
            for c in range(KC):
                ins = self.nc.tensor.transpose(self.tile(b, 250)[:, c * P:c * P + P], src[:, b, c * 128:c * 128 + 128],
                                               self.k.IDENT[0:P, 0:P])
        ins.then_inc(ready, 1)

    def turn_rows(self, pe, i):
        pe.wait_ge(self.r_ready, i + 1)
        self.turn(pe, self.R, self.rt_turned, i)

    def hidden(self, pe, i):
        pe.wait_ge(self.rt_ready, i + 1)
        for c in range(self.nh):
            for q, (lo, hi) in enumerate(PIECES):
                pe.wait_ge(self.h_free, i * 2 * self.nh + 2 * c + q + 1)
                for kc in range(KC):
                    ins = self.nc.tensor.matmul(self.HP[:, q, 0:hi - lo], self.W1[:, kc, c * 128:c * 128 + 128],
                                                self.RT[:, kc, lo // P:hi // P, :], start=(kc == 0), stop=(kc == KC - 1))
                ins.then_inc(self.h_ready, 1)

    def outputs(self, pe, i):
        pe.wait_ge(self.ht_ready, i + 1)
        for b in range(B):
            for c in range(self.nh):
                ins = self.nc.tensor.matmul(self.tile(b, D)[0:P], self.HT[:, c, b * P:b * P + P], self.W2[:, c, :],
                                            start=(c == 0), stop=(c == self.nh - 1))
        ins.then_inc(self.y_ready, 1)

    def keep_turned(self, ready):
        for b in range(B):
            ins = self.nc.scalar.activation(self.RT[:, :, b, :], self.tile(b, 250).rearrange("p (c n) -> p c n", c=KC), ACT.Copy)
        ins.then_inc(ready, 1)

    def root(self, act, count):
        act.wait_ge(self.n_var, count)
        self.nc.scalar.activation(self.sd[:], self.var[:], ACT.Sqrt).then_inc(self.n_sd, 1)

    def keep_rows(self, act, i):
        act.wait_ge(self.rt_turned, i + 1)
        self.keep_turned(self.rt_ready)

    def activate(self, act, i, roots={}):
        for c in range(self.nh):
            if c in roots:
                roots[c]()
            for q, (lo, hi) in enumerate(PIECES):
                act.wait_ge(self.h_ready, i * 2 * self.nh + 2 * c + q + 1)
                self.nc.scalar.activation(self.HT[:, c, lo:hi], self.HP[:, q, 0:hi - lo], self.func,
                                          bias=self.b1[:, c:c + 1]).then_inc(self.h_free, 1)
        act.drain().then_inc(self.ht_ready, 1)

    def keep_outputs(self, act, i):
        act.wait_ge(self.y_ready, i + 1)
        for q in range(3):
            m = min(2, B - 2 * q)
            ins = self.nc.scalar.activation(self.Y[:, 2 * q:2 * q + m, :],
                                            self.PTY[0:P, q, 0:m * D].rearrange("p (b d) -> p b d", b=m), ACT.Copy)
        ins.then_inc(self.y_kept, 1)

    def layernorm(self, v, src, count, gm, writable=None):
        for b in range(B):
            v.bn_stats(self.stat[:, b, :], src[:, b, :])
        v.drain()
        for b in range(B):
            v.bn_aggr(self.mv[:, b, :], self.stat[:, b, :])
        v.drain()
        v.tensor_scalar(self.var[:], self.mv[:, :, 1], self.eps, None, ALU.add).then_inc(self.n_var, 1)
        v.wait_ge(self.n_sd, count)
        v.reciprocal(self.var[:], self.sd[:])
        v.drain()
        if writable is not None:
            v.wait_ge(*writable)
        for b in range(B):
            v.tensor_scalar(self.R[:, b, :], src[:, b, :], self.mv[:, b, 0:1], self.var[:, b:b + 1], ALU.subtract, ALU.mult)
        v.drain()
        v.tensor_tensor(self.R[:], self.R[:], self.wide(gm), ALU.mult)
        if gm == 1:
            v.drain()
            v.tensor_tensor(self.R[:], self.R[:], self.wide(gm + 1), ALU.add)
        return v.drain()

    def finish(self, v, i):
        v.wait_ge(self.y_kept, i + 2)
        v.tensor_tensor(self.R[:], self.R[:], self.Y[:], ALU.add)
        v.drain()
        v.tensor_tensor(self.R[:], self.R[:], self.wide(3), ALU.add)
        v.drain()
        self.layernorm(v, self.R, 2 * i + 2, 4).then_inc(self.done, 1)

    def add(self, pool, i):
        x = self.k.X[:, bass.ds(i * B, B), :]
        pool.wait_ge(self.done, i + 1)
        pool.sem_inc(self.adding, 1)
        self.nc.gpsimd.tensor_tensor(x, x, self.R[:], ALU.add)
        pool.drain().then_inc(self.added, 1)
        self.nc.gpsimd.tensor_tensor(x, x, self.wide(5), ALU.add)
        pool.drain()


def stage_posts(k, XN):
    nc, a = k.nc, k.a
    with k.scope() as s:
        HP = s.ps("HP", [128, 2, 512])
        M = Post(k, s, HP, "M_", 2, ACT.Relu, 1e-6, a["L1_mix_W1"], a["L1_mix_bias1"], a["L1_mix_W2"], a["L1_mix_bo"],
                 a["L1_mix_g1"], a["L1_mix_beta1"], a["L1_mix_bias2"], a["L1_mix_g2"], a["L1_mix_beta2"])
        G = Post(k, s, HP, "G_", 4, ACT.Gelu, 1e-5, a["L1_gnn_ffn_w1"], a["L1_gnn_ffn_b1"], a["L1_gnn_ffn_w2"], a["L1_gnn_Wo_b"],
                 a["L1_gnn_ln1_g"], a["L1_gnn_ln1_b"], a["L1_gnn_ffn_b2"], a["L1_gnn_ln2_g"], a["L1_gnn_ln2_b"])
        MS = s.sb("MS", [P, B, D])
        WO = s.sb("WO", [128, KC, D])
        base = s.sb("base", [P, P])
        idx = s.sb("idx", [P, B], I32)
        A = s.sb("A", [P, B, GW])
        GM = s.sb("GM", [P, B, P])
        sem = s.sem
        loaded, staged, go, open_ready, sums_ready, sums_used, sum_ready, sum_used = (sem(x) for x in (
            "loaded", "staged", "go", "open_ready", "sums_ready", "sums_used", "sum_ready", "sum_used"))
        a_ready, msg_turned, at_ready, att_ready = (sem(x) for x in ("a_ready", "msg_turned", "at_ready", "att_ready"))
        rows = s.gather_sem("rows")
        NL = 16 * (M.loads + G.loads + 2)
        wsum = G.PTY[0:P, 2, 256:256 + B * H]

        with nc.Block() as block:
            @block.sync
            def _(sp):
                M.sync(sp, loaded)
                G.sync(sp, loaded)
                sp.dma_start(WO[:], chunks(a["L1_gnn_Wo_w"])).then_inc(loaded, 16)
                sp.dma_start(base[:], a["c_base"]).then_inc(loaded, 16)
                sp.wait_ge(loaded, NL)

            @block.gpsimd
            def _(pool):
                def fetch(i):
                    pool.wait_ge(staged, i + 1)
                    pool.sem_inc(go, 1)
                    for b in range(B):
                        nc.gpsimd.indirect_dma_start(out=A[:, b, :], out_offset=None, in_=k.run,
                                                     in_offset=bass.IndirectOffsetOnAxis(ap=idx[:, b:b + 1], axis=0)
                                                     ).then_inc(rows, 16)

                def add_up(i):
                    pool.wait_ge(sum_used, i + 1)
                    pool.sem_inc(go, 1)
                    nc.gpsimd.tensor_tensor(MS[:], k.ACC[:, bass.ds(i * B, B), :], XN[:, bass.ds(i * B, B), 0:D], ALU.add)
                    pool.drain()
                    nc.gpsimd.tensor_tensor(MS[:], MS[:], M.wide(0), ALU.add).then_inc(sum_ready, 1)

                fetch(0)
                pool.wait_ge(loaded, NL)
                add_up(0)
                with pool.Fori(0, ITERS - 1) as i:
                    add_up(i + 1)
                    fetch(i + 1)
                    M.add(pool, i)
                    G.add(pool, i)
                M.add(pool, ITERS - 1)
                G.add(pool, ITERS - 1)

            @block.tensor
            def _(pe):
                def open_sums(i):
                    for b in range(B):
                        pe.wait_ge(open_ready, i * B + b + 1)
                        nc.tensor.matmul(G.tile(b, D)[0:P], GM[:, b, :], k.RLAST[:, 0:D], start=True, stop=True)
                        ins = nc.tensor.matmul(wsum[:, b * H:(b + 1) * H], GM[:, b, :], k.RLAST[:, D:GW], start=True, stop=True)
                    ins.then_inc(sums_ready, 1)

                def five_tiles(i, last):
                    pe.wait_ge(a_ready, i + 1)
                    G.turn(pe, A, msg_turned, i)
                    M.turn_rows(pe, i)
                    pe.wait_ge(at_ready, i + 1)
                    for b in range(B):
                        for c in range(KC):
                            ins = nc.tensor.matmul(G.tile(b, D)[0:P], G.RT[:, c, b, :], WO[:, c, :], start=(c == 0), stop=(c == KC - 1))
                    ins.then_inc(att_ready, 1)
                    M.hidden(pe, i)
                    M.outputs(pe, i)
                    G.turn_rows(pe, i)
                    if not last:
                        pe.wait_ge(G.rt_ready, i + 1)
                        open_sums(i + 1)
                    G.hidden(pe, i)
                    if not last:
                        pe.wait_ge(sums_used, i + 2)
                    G.outputs(pe, i)

                pe.wait_ge(loaded, NL)
                open_sums(0)
                with pe.Fori(0, ITERS - 1) as i:
                    five_tiles(i, False)
                five_tiles(ITERS - 1, True)

            @block.scalar
            def _(act):
                for post in (M, G):
                    act.sem_inc(post.h_free, 2)
                    act.sem_inc(post.y_kept, 1)
                act.wait_ge(loaded, NL)
                M.root(act, 1)

                def five_tiles(i, last):
                    act.wait_ge(msg_turned, i + 1)
                    G.keep_turned(at_ready)
                    M.keep_rows(act, i)
                    M.activate(act, i)
                    M.keep_outputs(act, i)
                    G.root(act, 2 * i + 1)
                    G.keep_rows(act, i)
                    roots = {2: lambda: M.root(act, 2 * i + 2)}
                    if not last:
                        roots[3] = lambda: M.root(act, 2 * i + 3)
                    G.activate(act, i, roots)
                    G.keep_outputs(act, i)
                    G.root(act, 2 * i + 2)

                with act.Fori(0, ITERS - 1) as i:
                    five_tiles(i, False)
                five_tiles(ITERS - 1, True)

            @block.vector
            def _(v):
                def stage_fetch(i):
                    v.tensor_copy(idx[:], k.LAST[:, bass.ds(i * B, B)]).then_inc(staged, 1)
                    for b in range(B):
                        open_nodes(v, k, GM[:, b, :], base[:], i * B + b).then_inc(open_ready, 1)

                def messages(i):
                    v.wait_ge(rows, (i + 1) * 16 * B)
                    v.wait_ge(sums_ready, i + 1)
                    for b in range(B):
                        v.tensor_tensor(A[:, b, 0:D], A[:, b, 0:D], G.tile(b, D)[0:P], ALU.add)
                    v.tensor_tensor(A[:, :, D:GW], A[:, :, D:GW], wsum.rearrange("p (b h) -> p b h", h=H), ALU.add)
                    v.drain().then_inc(sums_used, 1)
                    v.tensor_scalar(A[:, :, D:GW], A[:, :, D:GW], 1e-8, None, ALU.add)
                    v.drain()
                    v.reciprocal(A[:, :, D:GW], A[:, :, D:GW])
                    v.drain()
                    g = A[:, :, 0:D].rearrange("p b (h d) -> p b h d", h=H)
                    v.tensor_tensor(g, g, A[:, :, D:GW].unsqueeze(3).to_broadcast([P, B, H, DH]), ALU.mult)
                    v.drain()
                    for b in range(B):
                        v.tensor_scalar(A[:, b, 0:D], A[:, b, 0:D], k.HAS[:, bass.ds(i * B + b, 1)], None, ALU.mult)
                    v.drain().then_inc(a_ready, 1)

                def graph_rows(i, first, last):
                    v.wait_ge(att_ready, i + 1)
                    if not last:
                        stage_fetch(i + 1)
                    if not first:
                        v.wait_ge(G.added, i)
                    for b in range(B):
                        v.tensor_tensor(G.R[:, b, :], G.tile(b, D)[0:P], XN[:, i * B + b, 0:D], ALU.add)
                    v.drain()
                    v.tensor_tensor(G.R[:], G.R[:], G.wide(0), ALU.add)
                    v.drain()
                    G.layernorm(v, G.R, 2 * i + 1, 1).then_inc(G.r_ready, 1)

                def mix_rows(i, first):
                    v.wait_ge(sum_ready, i + 1)
                    M.layernorm(v, MS, 2 * i + 1, 1, None if first else (M.added, i)).then_inc(M.r_ready, 1)
                    v.sem_inc(sum_used, 1)

                def five_tiles(i, first, last):
                    graph_rows(i, first, last)
                    if not last:
                        messages(i + 1)
                    M.finish(v, i)
                    if not last:
                        mix_rows(i + 1, False)
                    G.finish(v, i)

                v.sem_inc(sum_used, 1)
                v.wait_ge(loaded, NL)
                stage_fetch(0)
                mix_rows(0, True)
                messages(0)
                five_tiles(0, True, False)
                with v.Fori(1, ITERS - 1) as i:
                    five_tiles(i, False, False)
                five_tiles(ITERS - 1, False, True)


def stage_linear_attention(k, XN, XNT, S, h0, heads, with_scores):
    nc, a = k.nc, k.a
    CB = B * P
    with k.scope() as s:
        WQ = s.sb("WQ", [128, KC, KD])
        WK = s.sb("WK", [128, KC, KD])
        WV = s.sb("WV", [128, KC, KD])
        WO = s.sb("WO", [128, KC, D])
        bv = s.sb("bv", [1, KD])
        PR = s.sb("PR", [128, 2, KD])
        PJ = s.sb("PJ", [128, KC, KD])
        bqk = s.sb("bqk", [128, 2, H, KC])
        bcur = s.sb("bcur", [128, 2, KC])
        half = s.sb("half", [128, 128])
        shift = s.sb("shift", [128, 1])
        QT = s.sb("QT", [128, KC, CB])
        SQ = s.sb("SQ", [128, KC, CB])
        PH = s.sb("PH", [128, 2, CB])
        PK = s.sb("PK", [P, B, KD])
        nb = s.sb("nb", [P, B])
        AS = s.sb("AS", [128, 2, D + 1])
        AT = s.sb("AT", [128, KC, KD])
        AL = s.sb("AL", [1, KD])
        KVT = s.sb("KVT", [128, KC, KD])
        KO = s.sb("KO", [128, 2, D + 1])
        rz = s.sb("rz", [P, 3])
        CP = s.ps("CP", [128, 2, 512])
        UP = s.ps("UP", [128, 3, 512])
        AP = s.ps("AP", [128, 2, 512])
        TP = s.ps("TP", [128, 512])
        sem = s.sem
        (loaded, proj_turned, ready0, wk_loaded, wq_loaded, wvo_loaded, k_used, q_used, vo_used,
         c_ready, c_free, qt_ready, qt_free, sq_ready, u_ready, pk_exp, pk_ready, a_zeroed, a_ready, as_ready,
         t_ready, t_kept, kv_ready, kv_kept, ko_ready, ko_kept, ph_exp, ph_ready, ph_free, o_ready,
         pk_free, u_free, begun) = (
            sem(x) for x in (
                "loaded", "proj_turned", "ready0", "wk_loaded", "wq_loaded", "wvo_loaded", "k_used", "q_used",
                "vo_used", "c_ready", "c_free", "qt_ready", "qt_free", "sq_ready", "u_ready", "pk_exp", "pk_ready",
                "a_zeroed", "a_ready", "as_ready", "t_ready", "t_kept", "kv_ready", "kv_kept", "ko_ready", "ko_kept",
                "ph_exp", "ph_ready", "ph_free", "o_ready", "pk_free", "u_free", "begun"))
        if with_scores:
            edges = EdgeScores(k, s, S, s.sb("GK", [P, CW, D]), s.sb("GQ", [P, CW, D]), s.sb("ki", [P, CW], I32),
                               s.sb("qi", [P, CW], I32))
            assert STEPS == heads * ITERS
        else:
            edges = EdgeSums(k, s, k.sup, k.run, s.sb("G", [P, CW, GW]), s.sb("idx", [P, CW], I32), S)
            assert STEPS == (2 * heads - 1) * (ITERS - 1) + ITERS
        QTS, CPS = 2 * ITERS, 4 * ITERS + 8 * ITERS

        with nc.Block() as block:
            @block.sync
            def _(sp):
                sp.dma_start(PR[:], chunks(a["L1_mix_proj"])).then_inc(loaded, 16)
                for m, x in enumerate((a["L1_mix_bq"], a["L1_mix_bk"])):
                    for c in range(KC):
                        sp.dma_start(bqk[:, m, :, c], x.rearrange("h (c p) -> c p h", p=128)[c],
                                     allow_slow_non_contiguous=True).then_inc(loaded, 16)

                def load_k(h):
                    sp.wait_ge(k_used, h + 1)
                    sp.dma_start(WK[:], chunks(a["L1_mix_Wk"].rearrange("p h n -> p (h n)"))[:, :, bass.ds((h0 + h) * KD, KD)]).then_inc(wk_loaded, 16)

                def load_vo(h):
                    sp.wait_ge(vo_used, h + 1)
                    sp.dma_start(WV[:], chunks(a["L1_mix_Wv"].rearrange("p h n -> p (h n)"))[:, :, bass.ds((h0 + h) * KD, KD)]).then_inc(wvo_loaded, 16)
                    sp.dma_start(WO[:], a["L1_mix_Wo"].rearrange("h (c p) n -> h p c n", p=128)[h0 + h]).then_inc(wvo_loaded, 16)
                    sp.dma_start(bv[:], a["L1_mix_bv"][bass.ds(h0 + h, 1), :]).then_inc(wvo_loaded, 16)

                def load_q(h):
                    sp.wait_ge(q_used, h + 1)
                    sp.dma_start(WQ[:], chunks(a["L1_mix_Wq"].rearrange("p h n -> p (h n)"))[:, :, bass.ds((h0 + h) * KD, KD)]).then_inc(wq_loaded, 16)

                if with_scores:
                    with sp.Fori(0, heads) as h:
                        load_k(h)
                        load_vo(h)
                        load_q(h)
                else:
                    load_k(0)
                    load_vo(0)
                    load_q(0)
                    edges.sync_begin(sp)
                    with sp.Fori(0, heads - 1) as h:
                        edges.sync_steps(sp, 2 * h * (ITERS - 1), ITERS - 1)
                        load_k(h + 1)
                        load_vo(h + 1)
                        edges.sync_steps(sp, (2 * h + 1) * (ITERS - 1), ITERS - 1)
                        load_q(h + 1)
                    edges.sync_steps(sp, 2 * (heads - 1) * (ITERS - 1), 2 * ITERS - 1)
                    edges.sync_end(sp)
                sp.wait_ge(wq_loaded, 16 * heads)

            @block.gpsimd
            def _(pool):
                edges.pool(pool)

            @block.tensor
            def _(pe):
                for free in (qt_free, k_used, vo_used, q_used):
                    pe.sem_inc(free, 1)
                pe.sem_inc(pk_free, B)
                pe.sem_inc(ph_free, 1)
                pe.wait_ge(loaded, 80)
                for r in range(2):
                    for c in range(KC):
                        ins = nc.tensor.transpose(AP[:, r, c * 128:c * 128 + 128], PR[:, r, c * 128:c * 128 + 128], k.IDENT[:])
                ins.then_inc(proj_turned, 1)
                pe.wait_ge(ready0, 1)

                def turned(W, base_c, i):
                    for c in range(KC):
                        for q, (lo, hi) in enumerate(PIECES):
                            pe.wait_ge(c_free, base_c + 2 * c + q + 1)
                            for kc in range(KC):
                                ins = nc.tensor.matmul(CP[:, q, 0:hi - lo], W[:, kc, c * 128:c * 128 + 128],
                                                       XNT[:, kc, bass.ds(i * CB + lo, hi - lo)],
                                                       start=(kc == 0), stop=(kc == KC - 1))
                            ins.then_inc(c_ready, 1)

                def key_sums(h, i, b):
                    pe.wait_ge(pk_ready, h * T + i * B + b + 1)
                    for r in range(2):
                        ins = nc.tensor.matmul(AP[:, r, 0:D + 1], PK[:, b, r * 128:r * 128 + 128], XN[:, i * B + b, :],
                                               start=False, stop=False, skip_group_check=True)
                    ins.then_inc(pk_free, 1)

                def key_item(h, i, first):
                    turned(WK, h * CPS + i * 4, i)
                    if not first:
                        key_sums(h, i - 1, B - 2)
                        key_sums(h, i - 1, B - 1)
                    pe.wait_ge(sq_ready, h * QTS + i + 1)
                    for b in range(B):
                        pe.wait_ge(u_free, h * 2 * T + i * B + b + 1)
                        for kc in range(KC):
                            nc.tensor.matmul(UP[0:P, b % 3, 0:KD], QT[:, kc, b * P:b * P + P], PJ[:, kc, :],
                                             start=(kc == 0), stop=(kc == KC - 1))
                        nc.tensor.matmul(UP[0:P, b % 3, KD:KD + 1], SQ[:, 0, b * P:b * P + P], half[:, 0:1],
                                         start=True, stop=True).then_inc(u_ready, 1)
                        if b >= 2:
                            key_sums(h, i, b - 2)
                    pe.drain().then_inc(qt_free, 1)

                def phi_q(h, i):
                    for r in range(2):
                        for q, (lo, hi) in enumerate(PIECES):
                            pe.wait_ge(c_free, h * CPS + 4 * ITERS + i * 8 + 4 + 2 * r + q + 1)
                            for kc in range(KC):
                                nc.tensor.matmul(CP[:, q, 0:hi - lo], PJ[:, kc, r * 128:r * 128 + 128], QT[:, kc, lo:hi],
                                                 start=(kc == 0), stop=False)
                            if r == 0 and q == 0:
                                pe.wait_ge(sq_ready, h * QTS + ITERS + i + 1)
                            nc.tensor.matmul(CP[:, q, 0:hi - lo], half[:], SQ[:, 0, lo:hi],
                                             start=False, stop=True).then_inc(c_ready, 1)
                    pe.drain().then_inc(qt_free, 1)

                def outputs(h, i):
                    pe.wait_ge(ph_ready, h * ITERS + i + 1)
                    for b in range(B):
                        pe.wait_ge(u_free, h * 2 * T + T + i * B + b + 1)
                        for r in range(2):
                            ins = nc.tensor.matmul(UP[0:P, b % 3, 0:D + 1], PH[:, r, b * P:b * P + P], KO[:, r, :],
                                                   start=(r == 0), stop=(r == 1))
                        ins.then_inc(o_ready, 1)
                    pe.drain().then_inc(ph_free, 1)

                def query_turned(h, i):
                    turned(WQ, h * CPS + 4 * ITERS + i * 8, i)

                with pe.Fori(0, heads) as h:
                    pe.wait_ge(wk_loaded, 16 * h + 16)
                    pe.wait_ge(a_zeroed, h + 1)
                    pe.sem_inc(begun, 1)
                    key_item(h, 0, True)
                    with pe.Fori(1, ITERS) as i:
                        key_item(h, i, False)
                    key_sums(h, ITERS - 1, B - 2)
                    key_sums(h, ITERS - 1, B - 1)
                    pe.drain().then_inc(a_ready, 1)
                    pe.sem_inc(k_used, 1)
                    pe.wait_ge(wq_loaded, 16 * h + 16)
                    query_turned(h, 0)
                    pe.wait_ge(as_ready, h + 1)
                    for c in range(KC):
                        for r in range(2):
                            ins = nc.tensor.transpose(TP[:, c * 256 + r * 128:c * 256 + r * 128 + 128],
                                                      AS[:, r, c * 128:c * 128 + 128], k.IDENT[:])
                    ins.then_inc(t_ready, 1)
                    pe.wait_ge(qt_ready, h * QTS + ITERS + 1)
                    phi_q(h, 0)
                    pe.wait_ge(t_kept, 2 * h + 1)
                    for r in range(2):
                        ins = nc.tensor.transpose(TP[0:1, r * 128:r * 128 + 128], AS[:, r, D:D + 1], k.IDENT[:])
                    ins.then_inc(t_ready, 1)
                    pe.wait_ge(t_kept, 2 * h + 2)
                    pe.wait_ge(wvo_loaded, 48 * h + 48)
                    for c in range(KC):
                        for kc in range(KC):
                            nc.tensor.matmul(TP[:, c * 256:c * 256 + 256], WV[:, kc, c * 128:c * 128 + 128], AT[:, kc, :],
                                             start=(kc == 0), stop=False)
                        ins = nc.tensor.matmul(TP[:, c * 256:c * 256 + 256], bv[:, c * 128:c * 128 + 128], AL[:],
                                               start=False, stop=True)
                    ins.then_inc(kv_ready, 1)
                    pe.wait_ge(kv_kept, h + 1)
                    for r in range(2):
                        for kc in range(KC):
                            ins = nc.tensor.matmul(TP[:, r * 256:r * 256 + 256], KVT[:, kc, r * 128:r * 128 + 128], WO[:, kc, :],
                                                   start=(kc == 0), stop=(kc == KC - 1))
                    ins.then_inc(ko_ready, 1)
                    pe.drain().then_inc(vo_used, 1)
                    pe.wait_ge(ko_kept, h + 1)
                    pe.sem_inc(begun, 1)
                    with pe.Fori(1, ITERS) as i:
                        query_turned(h, i)
                        outputs(h, i - 1)
                        pe.wait_ge(qt_ready, h * QTS + ITERS + i + 1)
                        phi_q(h, i)
                    outputs(h, ITERS - 1)
                    pe.sem_inc(q_used, 1)

            @block.scalar
            def _(act):
                act.sem_inc(c_free, 2)
                act.wait_ge(ready0, 1)

                def turned(m, item, cbase):
                    act.wait_ge(qt_free, item + 1)
                    for c in range(KC):
                        for q, (lo, hi) in enumerate(PIECES):
                            act.wait_ge(c_ready, cbase + 2 * c + q + 1)
                            nc.scalar.activation(QT[:, c, lo:hi], CP[:, q, 0:hi - lo], ACT.Identity, scale=QSCALE,
                                                 bias=bcur[:, m, c:c + 1])
                            nc.scalar.activation(SQ[:, c, lo:hi], CP[:, q, 0:hi - lo], ACT.Square, scale=QSCALE,
                                                 bias=bcur[:, m, c:c + 1]).then_inc(c_free, 1)
                    act.drain().then_inc(qt_ready, 1)

                def key_item(h, i):
                    turned(1, h * QTS + i, h * CPS + i * 4)
                    for b in range(B):
                        n = h * T + i * B + b
                        act.wait_ge(pk_free, n + 1)
                        act.wait_ge(u_ready, n + 1)
                        nc.scalar.activation(nb[:, b:b + 1], UP[0:P, b % 3, KD:KD + 1], ACT.Identity, bias=shift[0:P, 0:1])
                        act.drain()
                        nc.scalar.activation(PK[:, b, :], UP[0:P, b % 3, 0:KD], ACT.Exp, bias=nb[:, b:b + 1]
                                             ).then_inc(pk_exp, 1)
                        act.drain().then_inc(u_free, 1)

                def query_turned(h, i):
                    turned(0, h * QTS + ITERS + i, h * CPS + 4 * ITERS + i * 8)

                def phi_q(h, i):
                    act.wait_ge(ph_free, h * ITERS + i + 1)
                    for r in range(2):
                        for q, (lo, hi) in enumerate(PIECES):
                            act.wait_ge(c_ready, h * CPS + 4 * ITERS + i * 8 + 4 + 2 * r + q + 1)
                            nc.scalar.activation(PH[:, r, lo:hi], CP[:, q, 0:hi - lo], ACT.Exp, bias=shift[:, 0:1]
                                                 ).then_inc(c_free, 1)
                    act.drain().then_inc(ph_exp, 1)

                with act.Fori(0, heads) as h:
                    nc.scalar.activation(bcur[:], bqk[:, :, h0 + h, :], ACT.Copy)
                    act.drain()
                    with act.Fori(0, ITERS) as i:
                        key_item(h, i)
                    act.wait_ge(a_ready, h + 1)
                    nc.scalar.activation(AS[:], AP[:, :, 0:D + 1], ACT.Copy).then_inc(as_ready, 1)
                    query_turned(h, 0)
                    act.wait_ge(t_ready, 2 * h + 1)
                    nc.scalar.activation(AT[:], TP[:].rearrange("p (c m) -> p c m", c=KC), ACT.Copy).then_inc(t_kept, 1)
                    phi_q(h, 0)
                    act.wait_ge(t_ready, 2 * h + 2)
                    nc.scalar.activation(AL[:], TP[0:1, 0:KD], ACT.Copy).then_inc(t_kept, 1)
                    act.wait_ge(kv_ready, h + 1)
                    nc.scalar.activation(KVT[:], TP[:].rearrange("p (c m) -> p c m", c=KC), ACT.Copy).then_inc(kv_kept, 1)
                    act.wait_ge(ko_ready, h + 1)
                    nc.scalar.activation(KO[:, :, 0:D], TP[:].rearrange("p (c m) -> p c m", c=2), ACT.Copy)
                    nc.scalar.activation(KO[:, :, D:D + 1], AS[:, :, D:D + 1], ACT.Copy)
                    act.drain().then_inc(ko_kept, 1)
                    with act.Fori(1, ITERS) as i:
                        query_turned(h, i)
                        phi_q(h, i)

            @block.vector
            def _(v):
                v.memset(half[:], -0.5)
                v.memset(shift[:], -LN_SQRT_M)
                v.wait_ge(proj_turned, 1)
                v.tensor_copy(PJ[:].rearrange("p c (r m) -> p r c m", r=2), AP[:, :, 0:256].rearrange("p r (c m) -> p r c m", c=KC))
                v.tensor_scalar(bqk[:], bqk[:], QSCALE, None, ALU.mult)
                v.drain()
                v.memset(AP[:], 0.0)
                if h0 == 0:
                    v.memset(k.ACC[:], 0.0)
                edges.begin(v)
                v.sem_inc(u_free, 2)
                v.sem_inc(a_zeroed, 1)
                v.drain().then_inc(ready0, 1)

                SHARE = (3, 3, 3, 3, 4)

                def edge_part(h, phase, i, at):
                    if with_scores:
                        if at in (1, 3):
                            u = 2 * (phase * ITERS + i) + at // 2
                            edges.sub(v, h * ITERS + u // 4, u % 4)
                    elif isinstance(h, int) and phase == 0:
                        edges.sub(v, 2 * h * (ITERS - 1) + i, at)
                    elif at < SHARE[i]:
                        u = sum(SHARE[:i]) + at
                        late = 1 if isinstance(h, int) else 0
                        edges.sub(v, (2 * h + phase) * (ITERS - 1) + late + u // 4, u % 4)

                def squares(item):
                    v.wait_ge(qt_ready, item + 1)
                    v.tensor_tensor(SQ[:, 0, :], SQ[:, 0, :], SQ[:, 1, :], ALU.add).then_inc(sq_ready, 1)

                def key_item(h, i):
                    squares(h * QTS + i)
                    for b in range(B):
                        n = h * T + i * B + b
                        if with_scores or b < 3:
                            edge_part(h, 0, i, b)
                        v.wait_ge(pk_exp, n + 1)
                        v.tensor_scalar(PK[:, b, :], PK[:, b, :], EPS_ATT, None, ALU.add).then_inc(pk_ready, 1)
                    if not with_scores:
                        edge_part(h, 0, i, 3)

                def add_outputs(h, i, edges_of=None):
                    for b in range(B):
                        v.wait_ge(o_ready, h * T + i * B + b + 1)
                        v.reciprocal(rz[:, b % 3:b % 3 + 1], UP[0:P, b % 3, D:D + 1])
                        v.drain()
                        v.scalar_tensor_tensor(k.ACC[:, i * B + b, :], UP[0:P, b % 3, 0:D], rz[:, b % 3:b % 3 + 1],
                                               k.ACC[:, i * B + b, :], ALU.mult, ALU.add).then_inc(u_free, 1)
                        if edges_of is not None and b == 2:
                            edge_part(h, 1, edges_of, 0)

                def query_item(h, i, first):
                    squares(h * QTS + ITERS + i)
                    if not first:
                        add_outputs(h, i - 1, i)
                    else:
                        edge_part(h, 1, i, 0)
                    edge_part(h, 1, i, 1)
                    edge_part(h, 1, i, 2)
                    v.wait_ge(ph_exp, h * ITERS + i + 1)
                    v.tensor_scalar(PH[:], PH[:], EPS_ATT, None, ALU.add).then_inc(ph_ready, 1)
                    edge_part(h, 1, i, 3)

                def between(h):
                    v.wait_ge(as_ready, h + 1)
                    v.memset(AP[:], 0.0).then_inc(a_zeroed, 1)

                with v.Fori(0, heads if with_scores else heads - 1) as h:
                    for i in range(ITERS):
                        key_item(h, i)
                    between(h)
                    for i in range(ITERS):
                        query_item(h, i, i == 0)
                    add_outputs(h, ITERS - 1)
                if not with_scores:
                    last = heads - 1
                    with v.Fori(0, ITERS) as i:
                        key_item(last, i)
                    between(last)
                    for i in range(ITERS):
                        query_item(last, i, i == 0)
                    edges.end(v)
                    add_outputs(last, ITERS - 1)


def layer1_mix(k):
    a = k.a
    with k.scope() as f:
        k.ACC = f.sb("ACC", [P, T, D])
        XN = f.sb("XN", [P, T, D + 1])
        with k.scope() as g:
            XNT = g.sb("XNT", [128, KC, N])
            stage_normalise(k, 1e-5, XNT, XN=XN, tables=(
                (a["L1_gnn_Wq"], k.queries), (a["L1_gnn_Wk"], k.keys), (a["L1_gnn_Wv"], k.sup)))
            S = g.sb("S", [P, H, TE])
            stage_linear_attention(k, XN, XNT, S, 0, 5, True)
            stage_edge_weights(k, S)
            stage_linear_attention(k, XN, XNT, S, 5, 3, False)
        stage_posts(k, XN)

def program(nc, a, out):
    with ExitStack() as stack:
        k = Core(nc, a, stack)
        keep = stack.enter_context(k.scope())
        k.X = keep.sb("X", [P, T, D])
        k.IDENT = keep.sb("IDENT", [128, 128])
        k.NODE = keep.sb("NODE", [P, T])
        k.MV = keep.sb("MV", [P, T, 2])
        k.RSTD = keep.sb("RSTD", [P, T])
        k.SD = keep.sb("SD", [P, T])
        k.SRC = keep.sb("SRC", [P, TE], I32)
        k.DST = keep.sb("DST", [P, TE], I32)
        k.SAME = keep.sb("SAME", [P, TE])
        k.FROM_LEFT = keep.sb("FROM_LEFT", [P, P])
        k.FROM_RIGHT = keep.sb("FROM_RIGHT", [P, P])
        k.OPEN = keep.sb("OPEN", [P, T])
        k.LAST = keep.sb("LAST", [P, T], I32)
        k.HAS = keep.sb("HAS", [P, T])
        k.RLAST = keep.sb("RLAST", [P, GW])
        k.keys = nc.dram_tensor("keys", [N, D], F32, kind="Internal").ap()
        k.queries = nc.dram_tensor("queries", [N, D], F32, kind="Internal").ap()
        k.weights = nc.dram_tensor("router_weights", [N, 1], F32, kind="Internal").ap()
        k.sup = nc.dram_tensor("support", [N, D], F32, kind="Internal").ap()
        k.run = nc.dram_tensor("running_sums", [E, GW], F32, kind="Internal").ap()
        k.run0 = nc.dram_tensor("running_sums0", [E, D], F32, kind="Internal").ap()
        k.by_expert = nc.dram_tensor("rows_by_expert", [SLOTS * P, D], F32, kind="Internal").ap()
        k.expert_out = nc.dram_tensor("expert_outputs", [SLOTS * P, D], F32, kind="Internal").ap()
        with k.scope() as s0:
            s0.WPT = s0.sb("WPT", [128, KC, D])
            s0.bias = s0.sb("bias", [P, 3 * D])
            s0.second = s0.sb("second", [128, H * FC])
            s0.fac = s0.sb("fac", [P, H])
            s0.bsum = s0.sb("bsum", [P, 2, D])
            s0.KV = s0.sb("KV", [128, H * FC, V1])
            k.QKV = s0.sb("QKV", [P, T, 3 * D])
            with k.scope() as w:
                last_edges = LastEdges(k, w)
                stage_edges(k, last_edges.firstrow)
                W = w.sb("W", [128, KC, 4 * D])
                stage_weights0(k, s0, W)
                stage_normalise(k, 1e-5, tables=[(None, None)] * 3 + [(None, k.sup)], W=W, KEPT=k.QKV,
                                beside=last_edges)
            stage_layer0_mix(k, s0)
            stage_layer0_nodes(k, s0)
        with k.scope() as f:
            XNT = f.sb("XNT", [128, KC, N])
            f.selw = f.sb("selw", [P, T])
            stage_normalise(k, 1e-5, XNT, ranked=f)
            stage_layer0_ffn(k, f, XNT)
        layer1_mix(k)
        with k.scope() as r:
            r.W1 = r.sb("W1", [128, KC, HC, 128])
            r.b1 = r.sb("b1", [128, HC])
            r.prob = r.sb("prob", [P, T])
            r.pos = r.sb("pos", [P, T], I32)
            r.weight_row = r.sb("weight_row", [128, SLOTS], I32)
            r.bias_row = r.sb("bias_row", [P, SLOTS], I32)
            with k.scope() as f:
                XNT = f.sb("XNT", [128, KC, N])
                XN = f.sb("XN", [P, T, D + 1])
                stage_normalise(k, 1e-5, XNT, XN=XN)
                stage_gate(k, r, XNT, XN)
            stage_experts(k, r)
            stage_combine(k, r, out)


def kernel(**inputs):
    import concourse.bacc as bacc
    from concourse.bass_utils import run_bass_kernel_spmd

    nc = bacc.Bacc("TRN2", target_bir_lowering=False, num_devices=1)
    arrays = {name: np.ascontiguousarray(x) for name, x in inputs.items() if name != "L0_ffn_attention_mask"}
    arrays["L0_mix_temperature"] = arrays["L0_mix_temperature"].reshape(H)
    arrays.update(constants())
    a = {name: nc.dram_tensor(name, x.shape, mybir.dt.from_np(x.dtype), kind="ExternalInput").ap()
         for name, x in arrays.items()}
    out = nc.dram_tensor("out", (N, D), F32, kind="ExternalOutput").ap()
    program(nc, a, out)
    return run_bass_kernel_spmd(nc, [arrays], core_ids=[0]).results[0]["out"]
```
